# Optimizing a Trainium2 kernel written in Bass

```python
import numpy as np
import jax
import jax.numpy as jnp

def _softmax(x, axis=-1):
    return jax.nn.softmax(x, axis=axis)

def _gelu(x):
    return jax.nn.gelu(x, approximate=True)

def _silu(x):
    return jax.nn.silu(x)

def _sigmoid(x):
    return jax.nn.sigmoid(x)

def _layernorm(x, axis=-1, eps=1e-05):
    m = jnp.mean(x, axis=axis, keepdims=True)
    v = jnp.var(x, axis=axis, keepdims=True)
    return (x - m) / jnp.sqrt(v + eps)

def _scatter_add(tgt, idx, src, axis=0):
    return tgt.at[idx].add(src)

def _segment_sum(src, seg, n):
    return jax.ops.segment_sum(src, seg, n)
kernel_name = 'mk_adaln_d2_jaxref_r8_34516f'

def setup_inputs(seed: int=0):
    np.random.seed(seed)
    _w = jnp.asarray

    def _L0_attn_setup():
        import jax, jax.numpy as jnp
        import numpy as np
        H, P, N, G, K, CH, E = (32, 128, 128, 8, 4, 32, 256)
        I = H * P
        CD = I + 2 * G * N
        PROJ = I + CD + H
        EPS = 1e-06

        def segsum(x):
            L = x.shape[-1]
            cs = jnp.cumsum(x, axis=-1)
            ss = cs[..., :, None] - cs[..., None, :]
            mask = jnp.tril(jnp.ones((L, L), dtype=bool))
            return jnp.where(mask, ss, -jnp.inf)
        key = jax.random.key(seed)
        ks = jax.random.split(key, 6)
        b, s = (2, 256)
        return {'x': jax.random.normal(ks[0], (b, s, E), jnp.float32), 'in_proj_w': jax.random.normal(ks[1], (PROJ, E), jnp.float32) / np.sqrt(E), 'conv_w': jax.random.normal(ks[2], (CD, 1, K), jnp.float32) / np.sqrt(K), 'conv_b': jax.random.normal(ks[3], (CD,), jnp.float32) * 0.02, 'dt_bias': jax.random.normal(ks[4], (H,), jnp.float32) * 0.1 + 1.0, 'A_log': jnp.log(jnp.arange(1, H + 1, dtype=jnp.float32)), 'D': jnp.ones((H,), jnp.float32), 'norm_w': jnp.ones((I,), jnp.float32), 'out_proj_w': jax.random.normal(ks[5], (E, I), jnp.float32) / np.sqrt(I)}
    _L0_attn_in = _L0_attn_setup()

    def _L0_ffn_setup():
        import jax, jax.numpy as jnp
        import numpy as np
        DIM = 256
        HID = 128
        E = 8
        K = 2
        SHID = HID * 1
        INIT = 0.02
        key = jax.random.key(seed)
        ks = jax.random.split(key, 9)
        return {'x': jax.random.normal(ks[0], (2, 128, DIM), jnp.float32), 'expert_bias': jnp.zeros((E,), jnp.float32), 'gate_w': jax.random.normal(ks[1], (E, DIM), jnp.float32) * INIT, 'w1': jax.random.normal(ks[2], (E, HID, DIM), jnp.float32) * INIT, 'w2': jax.random.normal(ks[3], (E, DIM, HID), jnp.float32) * INIT, 'w3': jax.random.normal(ks[4], (E, HID, DIM), jnp.float32) * INIT, 'sw1': jax.random.normal(ks[5], (SHID, DIM), jnp.float32) * INIT, 'sw2': jax.random.normal(ks[6], (DIM, SHID), jnp.float32) * INIT, 'sw3': jax.random.normal(ks[7], (SHID, DIM), jnp.float32) * INIT}
    _L0_ffn_in = _L0_ffn_setup()
    _L0_c = _w((lambda *s: np.random.randn(*s).astype(np.float32) * 0.05)(2, 256))
    _L0_wmod = _w((lambda *s: np.random.randn(*s).astype(np.float32) * 0.05)(256, 6 * 256) * 256 ** (-0.5))

    def _L1_attn_setup():
        import jax, jax.numpy as jnp
        import numpy as np
        DIM = 256
        NUM_HEADS = 128
        TOP_K = 32
        D_HEAD_V = DIM // NUM_HEADS
        key = jax.random.key(seed)
        ks = jax.random.split(key, 5)
        s = 1.0 / np.sqrt(DIM)
        x = jax.random.normal(ks[0], (4, 512, DIM), dtype=jnp.float32)
        Wq = jax.random.uniform(ks[1], (NUM_HEADS, DIM), minval=-s, maxval=s, dtype=jnp.float32)
        Wk = jax.random.uniform(ks[2], (NUM_HEADS, DIM), minval=-s, maxval=s, dtype=jnp.float32)
        Wv = jax.random.uniform(ks[3], (DIM, DIM), minval=-s, maxval=s, dtype=jnp.float32)
        Wo = jax.random.uniform(ks[4], (DIM, DIM), minval=-s, maxval=s, dtype=jnp.float32)
        return {'x': x, 'Wq': Wq, 'Wk': Wk, 'Wv': Wv, 'Wo': Wo}
    _L1_attn_in = _L1_attn_setup()

    def _L1_ffn_setup():
        import jax, jax.numpy as jnp
        import numpy as np
        B, S, H = (4, 512, 256)
        I = 176
        E = 8
        K = 2
        INIT = 0.02
        key = jax.random.key(seed)
        k0, k1, k2, k3, k4, k5 = jax.random.split(key, 6)
        return {'x': jax.random.normal(k0, (B, S, H), dtype=jnp.float32), 'w_shared1': jax.random.normal(k1, (H, I), dtype=jnp.float32) * INIT, 'w_shared2': jax.random.normal(k2, (I, H), dtype=jnp.float32) * INIT, 'w1': jax.random.normal(k3, (E, H, I), dtype=jnp.float32) * INIT, 'w2': jax.random.normal(k4, (E, I, H), dtype=jnp.float32) * INIT, 'w_router': jax.random.normal(k5, (H, E), dtype=jnp.float32) * INIT}
    _L1_ffn_in = _L1_ffn_setup()
    _L1_c = _w((lambda *s: np.random.randn(*s).astype(np.float32) * 0.05)(2, 256))
    _L1_wmod = _w((lambda *s: np.random.randn(*s).astype(np.float32) * 0.05)(256, 6 * 256) * 256 ** (-0.5))
    _d = {'L0_attn_x': _L0_attn_in['x'], 'L0_attn_in_proj_w': _L0_attn_in['in_proj_w'], 'L0_attn_conv_w': _L0_attn_in['conv_w'], 'L0_attn_conv_b': _L0_attn_in['conv_b'], 'L0_attn_dt_bias': _L0_attn_in['dt_bias'], 'L0_attn_A_log': _L0_attn_in['A_log'], 'L0_attn_D': _L0_attn_in['D'], 'L0_attn_norm_w': _L0_attn_in['norm_w'], 'L0_attn_out_proj_w': _L0_attn_in['out_proj_w'], 'L0_ffn_expert_bias': _L0_ffn_in['expert_bias'], 'L0_ffn_gate_w': _L0_ffn_in['gate_w'], 'L0_ffn_w1': _L0_ffn_in['w1'], 'L0_ffn_w2': _L0_ffn_in['w2'], 'L0_ffn_w3': _L0_ffn_in['w3'], 'L0_ffn_sw1': _L0_ffn_in['sw1'], 'L0_ffn_sw2': _L0_ffn_in['sw2'], 'L0_ffn_sw3': _L0_ffn_in['sw3'], 'L0_c': _L0_c, 'L0_wmod': _L0_wmod, 'L1_attn_Wq': _L1_attn_in['Wq'], 'L1_attn_Wk': _L1_attn_in['Wk'], 'L1_attn_Wv': _L1_attn_in['Wv'], 'L1_attn_Wo': _L1_attn_in['Wo'], 'L1_ffn_w_shared1': _L1_ffn_in['w_shared1'], 'L1_ffn_w_shared2': _L1_ffn_in['w_shared2'], 'L1_ffn_w1': _L1_ffn_in['w1'], 'L1_ffn_w2': _L1_ffn_in['w2'], 'L1_ffn_w_router': _L1_ffn_in['w_router'], 'L1_c': _L1_c, 'L1_wmod': _L1_wmod}
    _x0 = _d['L0_attn_x']
    _d['L0_attn_x'] = jax.random.normal(jax.random.fold_in(jax.random.key(seed), 1), (2, 512, 256), dtype=_x0.dtype)
    del _x0
    return _d

def reference(L0_attn_x, L0_attn_in_proj_w, L0_attn_conv_w, L0_attn_conv_b, L0_attn_dt_bias, L0_attn_A_log, L0_attn_D, L0_attn_norm_w, L0_attn_out_proj_w, L0_ffn_expert_bias, L0_ffn_gate_w, L0_ffn_w1, L0_ffn_w2, L0_ffn_w3, L0_ffn_sw1, L0_ffn_sw2, L0_ffn_sw3, L0_c, L0_wmod, L1_attn_Wq, L1_attn_Wk, L1_attn_Wv, L1_attn_Wo, L1_ffn_w_shared1, L1_ffn_w_shared2, L1_ffn_w1, L1_ffn_w2, L1_ffn_w_router, L1_c, L1_wmod):

    def _L0_attn_ref(x, in_proj_w, conv_w, conv_b, dt_bias, A_log, D, norm_w, out_proj_w):
        import jax, jax.numpy as jnp
        import numpy as np
        H, P, N, G, K, CH, E = (32, 128, 128, 8, 4, 32, 256)
        I = H * P
        CD = I + 2 * G * N
        PROJ = I + CD + H
        EPS = 1e-06

        def segsum(x):
            L = x.shape[-1]
            cs = jnp.cumsum(x, axis=-1)
            ss = cs[..., :, None] - cs[..., None, :]
            mask = jnp.tril(jnp.ones((L, L), dtype=bool))
            return jnp.where(mask, ss, -jnp.inf)
        b, s, _ = x.shape
        proj = x @ in_proj_w.T
        gate, hbc, dt = jnp.split(proj, [I, I + CD], axis=-1)
        hbc_t = jnp.transpose(hbc, (0, 2, 1))
        conv = jax.lax.conv_general_dilated(hbc_t, conv_w, window_strides=(1,), padding=[(K - 1, 0)], feature_group_count=CD, dimension_numbers=('NCH', 'OIH', 'NCH'))
        hbc = jax.nn.silu(jnp.transpose(conv + conv_b[None, :, None], (0, 2, 1)))
        hs, B, C = jnp.split(hbc, [I, I + G * N], axis=-1)
        A = -jnp.exp(A_log.astype(jnp.float32))
        dt = jax.nn.softplus(dt.astype(jnp.float32) + dt_bias)
        dt = jnp.clip(dt, 0.0, None)
        X = hs.reshape(b, s, H, P).astype(jnp.float32)
        B = jnp.tile(B.reshape(b, s, G, N).astype(jnp.float32), (1, 1, H // G, 1))
        C = jnp.tile(C.reshape(b, s, G, N).astype(jnp.float32), (1, 1, H // G, 1))
        D_res = D[:, None] * X
        X = X * dt[..., None]
        A_bt = A * dt
        nc = s // CH
        Xc = X.reshape(b, nc, CH, H, P)
        Bc = B.reshape(b, nc, CH, H, N)
        Cc = C.reshape(b, nc, CH, H, N)
        Ac = jnp.transpose(A_bt.reshape(b, nc, CH, H), (0, 3, 1, 2))
        A_cum = jnp.cumsum(Ac, axis=-1)
        Lmat = jnp.exp(segsum(Ac))
        Y_diag = jnp.einsum('bclhn,bcshn,bhcls,bcshd->bclhd', Cc, Bc, Lmat, Xc)
        decay_states = jnp.exp(A_cum[..., -1:] - A_cum)
        states = jnp.einsum('bclhn,bhcl,bclhd->bchdn', Bc, decay_states, Xc)
        states = jnp.concatenate([jnp.zeros_like(states[:, :1]), states], axis=1)
        A_last = jnp.pad(A_cum[..., -1], ((0, 0), (0, 0), (1, 0)))
        decay_chunk = jnp.exp(segsum(A_last))
        new_states = jnp.einsum('bhij,bjhdn->bihdn', decay_chunk, states)
        states_prev = new_states[:, :-1]
        state_decay = jnp.exp(A_cum)
        Y_off = jnp.einsum('bclhn,bchdn,bhcl->bclhd', Cc, states_prev, state_decay)
        y = (Y_diag + Y_off).reshape(b, s, H, P) + D_res
        y = y.reshape(b, s, I)
        gs = I // G
        h32 = y * jax.nn.silu(gate.astype(jnp.float32))
        g = h32.reshape(b, s, I // gs, gs)
        var = jnp.mean(g * g, axis=-1, keepdims=True)
        h32 = (g * jax.lax.rsqrt(var + EPS)).reshape(b, s, I)
        return norm_w * h32 @ out_proj_w.T

    def _L0_ffn_ref(x, expert_bias, gate_w, w1, w2, w3, sw1, sw2, sw3):
        import jax, jax.numpy as jnp
        import numpy as np
        DIM = 256
        HID = 128
        E = 8
        K = 2
        SHID = HID * 1
        INIT = 0.02
        B, S, D = x.shape
        xf = x.reshape(-1, D)
        N = xf.shape[0]
        scores = jax.nn.sigmoid((xf @ gate_w.T).astype(jnp.float32))
        _, sel = jax.lax.top_k(scores + expert_bias[None, :], K)
        top_scores = jnp.take_along_axis(scores, sel, axis=1)
        flat_exp = sel.reshape(-1)
        order = jnp.argsort(flat_exp, stable=True)
        sorted_exp = flat_exp[order]
        tok_idx = order // K
        sc_sorted = top_scores.reshape(-1)[order]
        rin = xf[tok_idx] * sc_sorted[:, None].astype(x.dtype)
        out_sorted = jnp.zeros_like(rin)
        for e in range(E):
            m = (sorted_exp == e)[:, None].astype(rin.dtype)
            h = jax.nn.silu(rin @ w1[e].T) * (rin @ w3[e].T)
            out_sorted = out_sorted + m * (h @ w2[e].T)
        routed = jnp.zeros((N, D), x.dtype).at[tok_idx].add(out_sorted)
        shared = jax.nn.silu(xf @ sw1.T) * (xf @ sw3.T) @ sw2.T
        return (routed + shared).reshape(B, S, D)

    def _L1_attn_ref(x, Wq, Wk, Wv, Wo):
        import jax, jax.numpy as jnp
        import numpy as np
        DIM = 256
        NUM_HEADS = 128
        TOP_K = 32
        D_HEAD_V = DIM // NUM_HEADS
        B, S, _ = x.shape
        H, dv, k = (NUM_HEADS, D_HEAD_V, TOP_K)
        q = jnp.einsum('bsd,hd->bhs', x, Wq)
        keys = jnp.einsum('bsd,hd->bhs', x, Wk)
        v = jnp.einsum('bsd,ed->bse', x, Wv).reshape(B, S, H, dv).transpose(0, 2, 1, 3)
        k_idx = jnp.argsort(keys, axis=-1)
        k_sorted = jnp.take_along_axis(keys, k_idx, axis=-1)
        v_sorted = jnp.take_along_axis(v, k_idx[..., None], axis=2)
        top_keys = k_sorted[:, :, -k:]
        bot_keys = k_sorted[:, :, :k]
        top_vals = v_sorted[:, :, -k:, :]
        bot_vals = v_sorted[:, :, :k, :]
        attn_top = jax.nn.softmax(q[..., None] * top_keys[:, :, None, :], axis=-1)
        attn_bot = jax.nn.softmax(q[..., None] * bot_keys[:, :, None, :], axis=-1)
        out_top = jnp.einsum('bhsk,bhkd->bhsd', attn_top, top_vals)
        out_bot = jnp.einsum('bhsk,bhkd->bhsd', attn_bot, bot_vals)
        q_pos = (q > 0).astype(x.dtype)[..., None]
        out = q_pos * out_top + (1.0 - q_pos) * out_bot
        out = out.transpose(0, 2, 1, 3).reshape(B, S, H * dv)
        return jnp.einsum('bsd,ed->bse', out, Wo)

    def _L1_ffn_ref(x, w_shared1, w_shared2, w1, w2, w_router):
        import jax, jax.numpy as jnp
        import numpy as np
        B, S, H = (4, 512, 256)
        I = 176
        E = 8
        K = 2
        INIT = 0.02
        bs, seq_len, hidden = x.shape
        xf = x.reshape(-1, hidden)
        T = xf.shape[0]
        shared = jax.nn.silu(xf @ w_shared1) @ w_shared2
        router_logits = xf @ w_router
        routing_probs = jax.nn.softmax(router_logits, axis=-1)
        top_k_probs, top_k_idx = jax.lax.top_k(routing_probs, K)
        top_k_probs = top_k_probs / jnp.sum(top_k_probs, axis=-1, keepdims=True)
        comb = jnp.zeros((T, E), dtype=xf.dtype).at[jnp.arange(T)[:, None], top_k_idx].add(top_k_probs)
        routed = jnp.zeros_like(xf)
        for e in range(E):
            expert_out = jax.nn.silu(xf @ w1[e]) @ w2[e]
            routed = routed + comb[:, e:e + 1] * expert_out
        final = (shared + routed).reshape(bs, seq_len, hidden)
        return final
    x = L0_attn_x
    mod = (_silu(L0_c) @ L0_wmod).reshape(L0_c.shape[0], 6, 1, -1)
    sa, ca, ga, sb, cb, gb = (mod[:, 0], mod[:, 1], mod[:, 2], mod[:, 3], mod[:, 4], mod[:, 5])
    ga = (2 * (ga >= 0) - 1) * jnp.maximum(jnp.abs(ga), 0.25)
    gb = (2 * (gb >= 0) - 1) * jnp.maximum(jnp.abs(gb), 0.25)
    h = _layernorm(x, axis=-1) * (1 + ca) + sa
    x = x + ga * _L0_attn_ref(h, L0_attn_in_proj_w, L0_attn_conv_w, L0_attn_conv_b, L0_attn_dt_bias, L0_attn_A_log, L0_attn_D, L0_attn_norm_w, L0_attn_out_proj_w)
    h = _layernorm(x, axis=-1) * (1 + cb) + sb
    x = x + gb * _L0_ffn_ref(h, L0_ffn_expert_bias, L0_ffn_gate_w, L0_ffn_w1, L0_ffn_w2, L0_ffn_w3, L0_ffn_sw1, L0_ffn_sw2, L0_ffn_sw3)
    mod = (_silu(L1_c) @ L1_wmod).reshape(L1_c.shape[0], 6, 1, -1)
    sa, ca, ga, sb, cb, gb = (mod[:, 0], mod[:, 1], mod[:, 2], mod[:, 3], mod[:, 4], mod[:, 5])
    ga = (2 * (ga >= 0) - 1) * jnp.maximum(jnp.abs(ga), 0.25)
    gb = (2 * (gb >= 0) - 1) * jnp.maximum(jnp.abs(gb), 0.25)
    h = _layernorm(x, axis=-1) * (1 + ca) + sa
    x = x + ga * _L1_attn_ref(h, L1_attn_Wq, L1_attn_Wk, L1_attn_Wv, L1_attn_Wo)
    h = _layernorm(x, axis=-1) * (1 + cb) + sb
    x = x + gb * _L1_ffn_ref(h, L1_ffn_w_shared1, L1_ffn_w_shared2, L1_ffn_w1, L1_ffn_w2, L1_ffn_w_router)
    return x

_drawn_inputs = setup_inputs


def setup_inputs(seed=0):
    import zlib

    import numpy as np

    out = dict(_drawn_inputs(seed))
    spreads = {'L0_attn_D': (1.0, 0.6), 'L0_attn_norm_w': (1.0, 0.2), 'L0_ffn_expert_bias': (0.0, 0.8)}
    factors = {'L0_attn_conv_b': 7.832,
     'L0_attn_dt_bias': 6.583,
     'L0_ffn_gate_w': 8.0,
     'L0_ffn_w1': 8.0,
     'L0_ffn_w2': 8.0,
     'L0_ffn_w3': 8.0,
     'L0_ffn_sw1': 8.0,
     'L0_ffn_sw2': 8.0,
     'L0_ffn_sw3': 8.0,
     'L1_attn_Wq': 3.78,
     'L1_attn_Wk': 3.283,
     'L1_attn_Wv': 3.1,
     'L1_attn_Wo': 3.101,
     'L1_ffn_w_shared1': 5.386,
     'L1_ffn_w_shared2': 5.354,
     'L1_ffn_w1': 7.606,
     'L1_ffn_w2': 7.495,
     'L1_ffn_w_router': 8.0}
    for name, (base, spread) in spreads.items():
        noise = np.random.default_rng([zlib.crc32(name.encode()), seed]).standard_normal(out[name].shape)
        drawn = base * np.exp(spread * noise) if base else spread * noise
        out[name] = jnp.asarray(drawn.astype(out[name].dtype))
    for name, factor in factors.items():
        out[name] = (out[name] * factor).astype(out[name].dtype)
    return out
```

```python
from contextlib import ExitStack

import concourse.bass as bass
from concourse import mybir

B, S, D = 2, 512, 256
T = B * S
P = 128
KT = D // P
NT = T // P
TB = S // P
H = 32
G = 8
NG = 8
HG = H // NG
LN_EPS = 1e-5
RMS_EPS = 1e-6
E = 8
E1 = E + 1
HID1 = 176
FT = (E1, -(-E1 * HID1 // P))
K = 32
QG = 4
NQ = P // QG
NEG = -3.0e38
CST = 3 * P + H + E * E + QG + 2 * K
C_STACK = 3 * P
C_LOWER = C_STACK + H
C_BLOCK = C_LOWER + E * E
C_IOTA = C_BLOCK + QG
WB = D + 8
PIECES = 3


def build_block(nc, io, stop=None):
    fp32, bf16, i32 = mybir.dt.float32, mybir.dt.bfloat16, mybir.dt.int32
    ALU = mybir.AluOpType
    ACT = mybir.ActivationFunctionType
    ctx = ExitStack()
    with ctx:
        def sb(name, shape, dt=fp32):
            return ctx.enter_context(nc.sbuf_tensor(name, shape, dt))

        def sem(name):
            return ctx.enter_context(nc.semaphore(name))

        bank = [ctx.enter_context(nc.psum_tensor(f"bank{n}", [P, 512], fp32)) for n in range(8)]

        x_sb = sb("x_sb", [P, NT, D])
        acc = sb("acc", [P, NT, D])
        xT = sb("xT", [P, 4, S])
        hT = xT[:, :, :].rearrange("p (k c) s -> p k (c s)", k=KT)
        hTs = sb("hTs", [P, 2, KT, T], bf16)
        cst = sb("cst", [P, CST])
        ident, tri, ones = cst[:, 0:P], cst[:, P:2 * P], cst[:, 2 * P:3 * P]
        identb = sb("identb", [P, P], bf16)
        identb96 = sb("identb96", [PIECES * H, H], bf16)
        cT = sb("cT", [P, 2 * KT * B])
        sc = sb("sc", [P, 2 * KT * B])
        mods = sb("mods", [P, 2, 4, KT, B])
        gm = sb("gm", [P, 2, 2, B, D])
        small = sb("small", [P, 2 * H + E])
        wdt = sb("wdt", [P, KT, H])
        bcp = sb("bcp", [P, G, 2, 5])
        stats = sb("stats", [P, NT, 6])
        mv = sb("mv", [P, NT, 2])
        rstd = sb("rstd", [P, NT])
        nwt = sb("nwt", [P, 3, NT])
        router = sb("router", [P, 2, KT, E])
        later = ExitStack()
        resident_sb = sb
        scan = ctx.enter_context(ExitStack())

        def sb(name, shape, dt=fp32):
            return scan.enter_context(nc.sbuf_tensor(name, shape, dt))

        dtv = sb("dtv", [P, NT, H])
        cs = sb("cs", [P, NT, H])
        dec = sb("dec", [P, NT, H])
        etot = sb("etot", [P, NT, H])
        csp = sb("csp", [P, NT, PIECES, H], bf16)
        csT = sb("csT", [PIECES * H, T], bf16)
        wbs = sb("wbs", [P, 2, G, 512], bf16)
        CBm = sb("CBm", [P, G, TB, P])
        Btok = sb("Btok", [P, G, TB, P])
        CT = sb("CT", [P, G, S])
        BT = sb("BT", [P, S])
        wA = sb("wA", [P, 2, 512])
        whl = sb("whl", [P, 2, 2, 512], bf16)
        wB = sb("wB", [P, 8, WB])
        raw = sb("raw", [P, 2, S + 3])
        u = sb("u", [P, 2, S])
        thx = sb("thx", [P, S])
        thg = sb("thg", [P, S])
        gs = sb("gs", [P, 4, S])
        rel = sb("rel", [P, S])
        Lm = sb("Lm", [P, 2, S])
        scb = Lm[:, :, :].rearrange("p a (b n) -> p (a b) n", n=P)
        Em = sb("Em", [P, 2, S - P])
        Mm = sb("Mm", [P, 2, S])
        dtmp = Mm[:, :, :].rearrange("p a (b t h) -> p (a b) t h", t=NT, h=H)
        Xdt = sb("Xdt", [P, 2, S])
        Xw = sb("Xw", [P, 2, S - P])
        CE = sb("CE", [P, 2, S - P])
        St = sb("St", [P, 2, S - P])
        yv = sb("yv", [P, 2, S])
        yb = sb("yb", [P, 8, S])
        ysq = sb("ysq", [P, S])
        sqa = sb("sqa", [P, 2, S])
        ssv = sb("ssv", [P, TB])
        rg = sb("rg", [P, TB])
        wm = yb[:, :, :].rearrange("p a b -> p (a b)")[:, 0:KT * 6 * D].rearrange(
            "p (k n) -> p k n", k=KT)
        wm1 = Btok[:, :, :, :].rearrange("p a b c -> p (a b c)")[:, 0:KT * 6 * D].rearrange(
            "p (k n) -> p k n", k=KT)
        wbf = CBm[:, :, :, :].rearrange("p a b c -> p a (b c)")

        yv_sign = yb[:, 0:4, :].rearrange("p a b -> p (a b)")

        scan.close()
        def sb(name, shape, dt=fp32):
            return later.enter_context(nc.sbuf_tensor(name, shape, dt))

        sel = sb("sel", [PIECES * E1, sum(FT) * P], bf16)
        F1 = max(FT)
        w13 = sb("w13", [P, F1, 512])
        w13s = sb("w13s", [P, 2, F1, 512], bf16)
        w2 = sb("w2", [P, F1, D])
        selw = w2[0:PIECES * E1, :, :].rearrange("p f d -> p (f d)")[:, 0:sum(FT) * P]
        pr = sb("pr", [P, NT, E])
        prb = sb("prb", [P, NT, E])
        rank = sb("rank", [P, NT, E])
        cmpa = sb("cmpa", [P, NT, E, E])
        cmpb = sb("cmpb", [P, NT, E, E])
        comb = sb("comb", [P, NT, E1])
        cpt = sb("cpt", [P, NT, E1])
        cpb = sb("cpb", [P, NT, PIECES, E1], bf16)
        cbT = sb("cbT", [PIECES * E1, T], bf16)
        r1 = sb("r1", [P, NT])
        sS = sb("sS", [P, 2, S])
        ua = sb("ua", [P, 2, S])
        uc = sb("uc", [P, 2, S])
        fth = sb("fth", [P, 2, S])
        fg = sb("fg", [P, S])
        hf = sb("hf", [P, 2, S])
        xo = sb("xo", [P, TB, D])
        zerob = sb("zerob", [P, P + S], bf16)
        later.close()
        def sb(name, shape, dt=fp32):
            return ctx.enter_context(nc.sbuf_tensor(name, shape, dt))

        wqk = sb("wqk", [P, 2, KT, P])
        wv = sb("wv", [P, KT, D])
        wo = sb("wo", [P, KT, D])
        qs = sb("qs", [P, B, S])
        qp = sb("qp", [P, PIECES, B, S], bf16)
        ks = sb("ks", [P, B, S])
        wk = sb("wk", [P, 3, S])
        m8 = sb("m8", [P, 2, 8])
        ext = sb("ext", [P, B, 2])
        hit = sb("hit", [P, 2, S])
        rk = sb("rk", [P, S])
        code = sb("code", [P, 3, S], bf16)
        cdT = sb("cdT", [P, TB, P], bf16)
        kd = sb("kd", [P, 2, S])
        PV = sb("PV", [P, TB, PIECES, P, 4], bf16)
        pvr = sb("pvr", [P, TB * P])
        iotak = sb("iotak", [P, 2, K, QG], bf16)
        selQ = sb("selQ", [P, NQ, K, QG], bf16)
        OH = sb("OH", [P, TB, 2, NQ, P], bf16)
        gat = sb("gat", [P, 8, 16])
        gam = sb("gam", [P, 8, 16])
        scl = sb("scl", [P, NQ, 2])
        VW = sb("VW", [P, NQ, QG, 5])
        tb_ = sb("tb", [P, 2, S])
        arg = sb("arg", [P, 2, S])
        Ex = sb("Ex", [P, 4, S])
        ohf = OH[:, :, :, :, :].rearrange("p t s g m -> p (t s g m)").bitcast(fp32)
        O5 = ohf[:, 0:2560].rearrange("p (t h c) -> p t h c", t=TB, c=5)
        qm = ohf[:, 2560:3072].rearrange("p (t h) -> p t h", t=TB)
        rden = ohf[:, 3072:3584].rearrange("p (t h) -> p t h", t=TB)
        att = ohf[:, 3584:4608].rearrange("p (t h j) -> p t h j", t=TB, j=2)
        attT = ohf[:, 4608:5632].rearrange("p (k s) -> p k s", k=KT)
        attf = att.rearrange("p t h j -> p t (h j)")

        names = ("d_cst d_x d_c d_wm0 d_wm1 d_small d_wbc d_out "
                 "modp_done gmod_done sc_done mods_done gm_done thc_done scb_done "
                 "dve_seq pool_seq act_seq xh_done tr_done hT_done hts_done "
                 "dtp_done dtz_done dta_done dcs_done dex_done csp_done cspT_done csT_done e_dt "
                 "bcp_done wbs_done idb_done "
                 "c_proj c_raw c_step c_th c_bc c_mm c_cbm c_btok "
                 "wsplit whi_done wo_done px raw_done tr_x xdt_done pg thg_done gs_done pc e_done rel_done L_done "
                 "M_done c0_done cv_step thx_done xT_done xw_done ce_done ps rc_step py yc_done "
                 "yb_done ysq_done sq_add ssq_done out_done rg_step oa_done "
                 "x1_done "
                 "d_sel d_w13 d_w2 d_attn sel_done zb_done "
                 "rt_p rt_act rt_dve cp_done cpT_p cbT_done fw_hi fw_done "
                 "fu fs_c fa_done fth_done fh_done fout zero_done xf_done "
                 "a_qk a_v a_qkc a_code a_cT a_cTc a_kd a_kT a_pv a_vp a_oh a_gat a_vw a_iota "
                 "a_qp a_Q a_tb a_arg a_E a_PV a_O5 a_qT a_qm a_att a_attT a_attc a_out a_x a_tbr").split()
        q = {n: sem(n) for n in names}
        d_wA = [sem(f"d_wA{n}") for n in range(2)]
        d_wB = [sem(f"d_wB{n}") for n in range(8)]

        block = ctx.enter_context(nc.Block())

        NWT = 13

        def rsqrt_steps(dve, out, v, tmp, step, first):
            n = first
            nc.vector.tensor_scalar(tmp[0].bitcast(i32), v.bitcast(i32), 1, None,
                                    ALU.logical_shift_right).then_inc(step, 1)
            dve.wait_ge(step, n + 1)
            nc.vector.tensor_scalar(out.bitcast(i32), tmp[0].bitcast(i32), -1.0, float(0x5f3759df),
                                    ALU.mult, ALU.add).then_inc(step, 1)
            n = 2
            for _ in range(3):
                dve.wait_ge(step, first + n)
                nc.vector.tensor_tensor(tmp[0], out, out, ALU.mult).then_inc(step, 1)
                dve.wait_ge(step, first + n + 1)
                nc.vector.scalar_tensor_tensor(out=tmp[1], in0=tmp[0], scalar=-0.5, in1=v, op0=ALU.mult,
                                               op1=ALU.mult).then_inc(step, 1)
                dve.wait_ge(step, first + n + 2)
                nc.vector.scalar_tensor_tensor(out=out, in0=tmp[1], scalar=1.5, in1=out, op0=ALU.add,
                                               op1=ALU.mult).then_inc(step, 1)
                n += 3
            dve.wait_ge(step, first + n)
            nc.vector.tensor_tensor(tmp[0], out, out, ALU.mult).then_inc(step, 1)
            dve.wait_ge(step, first + n + 1)
            nc.vector.scalar_tensor_tensor(out=tmp[1], in0=tmp[0], scalar=-0.5, in1=v, op0=ALU.mult,
                                           op1=ALU.mult).then_inc(step, 1)
            dve.wait_ge(step, first + n + 2)

        def slots(eng, b, slot):
            for i in range(8):
                slot(i, 0, b)
            with eng.Fori(1, 4) as it:
                for i in range(8):
                    slot(i, it, b)
            for i in range(5):
                slot(i, 4, b)

        def stages(i, it):
            def head(back):
                j, n = i - back, it
                if j < 0:
                    j, n = j + 8, it - 1
                if type(n) is int and not 0 <= n < H // 8:
                    return None
                return j, n
            return head

        @block.sync
        def _(sp):
            sp.dma_start(cst[:], io["cst"][:, :]).then_inc(q["d_cst"], 16)
            sp.dma_start(cT[:], io["cT"][:, :]).then_inc(q["d_c"], 16)
            sp.dma_start(x_sb[:], io["x"].rearrange("(t p) d -> p t d", p=P)).then_inc(q["d_x"], 16)
            sp.dma_start(wm, io["wmod"][0]).then_inc(q["d_wm0"], 16)
            sp.dma_start(wm1, io["wmod"][1]).then_inc(q["d_wm1"], 16)
            sp.dma_start(small[:], io["small"].partition_broadcast(P)).then_inc(q["d_small"], 16)
            sp.dma_start(wdt[:], io["wdt"]).then_inc(q["d_small"], 16)
            sp.dma_start(bcp[:], io["bcp"]).then_inc(q["d_small"], 16)
            sp.dma_start(router[:], io["router"]).then_inc(q["d_small"], 16)
            sp.dma_start(wbf, io["wbc"]).then_inc(q["d_wbc"], 16)

            def load_slot(i, it, b):
                if type(it) is int and it >= H // 8:
                    return
                hh = H * b + 8 * it + i
                if type(it) is int:
                    k = 8 * it + i
                    split, outs, kk = hh - 1, 2 * (hh // 4 - 1), k
                else:
                    kk = sp.snap(8 * it + i)
                    split, outs = sp.snap(hh - 1), sp.snap(2 * (8 * b + 2 * it + i // 4 - 1))
                if type(split) is not int or split > 0:
                    sp.wait_ge(q["wsplit"], split)
                sp.dma_start(wA[:, i % 2, :], io["win"][bass.ds(kk, 1)].squeeze(0)).then_inc(d_wA[i % 2], 16)
                if type(outs) is not int or outs > 0:
                    sp.wait_ge(q["out_done"], outs)
                sp.dma_start(wB[:, i, :], io["wob"][bass.ds(kk, 1)].squeeze(0)).then_inc(d_wB[i], 16)

            for b in range(B):
                slots(sp, b, load_slot)
            sp.wait_ge(q["wsplit"], B * H - 1)
            sp.dma_start(wA[:, 0, :], io["win"][0]).then_inc(d_wA[0], 16)

            def experts_load(L):
                n = FT[L]
                if L == 0:
                    sp.wait_ge(q["x1_done"], 1)
                else:
                    sp.wait_ge(q["a_x"], B)
                sp.dma_start(selw, io["sel"]).then_inc(q["d_sel"], 16)
                sp.wait_ge(q["sel_done"], L + 1)
                sp.dma_start(w13[:, 0:n, 0:io[f"w13_{L}"].shape[2]], io[f"w13_{L}"]).then_inc(q["d_w13"], 16)
                sp.dma_start(w2[:, 0:n, :], io[f"w2_{L}"]).then_inc(q["d_w2"], 16)

            def store():
                sp.dma_start(io["out"].rearrange("(t p) d -> p t d", p=P), x_sb[:]).then_inc(q["d_out"], 16)
                sp.wait_ge(q["d_out"], 16)

            if stop == 0:
                sp.wait_ge(q["x1_done"], 1)
                return store()
            experts_load(0)
            sp.wait_ge(q["xf_done"], B)
            if stop == 1:
                return store()
            sp.dma_start(wqk[:], io["wqk"]).then_inc(q["d_attn"], 16)
            sp.dma_start(wv[:], io["wv"]).then_inc(q["d_attn"], 16)
            sp.dma_start(wo[:], io["wo"]).then_inc(q["d_attn"], 16)
            sp.wait_ge(q["a_x"], B)
            if stop == 2:
                return store()
            experts_load(1)
            sp.wait_ge(q["xf_done"], 2 * B)
            store()

        @block.tensor
        def _(pe):
            pe.wait_ge(q["sc_done"], 1)
            for L in range(2):
                w = (wm, wm1)[L]
                pe.wait_ge(q[f"d_wm{L}"], 16)
                for n, m in enumerate((0, 1, 3, 4)):
                    for ft in range(KT):
                        o = ((L * 4 + n) * KT + ft) * B
                        for kt in range(KT):
                            last = nc.tensor.matmul(
                                bank[0][:, o:o + B], w[:, kt, m * D + ft * P:m * D + (ft + 1) * P],
                                sc[:, (L * KT + kt) * B:(L * KT + kt + 1) * B],
                                start=kt == 0, stop=kt == KT - 1)
            last.then_inc(q["modp_done"], 1)
            pe.wait_ge(q["scb_done"], 1)
            for L in range(2):
                w = (wm, wm1)[L]
                for n, m in enumerate((2, 5)):
                    for b in range(B):
                        o = (L * 2 + n) * B + b
                        for kt in range(KT):
                            last = nc.tensor.matmul(
                                bank[1 + o // 2][:, (o % 2) * D:(o % 2 + 1) * D],
                                scb[:, (L * KT + kt) * B + b, :], w[:, kt, m * D:(m + 1) * D],
                                start=kt == 0, stop=kt == KT - 1)
            last.then_inc(q["gmod_done"], 1)

            def transposed_rows(n):
                for b in range(B):
                    pe.wait_ge(q["xh_done"], n * B + b + 1)
                    for ft in range(KT):
                        for t in range(TB):
                            last = nc.tensor.transpose(
                                bank[b * KT + ft][:, t * P:(t + 1) * P],
                                acc[:, b * TB + t, ft * P:(ft + 1) * P], ident)
                        last.then_inc(q["tr_done"], 1)

            pe.wait_ge(q["gm_done"], 1)
            transposed_rows(0)

            pe.wait_ge(q["hT_done"], 4)
            pe.wait_ge(q["d_small"], 64)
            for t in range(NT):
                for kt in range(KT):
                    last = nc.tensor.matmul(bank[4][:, t * H:(t + 1) * H], hT[:, kt, t * P:(t + 1) * P],
                                            wdt[:, kt, :], start=kt == 0, stop=kt == KT - 1)
            last.then_inc(q["dtp_done"], 1)
            pe.wait_ge(q["dta_done"], 1)
            ab = dtmp[:, 2, :, :].rearrange("p t h -> p (t h)")
            nc.tensor.matmul(bank[5][:, 0:NT * H], tri, ab, start=True, stop=True)
            nc.tensor.matmul(bank[6][:, 0:NT * H], ones, ab, start=True, stop=True).then_inc(q["dcs_done"], 1)
            pe.wait_ge(q["csp_done"], 1)
            pe.wait_ge(q["idb_done"], 1)
            cspT = bank[7][:, :].bitcast(bf16)
            for t in range(NT):
                last = nc.tensor.transpose(cspT[0:PIECES * H, t * P:(t + 1) * P],
                                           csp[:, t, :, :].rearrange("p a h -> p (a h)"), identb[:])
            last.then_inc(q["cspT_done"], 1)

            def split_product(out, wpart, hpart):
                n = 0
                for a, c in ((0, 0), (0, 1), (1, 0)):
                    for kt in range(KT):
                        last = nc.tensor.matmul(out, wpart(a, kt), hpart(c, kt), start=n == 0, stop=n == 5)
                        n += 1
                return last

            def group_stage1(g, b):
                pe.wait_ge(q["c_raw"], G * b + g) if not (type(g) is int and G * b + g == 0) else None
                for n in range(2):
                    last = split_product(
                        bank[n][:, :],
                        lambda a, kt: wbs[:, a, bass.ds(g, 1), (n * KT + kt) * P:(n * KT + kt + 1) * P].squeeze(1),
                        lambda a, kt: hTs[:, a, kt, b * S:(b + 1) * S])
                last.then_inc(q["c_proj"], 1)

            def group_stage2(g, b):
                pe.wait_ge(q["c_bc"], G * b + g + 1)
                if not (type(g) is int and G * b + g == 0):
                    pe.wait_ge(q["c_cbm"], G * b + g)
                    pe.wait_ge(q["c_btok"], G * b + g)
                for t in range(TB):
                    nc.tensor.matmul(bank[2][:, t * P:(t + 1) * P], BT[:, t * P:(t + 1) * P],
                                     CT[:, bass.ds(g, 1), t * P:(t + 1) * P].squeeze(1), start=True, stop=True)
                for t in range(TB):
                    last = nc.tensor.transpose(bank[3][:, t * P:(t + 1) * P], BT[:, t * P:(t + 1) * P], ident)
                last.then_inc(q["c_mm"], 1)

            def scan_slot(i, it, b):
                head = stages(i, it)
                h1, h2, h3 = head(0), head(1), head(2)
                n1, n2, n3 = (H * b + 8 * h[1] + h[0] if h else None for h in (h1, h2, h3))

                def since(name, n):
                    if type(n) is not int or n > 0:
                        pe.wait_ge(q[name], n)

                if h1:
                    w = whl[:, i % 2, :, :]
                    pe.wait_ge(q["wsplit"], n1 + 1)
                    since("raw_done", n1)
                    split_product(bank[0][:, :], lambda a, kt: w[:, a, kt * P:(kt + 1) * P],
                                  lambda a, kt: hTs[:, a, kt, b * S:(b + 1) * S]).then_inc(q["px"], 1)
                if h2:
                    j = h2[0]
                    pe.wait_ge(q["xT_done"], n2 + 1)
                    since("xdt_done", n2)
                    for t in range(TB):
                        last = nc.tensor.transpose(bank[2][:, t * P:(t + 1) * P],
                                                   xT[:, j % 4, t * P:(t + 1) * P], ident)
                    last.then_inc(q["tr_x"], 1)
                if h1:
                    since("gs_done", n1)
                    split_product(bank[1][:, :], lambda a, kt: w[:, a, (KT + kt) * P:(KT + kt + 1) * P],
                                  lambda a, kt: hTs[:, a, kt, b * S:(b + 1) * S]).then_inc(q["pg"], 1)
                if h2:
                    since("rel_done", n2)
                    pe.wait_ge(q["csT_done"], 1)
                    hcol = 8 * h2[1] + h2[0]
                    nc.tensor.matmul(
                        bank[3][:, :],
                        identb96[:, bass.ds(hcol, 1)].to_broadcast([PIECES * H, P]),
                        csT[:, b * S:(b + 1) * S], start=True, stop=True).then_inc(q["pc"], 1)
                if h3:
                    j = h3[0]
                    pe.wait_ge(q["xw_done"], n3 + 1)
                    since("rc_step", 3 * n3)
                    for c in range(TB - 1):
                        last = nc.tensor.matmul(bank[4][:, c * P:(c + 1) * P], Btok[:, j, c, :],
                                                Xw[:, j % 2, c * P:(c + 1) * P], start=True, stop=True)
                    last.then_inc(q["ps"], 1)
                    pe.wait_ge(q["M_done"], n3 + 1)
                    since("yc_done", n3)
                    for c in range(TB):
                        nc.tensor.matmul(bank[5][:, c * P:(c + 1) * P], Xdt[:, j % 2, c * P:(c + 1) * P],
                                         Mm[:, j % 2, c * P:(c + 1) * P], start=c == 0, stop=c == 0,
                                         skip_group_check=True)
                out_slot(i, it, b)
                if h3:
                    pe.wait_ge(q["rc_step"], 3 * n3 + 3)
                    pe.wait_ge(q["ce_done"], n3 + 1)
                    for c in range(1, TB):
                        last = nc.tensor.matmul(bank[5][:, c * P:(c + 1) * P], St[:, j % 2, (c - 1) * P:c * P],
                                                CE[:, j % 2, (c - 1) * P:c * P], start=False, stop=True,
                                                skip_group_check=True)
                    last.then_inc(q["py"], 1)

            def out_slot(i, it, b):
                e = out_event(i, it)
                if not e:
                    return
                half, j, gi = e
                jj = NG * b + gi
                y0 = 4 * j
                if half == 0:
                    pe.wait_ge(q["wo_done"], HG * (jj + 1))
                    pe.wait_ge(q["sq_add"], 3 * (jj + 1))
                    for t in range(TB):
                        last = nc.tensor.matmul(bank[7][:, t:t + 1], sqa[:, j, t * P:(t + 1) * P], ones[:, 0:1],
                                                start=True, stop=True)
                    last.then_inc(q["ssq_done"], 1)
                if type(jj) is not int or 2 * jj + half > 0:
                    pe.wait_ge(q["oa_done"], 2 * jj + half)
                for t in range(2):
                    tt = 2 * half + t
                    for m in range(HG):
                        last = nc.tensor.matmul(bank[6][:, t * D:(t + 1) * D],
                                                yb[:, y0 + m, tt * P:(tt + 1) * P], wB[:, y0 + m, 0:D],
                                                start=m == 0, stop=m == HG - 1)
                last.then_inc(q["out_done"], 1)

            for b in range(B):
                if b == 0:
                    pe.wait_ge(q["wbs_done"], 1)
                    pe.wait_ge(q["hts_done"], 4)
                else:
                    pe.wait_ge(q["oa_done"], 2 * NG * b)
                group_stage1(0, b)
                group_stage1(1, b)
                group_stage2(0, b)
                with pe.Fori(1, G - 1) as g:
                    group_stage1(g + 1, b)
                    group_stage2(g, b)
                group_stage2(G - 1, b)
                pe.wait_ge(q["c_cbm"], G * (b + 1))
                pe.wait_ge(q["c_btok"], G * (b + 1))
                slots(pe, b, scan_slot)
            if stop == 0:
                return

            def experts(L):
                n0, nf = 2 * L + 1, FT[L]
                w13n = 2 if L == 0 else 1
                transposed_rows(n0)
                pe.wait_ge(q["hT_done"], 4 * (n0 + 1))
                for t in range(NT):
                    for kt in range(KT):
                        last = nc.tensor.matmul(bank[4][:, t * E:(t + 1) * E], hT[:, kt, t * P:(t + 1) * P],
                                                router[:, L, kt, :], start=kt == 0, stop=kt == KT - 1)
                last.then_inc(q["rt_p"], 1)
                pe.wait_ge(q["cp_done"], L + 1)
                cT_ = bank[5][:, :].bitcast(bf16)
                for t in range(NT):
                    last = nc.tensor.transpose(cT_[0:PIECES * E1, t * P:(t + 1) * P],
                                               cpb[:, t, :, :].rearrange("p a e -> p (a e)"), identb[:])
                last.then_inc(q["cpT_p"], 1)
                pe.wait_ge(q["cbT_done"], L + 1)
                pe.wait_ge(q["hts_done"], 4 * (L + 2))
                pe.wait_ge(q["zb_done"], L + 1)
                pe.wait_ge(q["sel_done"], L + 1)

                def rows_in(f, b, first):
                    n = (FT[0] * B if L else 0) + nf * b + f
                    if not (type(f) is int and f == 0):
                        pe.wait_ge(q["fa_done"], n)
                    pe.wait_ge(q["fw_done"], (FT[0] if L else 0) + f + 1)
                    for m in range(w13n):
                        split_product(bank[m][:, :],
                                      lambda a, kt: w13s[:, a, bass.ds(f, 1), (m * KT + kt) * P:(m * KT + kt + 1) * P].squeeze(1),
                                      lambda a, kt: hTs[:, a, kt, b * S:(b + 1) * S])
                    nc.tensor.matmul(bank[2][:, :], sel[:, bass.ds((FT[0] * P if L else 0) + f * P, P)],
                                     cbT[:, b * S:(b + 1) * S], start=True, stop=True).then_inc(q["fu"], 1)

                def rows_out(f, b, buf):
                    n = (FT[0] * B if L else 0) + nf * b + f
                    pe.wait_ge(q["fh_done"], n + 1)
                    for t in range(TB):
                        last = nc.tensor.matmul(bank[6 + t // 2][:, (t % 2) * D:(t % 2 + 1) * D],
                                                hf[:, buf, t * P:(t + 1) * P], w2[:, bass.ds(f, 1), :].squeeze(1),
                                                start=False, stop=False, skip_group_check=True)
                    last.then_inc(q["fout"], 1)

                pe.wait_ge(q["d_w2"], 16 * (L + 1))
                for b in range(B):
                    if b:
                        pe.wait_ge(q["xf_done"], L * B + b)
                        pe.wait_ge(q["fa_done"], (FT[0] * B if L else 0) + nf * b)
                    for m in (6, 7):
                        nc.tensor.matmul(bank[m][:, :], zerob[:, 0:P], zerob[:, P:], start=True, stop=False,
                                         skip_group_check=True)
                    rows_in(0, b, True)
                    for m in range(2):
                        rows_in(m + 1, b, False)
                        rows_out(m, b, m)
                    with pe.Fori(1, (nf - 1) // 2) as i:
                        for m in range(2):
                            rows_in(2 * i + m + 1, b, False)
                            rows_out(2 * i + m, b, m)
                    rows_out(nf - 1, b, 0)

            pe.wait_ge(q["x1_done"], 1)
            experts(0)
            if stop == 1:
                return

            def heads():
                transposed_rows(2)
                pe.wait_ge(q["hT_done"], 12)
                pe.wait_ge(q["d_attn"], 48)
                for b in range(B):
                    hb = slice(b * S, (b + 1) * S)
                    if b:
                        pe.wait_ge(q["a_qkc"], b)
                    for m in range(2):
                        for kt in range(KT):
                            last = nc.tensor.matmul(bank[m][:, :], wqk[:, m, kt, :], hT[:, kt, hb],
                                                    start=kt == 0, stop=kt == KT - 1)
                    last.then_inc(q["a_qk"], 1)
                for b in range(B):
                    pe.wait_ge(q["a_kd"], b + 1)
                    pe.wait_ge(q["a_code"], b + 1)
                    cT_ = bank[2][:, :].bitcast(bf16)
                    for t in range(TB):
                        last = nc.tensor.transpose(cT_[:, t * P:(t + 1) * P], code[:, 2, t * P:(t + 1) * P], identb[:])
                    last.then_inc(q["a_cT"], 1)
                    if b:
                        pe.wait_ge(q["a_pv"], 3 * b)
                    for m in range(2):
                        for t in range(TB):
                            last = nc.tensor.transpose(bank[3 + m][:, t * P:(t + 1) * P],
                                                       kd[:, m, t * P:(t + 1) * P], ident)
                        last.then_inc(q["a_kT"], 1)
                    for t in range(TB):
                        for kt in range(KT):
                            last = nc.tensor.matmul(bank[5 + t // 2][:, (t % 2) * D:(t % 2 + 1) * D],
                                                    hT[:, kt, (b * TB + t) * P:(b * TB + t + 1) * P], wv[:, kt, :],
                                                    start=kt == 0, stop=kt == KT - 1)
                    last.then_inc(q["a_v"], 1)

                    pe.wait_ge(q["a_oh"], b + 1)
                    pe.wait_ge(q["a_pv"], 3 * (b + 1))
                    pe.wait_ge(q["a_vp"], b + 1)

                    def gather(n):
                        c = NQ // 4 * b + n
                        if not (type(n) is int and c == 0):
                            pe.wait_ge(q["a_gat"], c)
                        for g4 in range(4):
                            for side in range(2):
                                o = (g4 * 2 + side) * 48
                                for t in range(TB):
                                    last = nc.tensor.matmul(
                                        bank[7][:, o:o + 48],
                                        OH[:, t, side, bass.ds(4 * n + g4, 1), :].squeeze(1),
                                        PV[:, t, :, bass.ds(16 * n + 4 * g4, 4), :],
                                        start=t == 0, stop=t == TB - 1)
                        last.then_inc(q["a_vw"], 1)

                    gather(0)
                    with pe.Fori(1, NQ // 4) as n:
                        gather(n)
                    pe.wait_ge(q["a_qp"], b + 1)
                    pe.wait_ge(q["a_gat"], NQ // 4 * (b + 1))
                    pe.wait_ge(q["a_cTc"], b + 1)
                    pe.wait_ge(q["a_qkc"], B)

                    def spread(i, n):
                        c = NQ * b + 4 * n + i
                        if not (type(c) is int and c < 2):
                            pe.wait_ge(q["a_arg"], c - 1)
                        for pc in range(PIECES):
                            last = nc.tensor.matmul(
                                bank[i % 2][:, :],
                                selQ[:, bass.ds(4 * n + i, 1), :, :].squeeze(1).rearrange("p k h -> p (k h)"),
                                qp[:, pc, b, :], start=pc == 0, stop=pc == PIECES - 1)
                        last.then_inc(q["a_Q"], 1)

                    def weigh(i, n):
                        c = NQ * b + 4 * n + i
                        if i == 0 and not (type(n) is int and NQ // 4 * b + n == 0):
                            pe.wait_ge(q["a_O5"], NQ // 4 * b + n)
                        pe.wait_ge(q["a_E"], c + 1)
                        for t in range(TB):
                            last = nc.tensor.matmul(bank[2][:, (i * TB + t) * 20:(i * TB + t + 1) * 20],
                                                    Ex[:, i, t * P:(t + 1) * P],
                                                    VW[:, bass.ds(4 * n + i, 1), :, :].squeeze(1).rearrange("p h c -> p (h c)"),
                                                    start=True, stop=True)
                        last.then_inc(q["a_PV"], 1)

                    for i in range(4):
                        spread(i, 0)
                        if i > 1:
                            weigh(i - 2, 0)
                    with pe.Fori(1, NQ // 4) as n:
                        for i in range(4):
                            spread(i, n)
                            weigh((i - 2) % 4, n if i > 1 else n - 1)
                    weigh(2, NQ // 4 - 1)
                    weigh(3, NQ // 4 - 1)
                    for t in range(TB):
                        last = nc.tensor.transpose(bank[3][:, t * P:(t + 1) * P], qs[:, b, t * P:(t + 1) * P], ident)
                    last.then_inc(q["a_qT"], 1)
                    pe.wait_ge(q["a_att"], b + 1)
                    for kt in range(KT):
                        for t in range(TB):
                            last = nc.tensor.transpose(bank[4 + kt][:, t * P:(t + 1) * P],
                                                       attf[:, t, kt * P:(kt + 1) * P], ident)
                    last.then_inc(q["a_attT"], 1)
                    pe.wait_ge(q["a_attc"], b + 1)
                    for t in range(TB):
                        for kt in range(KT):
                            last = nc.tensor.matmul(bank[(6, 3)[t // 2]][:, (t % 2) * D:(t % 2 + 1) * D],
                                                    attT[:, kt, t * P:(t + 1) * P], wo[:, kt, :],
                                                    start=kt == 0, stop=kt == KT - 1)
                    last.then_inc(q["a_out"], 1)

            heads()
            if stop == 2:
                return
            pe.wait_ge(q["a_x"], B)
            experts(1)

        @block.scalar
        def _(act):
            act.wait_ge(q["d_c"], 16)
            nc.scalar.activation(sc[:], cT[:], ACT.Tanh, scale=0.5).then_inc(q["thc_done"], 1)

            def modulate(n, L):
                act.wait_ge(q["mods_done"], 1)
                for b in range(B):
                    for ft in range(KT):
                        act.wait_ge(q["tr_done"], 4 * n + b * KT + ft + 1)
                        nc.scalar.activation(hT[:, ft, b * S:(b + 1) * S], bank[b * KT + ft][:, :], ACT.Identity,
                                             bias=mods[:, L, 2 * (n % 2), ft, b:b + 1],
                                             scale=mods[:, L, 2 * (n % 2) + 1, ft, b:b + 1]).then_inc(q["hT_done"], 1)

            modulate(0, 0)
            act.wait_ge(q["dtz_done"], 2)
            nc.scalar.activation(dtmp[:, 1], dtmp[:, 1], ACT.Exp).then_inc(q["act_seq"], 1)
            act.wait_ge(q["act_seq"], 1)
            nc.scalar.activation(dtmp[:, 1], dtmp[:, 1], ACT.Ln, bias=1.0).then_inc(q["act_seq"], 1)
            nc.scalar.activation(small[:, H:2 * H], small[:, H:2 * H], ACT.Exp).then_inc(q["act_seq"], 1)
            act.wait_ge(q["dex_done"], 1)
            nc.scalar.activation(dec[:], dec[:], ACT.Exp).then_inc(q["e_dt"], 1)
            nc.scalar.activation(etot[:], etot[:], ACT.Exp).then_inc(q["e_dt"], 1)

            def group_stage1(g, b):
                n = G * b + g
                act.wait_ge(q["c_proj"], n + 1)
                if not (type(g) is int and n == 0):
                    act.wait_ge(q["c_step"], 8 * n - 1)
                nc.scalar.activation(raw[:, 0, 3:], bank[0][:, :], ACT.Copy)
                nc.scalar.activation(raw[:, 1, 3:], bank[1][:, :], ACT.Copy).then_inc(q["c_raw"], 1)
                act.wait_ge(q["c_step"], 8 * n + 8)
                if not (type(g) is int and n == 0):
                    act.wait_ge(q["c_bc"], n)
                nc.scalar.activation(thx[:], u[:, 0, :], ACT.Tanh)
                nc.scalar.activation(thg[:], u[:, 1, :], ACT.Tanh).then_inc(q["c_th"], 1)

            def group_stage2(g, b):
                n = G * b + g
                act.wait_ge(q["c_mm"], n + 1)
                nc.scalar.activation(Btok[:, bass.ds(g, 1), :, :].squeeze(1).rearrange("p t n -> p (t n)"),
                                     bank[3][:, :], ACT.Copy).then_inc(q["c_btok"], 1)

            def scan_slot(i, it, b):
                head = stages(i, it)
                h1, h2, h4 = head(0), head(1), head(3)
                n1, n2, n4 = (H * b + 8 * h[1] + h[0] if h else None for h in (h1, h2, h4))

                def since(name, n):
                    if type(n) is not int or n > 0:
                        act.wait_ge(q[name], n)

                if h1:
                    since("pg", n1)
                    since("wsplit", n1)
                    act.wait_ge(d_wA[(i + 1) % 2], 16 * (H // 2 * b + 4 * it + (i + 1) // 2 + 1))
                    nc.scalar.activation(whl[:, (i + 1) % 2, 0, :], wA[:, (i + 1) % 2, :], ACT.Copy)\
                        .then_inc(q["whi_done"], 1)
                if h1:
                    since("cv_step", 3 * n1 - 3)
                    since("xT_done", n1 - 1)
                    act.wait_ge(d_wB[i], 16 * (H // 8 * b + h1[1] + 1))
                    act.wait_ge(q["px"], n1 + 1)
                    nc.scalar.activation(raw[:, i % 2, 3:], bank[0][:, :], ACT.Copy)
                    nc.scalar.activation(u[:, i % 2, :], bank[0][:, :], ACT.Identity, scale=wB[:, i, D + 3:D + 4],
                                         bias=wB[:, i, D + 4:D + 5]).then_inc(q["raw_done"], 1)
                if h2:
                    j = h2[0]
                    hcol = 8 * h2[1] + h2[0]
                    since("ce_done", n2 - 1)
                    since("M_done", n2 - 1)
                    act.wait_ge(q["pc"], n2 + 1)
                    nc.scalar.activation(Em[:, j % 2, :], bank[3][:, P:S], ACT.Exp).then_inc(q["e_done"], 1)
                    since("L_done", n2)
                    for t in range(TB):
                        last = nc.scalar.activation(rel[:, t * P:(t + 1) * P], bank[3][:, t * P:(t + 1) * P],
                                                    ACT.Relu, scale=-1.0,
                                                    bias=cs[:, b * TB + t, bass.ds(hcol, 1)])
                    last.then_inc(q["rel_done"], 1)
                if h1:
                    since("gs_done", n1)
                    act.wait_ge(q["pg"], n1 + 1)
                    nc.scalar.activation(thg[:], bank[1][:, :], ACT.Tanh, scale=0.5).then_inc(q["thg_done"], 1)
                if h2:
                    act.wait_ge(q["rel_done"], n2 + 1)
                    nc.scalar.activation(Lm[:, j % 2, :], rel[:], ACT.Exp, scale=-1.0).then_inc(q["L_done"], 1)
                if h4:
                    j = h4[0]
                    jj = NG * b + 2 * h4[1] + j // 4
                    if j % HG == 0:
                        since("ssq_done", jj - 1)
                    elif j % HG > 1 or type(jj) is not int or jj > 0:
                        act.wait_ge(q["sq_add"], 3 * jj + j % HG - 1)
                    act.wait_ge(q["yb_done"], n4 + 1)
                    nc.scalar.activation(ysq[:] if j % HG else sqa[:, j // HG, :], yb[:, j, :], ACT.Square)\
                        .then_inc(q["ysq_done"], 1)
                if h1:
                    since("xT_done", n1)
                    act.wait_ge(q["cv_step"], 3 * n1 + 3)
                    nc.scalar.activation(thx[:], u[:, i % 2, :], ACT.Tanh, scale=0.5).then_inc(q["thx_done"], 1)

            act.wait_ge(d_wA[0], 16)
            nc.scalar.activation(whl[:, 0, 0, :], wA[:, 0, :], ACT.Copy).then_inc(q["whi_done"], 1)
            for b in range(B):
                if b:
                    act.wait_ge(q["oa_done"], 2 * NG * b)
                group_stage1(0, b)
                group_stage1(1, b)
                group_stage2(0, b)
                with act.Fori(1, G - 1) as g:
                    group_stage1(g + 1, b)
                    group_stage2(g, b)
                group_stage2(G - 1, b)
                act.wait_ge(q["c_bc"], G * (b + 1))
                slots(act, b, scan_slot)
            if stop == 0:
                return

            def experts(L):
                n0, nf = 2 * L + 1, FT[L]
                w = 512 if L == 0 else 256
                base = FT[0] * B if L else 0
                modulate(n0, L)
                act.wait_ge(q["d_w13"], 16 * (L + 1))
                if L:
                    act.wait_ge(q["a_x"], B)
                for f in range(nf):
                    nc.scalar.activation(w13s[:, 0, f, 0:w], w13[:, f, 0:w], ACT.Copy).then_inc(q["fw_hi"], 1)
                if L == 0:
                    act.wait_ge(q["rt_p"], 1)
                    nc.scalar.activation(pr[:].rearrange("p t e -> p (t e)"), bank[4][:, 0:NT * E], ACT.Tanh,
                                         scale=0.5).then_inc(q["rt_act"], 1)
                else:
                    act.wait_ge(q["rt_dve"], 1)
                    nc.scalar.activation(pr[:], pr[:], ACT.Exp).then_inc(q["rt_act"], 1)

                def hidden(f, b, buf):
                    n = base + nf * b + f
                    def since(name, m):
                        if type(m) is not int or m > 0:
                            act.wait_ge(q[name], m)
                    if L == 0:
                        since("fh_done", n - 1)
                        act.wait_ge(q["fu"], n + 1)
                        nc.scalar.activation(sS[:, buf, :], bank[2][:, :], ACT.Copy).then_inc(q["fs_c"], 1)
                        act.wait_ge(q["fa_done"], n + 1)
                        nc.scalar.activation(fth[:, buf, :], ua[:, buf, :], ACT.Tanh, scale=0.5)\
                            .then_inc(q["fth_done"], 1)
                    else:
                        since("fh_done", n - 1)
                        act.wait_ge(q["fu"], n + 1)
                        nc.scalar.activation(fth[:, buf, :], bank[0][:, :], ACT.Tanh, scale=0.5)\
                            .then_inc(q["fth_done"], 1)

                for b in range(B):
                    for m in range(2):
                        hidden(m, b, m)
                    with act.Fori(1, (nf - 1) // 2) as i:
                        for m in range(2):
                            hidden(2 * i + m, b, m)
                    hidden(nf - 1, b, 0)

            experts(0)
            if stop == 1:
                return

            def heads():
                modulate(2, 1)
                for b in range(B):
                    act.wait_ge(q["a_qk"], b + 1)
                    nc.scalar.activation(qs[:, b, :], bank[0][:, :], ACT.Copy)
                    nc.scalar.activation(ks[:, b, :], bank[1][:, :], ACT.Copy).then_inc(q["a_qkc"], 1)
                for b in range(B):
                    def part(i, n):
                        c = NQ * b + 4 * n + i
                        if not (type(c) is int and c < 2):
                            act.wait_ge(q["a_arg"], c - 1)
                        act.wait_ge(q["a_Q"], c + 1)
                        nc.scalar.activation(tb_[:, i % 2, :], bank[i % 2][:, :], ACT.Identity,
                                             scale=scl[:, bass.ds(4 * n + i, 1), 1:2].squeeze(1)).then_inc(q["a_tb"], 1)

                    def grow(i, n):
                        c = NQ * b + 4 * n + i
                        if not (type(c) is int and c < 4):
                            act.wait_ge(q["a_PV"], c - 3)
                        act.wait_ge(q["a_arg"], c + 1)
                        nc.scalar.activation(Ex[:, i, :], arg[:, i % 2, :], ACT.Exp).then_inc(q["a_E"], 1)

                    act.wait_ge(q["a_gat"], NQ // 4 * (b + 1))
                    for i in range(4):
                        part(i, 0)
                        if i:
                            grow(i - 1, 0)
                    with act.Fori(1, NQ // 4) as n:
                        for i in range(4):
                            part(i, n)
                            grow((i - 1) % 4, n if i else n - 1)
                    grow(3, NQ // 4 - 1)
                    act.wait_ge(q["a_attT"], b + 1)
                    for kt in range(KT):
                        last = nc.scalar.activation(attT[:, kt, :], bank[4 + kt][:, :], ACT.Copy)
                    last.then_inc(q["a_attc"], 1)

            heads()
            if stop == 2:
                return
            experts(1)

        @block.vector
        def _(dve):
            count = [0]

            def link(ins):
                count[0] += 1
                ins.then_inc(q["dve_seq"], 1)
                dve.wait_ge(q["dve_seq"], count[0])

            link(nc.vector.memset(raw[:, :, 0:3], 0.0))
            dve.wait_ge(q["thc_done"], 1)
            link(nc.vector.scalar_tensor_tensor(out=sc[:], in0=sc[:], scalar=1.0, in1=cT[:], op0=ALU.add, op1=ALU.mult))
            nc.vector.tensor_scalar(sc[:], sc[:], 0.5, None, ALU.mult).then_inc(q["sc_done"], 1)
            dve.wait_ge(q["sc_done"], 1)
            nc.vector.tensor_copy(scb, sc[:].unsqueeze(2).to_broadcast([P, 2 * KT * B, P])).then_inc(q["scb_done"], 1)
            dve.wait_ge(q["d_cst"], 16)
            nc.vector.tensor_copy(identb[:], ident).then_inc(q["idb_done"], 1)
            nc.vector.tensor_copy(identb96[:], cst[0:PIECES * H, C_STACK:C_STACK + H] ).then_inc(q["idb_done"], 1)
            dve.wait_ge(q["modp_done"], 1)
            link(nc.vector.tensor_copy(mods[:].rearrange("p a b c d -> p (a b c d)"), bank[0][:, 0:32]))
            for m in (1, 3):
                last = nc.vector.tensor_scalar(mods[:, :, m], mods[:, :, m], 1.0, None, ALU.add)
            last.then_inc(q["mods_done"], 1)
            dve.wait_ge(q["gmod_done"], 1)
            for o in range(4):
                nc.vector.tensor_copy(gm[:, o // 2, o % 2].rearrange("p b d -> p (b d)"), bank[1 + o][:, :])\
                    .then_inc(q["gm_done"], 1)

            def normalise(n):
                for t in range(NT):
                    last = nc.vector.bn_stats(stats[:, t, :], x_sb[:, t, :])
                link(last)
                for t in range(NT):
                    last = nc.vector.bn_aggr(mv[:, t, :], stats[:, t, :])
                link(last)
                link(nc.vector.tensor_scalar(nwt[:, 2, :], mv[:, :, 1], LN_EPS, None, ALU.add))
                rsqrt_steps(dve, rstd[:], nwt[:, 2, :], (nwt[:, 0, :], nwt[:, 1, :]), q["dve_seq"], count[0])
                count[0] += NWT
                for b in range(B):
                    for t in range(b * TB, (b + 1) * TB):
                        last = nc.vector.tensor_scalar(acc[:, t, :], x_sb[:, t, :], mv[:, t, 0:1], rstd[:, t:t + 1],
                                                       ALU.subtract, ALU.mult)
                    last.then_inc(q["xh_done"], 1)

            def split_rows(n):
                for b in range(B):
                    for ft in range(KT):
                        dve.wait_ge(q["hT_done"], 4 * n + b * KT + ft + 1)
                        part = slice(b * S, (b + 1) * S)
                        link(nc.vector.tensor_copy(hTs[:, 0, ft, part], hT[:, ft, part]))
                        nc.vector.tensor_tensor(hTs[:, 1, ft, part], hT[:, ft, part], hTs[:, 0, ft, part],
                                                ALU.subtract).then_inc(q["hts_done"], 1)

            dve.wait_ge(q["d_x"], 16)
            normalise(0)
            dve.wait_ge(q["gm_done"], 4)
            gv = gm[:].rearrange("p a b c d -> p (a b c d)")
            sg = yv_sign[:]
            link(nc.vector.tensor_scalar(sg, gv, 0.0, 2.0, ALU.is_ge, ALU.mult))
            link(nc.vector.scalar_tensor_tensor(out=gv, in0=gv, scalar=-1.0, in1=gv, op0=ALU.mult, op1=ALU.max))
            link(nc.vector.tensor_scalar(gv, gv, 0.25, None, ALU.max))
            link(nc.vector.scalar_tensor_tensor(out=gv, in0=sg, scalar=-1.0, in1=gv, op0=ALU.add, op1=ALU.mult))
            split_rows(0)
            dve.wait_ge(q["tr_done"], 4)
            link(nc.vector.memset(acc[:], 0.0))

            dve.wait_ge(q["dtp_done"], 1)
            dve.wait_ge(q["d_small"], 64)
            z, az, adt = dtmp[:, 0], dtmp[:, 1], dtmp[:, 2]
            nc.vector.tensor_tensor(z, bank[4][:, 0:NT * H].rearrange("p (t h) -> p t h", t=NT),
                                    small[:, 0:H].unsqueeze(1).to_broadcast([P, NT, H]), ALU.add)\
                .then_inc(q["dtz_done"], 1)
            dve.wait_ge(q["dtz_done"], 1)
            nc.vector.scalar_tensor_tensor(out=az, in0=z, scalar=-1.0, in1=z, op0=ALU.mult, op1=ALU.min).then_inc(q["dtz_done"], 1)
            dve.wait_ge(q["act_seq"], 3)
            link(nc.vector.scalar_tensor_tensor(out=dtv[:], in0=z, scalar=0.0, in1=az, op0=ALU.max, op1=ALU.add))
            link(nc.vector.tensor_scalar(dtv[:], dtv[:], 0.0, None, ALU.max))
            nc.vector.scalar_tensor_tensor(out=adt, in0=dtv[:], scalar=-1.0,
                                           in1=small[:, H:2 * H].unsqueeze(1).to_broadcast([P, NT, H]),
                                           op0=ALU.mult, op1=ALU.mult).then_inc(q["dta_done"], 1)
            dve.wait_ge(q["dcs_done"], 1)
            fl = "p t h -> p (t h)"
            link(nc.vector.tensor_copy(cs[:].rearrange(fl), bank[5][:, 0:NT * H]))
            nc.vector.tensor_copy(etot[:].rearrange(fl), bank[6][:, 0:NT * H])
            link(nc.vector.tensor_tensor(dec[:].rearrange(fl), bank[6][:, 0:NT * H], cs[:].rearrange(fl), ALU.subtract))
            link(nc.vector.tensor_copy(csp[:, :, 0, :], cs[:]))
            dve.wait_ge(q["dve_seq"], count[0])
            nc.vector.tensor_tensor(dtmp[:, 0], cs[:], csp[:, :, 0, :], ALU.subtract).then_inc(q["dex_done"], 1)
            dve.wait_ge(q["dex_done"], 1)
            link(nc.vector.tensor_copy(csp[:, :, 1, :], dtmp[:, 0]))
            nc.vector.tensor_tensor(csp[:, :, 2, :], dtmp[:, 0], csp[:, :, 1, :], ALU.subtract).then_inc(q["csp_done"], 1)
            dve.wait_ge(q["cspT_done"], 1)
            nc.vector.tensor_copy(csT[:], bank[7][:, :].bitcast(bf16)[0:PIECES * H, :]).then_inc(q["csT_done"], 1)

            def taps(out, src, w, n, step):
                for d in (1, 2, 3):
                    dve.wait_ge(q[step], n)
                    nc.vector.scalar_tensor_tensor(out=out, in0=src[:, 3 - d:3 - d + S], scalar=w(3 - d), in1=out,
                                                   op0=ALU.mult, op1=ALU.add).then_inc(q[step], 1)
                    n = n + 1

            def group_stage1(g, b):
                n = G * b + g
                dve.wait_ge(q["bcp_done"], 1)
                if not (type(g) is int and n == 0):
                    dve.wait_ge(q["c_bc"], n)
                dve.wait_ge(q["c_raw"], n + 1)
                for m in range(2):
                    w = lambda tap: bcp[:, bass.ds(g, 1), m, tap:tap + 1].squeeze(1)
                    nc.vector.tensor_scalar(u[:, m, :], raw[:, m, 3:3 + S], w(3), w(4), ALU.mult, ALU.add)\
                        .then_inc(q["c_step"], 1)
                    taps(u[:, m, :], raw[:, m, :], w, 8 * n + 4 * m + 1, "c_step")
                dve.wait_ge(q["c_th"], n + 1)
                if not (type(g) is int and n == 0):
                    dve.wait_ge(q["c_mm"], n)
                nc.vector.scalar_tensor_tensor(out=BT[:], in0=thx[:], scalar=1.0, in1=u[:, 0, :],
                                               op0=ALU.add, op1=ALU.mult)
                nc.vector.scalar_tensor_tensor(out=CT[:, bass.ds(g, 1), :].squeeze(1), in0=thg[:], scalar=1.0,
                                               in1=u[:, 1, :], op0=ALU.add, op1=ALU.mult).then_inc(q["c_bc"], 1)

            def group_stage2(g, b):
                dve.wait_ge(q["c_mm"], G * b + g + 1)
                nc.vector.tensor_tensor(CBm[:, bass.ds(g, 1), :, :].squeeze(1),
                                        bank[2][:, :].rearrange("p (t n) -> p t n", t=TB),
                                        tri.unsqueeze(1).to_broadcast([P, TB, P]), ALU.mult).then_inc(q["c_cbm"], 1)

            def scan_slot(i, it, b):
                head = stages(i, it)
                h1, h2, h3 = head(0), head(1), head(2)
                n1, n2, n3 = (H * b + 8 * h[1] + h[0] if h else None for h in (h1, h2, h3))

                def since(name, n):
                    if type(n) is not int or n > 0:
                        dve.wait_ge(q[name], n)

                def chunks(ap):
                    return ap.rearrange("p (t n) -> p t n", n=P)

                if h2:
                    j = h2[0]
                    hcol = 8 * h2[1] + h2[0]
                    since("py", n2 - 1)
                    since("xw_done", n2 - 1)
                    dve.wait_ge(q["tr_x"], n2 + 1)
                    nc.vector.tensor_tensor(chunks(Xdt[:, j % 2, :]), chunks(bank[2][:, :]),
                                            dtv[:, b * TB:(b + 1) * TB, bass.ds(hcol, 1)].to_broadcast([P, TB, P]),
                                            ALU.mult).then_inc(q["xdt_done"], 1)
                if h1:
                    w = lambda tap: wB[:, i, D + tap:D + tap + 1]
                    dve.wait_ge(q["raw_done"], n1 + 1)
                    since("cv_step", 3 * n1)
                    for d in (1, 2, 3):
                        if d > 1:
                            dve.wait_ge(q["cv_step"], 3 * n1 + d - 1)
                        nc.vector.scalar_tensor_tensor(out=u[:, i % 2, :], in0=raw[:, i % 2, 3 - d:3 - d + S],
                                                       scalar=w(3 - d), in1=u[:, i % 2, :],
                                                       op0=ALU.mult, op1=ALU.add).then_inc(q["cv_step"], 1)
                if h2:
                    dve.wait_ge(q["L_done"], n2 + 1)
                    nc.vector.tensor_tensor(Mm[:, j % 2, :], CBm[:, j, :, :].rearrange("p t n -> p (t n)"),
                                            Lm[:, j % 2, :], ALU.mult).then_inc(q["M_done"], 1)
                if h1:
                    since("yb_done", n1 - 3)
                    dve.wait_ge(q["thg_done"], n1 + 1)
                    nc.vector.scalar_tensor_tensor(out=gs[:, i % 4, :], in0=thg[:], scalar=1.0, in1=bank[1][:, :],
                                                   op0=ALU.add, op1=ALU.mult).then_inc(q["gs_done"], 1)
                if h3:
                    j = h3[0]
                    hcol = 8 * h3[1] + h3[0]
                    since("py", n3 - 1)
                    dve.wait_ge(q["ps"], n3 + 1)
                    s_of = lambda c: St[:, j % 2, c * P:(c + 1) * P]
                    nc.vector.tensor_copy(s_of(0), bank[4][:, 0:P]).then_inc(q["rc_step"], 1)
                    for c in (1, 2):
                        dve.wait_ge(q["rc_step"], 3 * n3 + c)
                        nc.vector.scalar_tensor_tensor(out=s_of(c), in0=s_of(c - 1),
                                                       scalar=etot[:, b * TB + c, bass.ds(hcol, 1)],
                                                       in1=bank[4][:, c * P:(c + 1) * P],
                                                       op0=ALU.mult, op1=ALU.add).then_inc(q["rc_step"], 1)
                if h1:
                    since("yc_done", n1 - 3)
                    dve.wait_ge(q["thx_done"], n1 + 1)
                    dve.wait_ge(q["cv_step"], 3 * n1 + 3)
                    nc.vector.scalar_tensor_tensor(out=xT[:, i % 4, :], in0=thx[:], scalar=1.0, in1=u[:, i % 2, :],
                                                   op0=ALU.add, op1=ALU.mult).then_inc(q["xT_done"], 1)
                out_slot(i, it, b)
                if h3:
                    since("yb_done", n3 - 1)
                    dve.wait_ge(q["xT_done"], n3 + 1)
                    dve.wait_ge(q["py"], n3 + 1)
                    nc.vector.scalar_tensor_tensor(out=yv[:, j % 2, :], in0=xT[:, j % 4, :],
                                                   scalar=wB[:, j, D + 5:D + 6], in1=bank[5][:, :],
                                                   op0=ALU.mult, op1=ALU.add).then_inc(q["yc_done"], 1)

            def out_slot(i, it, b):
                e = out_event(i, it)
                if not e:
                    return
                half, j, gi = e
                jj = NG * b + gi
                base = (NWT + 2) * jj
                step = q["rg_step"]
                if half == 0:
                    dve.wait_ge(q["ssq_done"], jj + 1)
                    if type(jj) is not int or jj > 0:
                        dve.wait_ge(step, base)
                        dve.wait_ge(q["oa_done"], 2 * jj)
                    nc.vector.tensor_scalar(ssv[:], bank[7][:, 0:TB], 1.0 / (16 * HG * P), RMS_EPS, ALU.mult, ALU.add)\
                        .then_inc(step, 1)
                    dve.wait_ge(step, base + 1)
                    rsqrt_steps(dve, rg[:], ssv[:], (nwt[:, 0, 0:TB], nwt[:, 1, 0:TB]), step, base + 1)
                    nc.vector.tensor_scalar(rg[:], rg[:], 0.25, None, ALU.mult).then_inc(step, 1)
                dve.wait_ge(step, base + NWT + 2)
                if type(jj) is not int or 2 * jj + half > 0:
                    dve.wait_ge(q["oa_done"], 2 * jj + half)
                dve.wait_ge(q["out_done"], 2 * jj + half + 1)
                for t in range(2):
                    tt = 2 * half + t
                    last = nc.vector.scalar_tensor_tensor(out=acc[:, b * TB + tt, :], in0=bank[6][:, t * D:(t + 1) * D],
                                                          scalar=rg[:, tt:tt + 1], in1=acc[:, b * TB + tt, :],
                                                          op0=ALU.mult, op1=ALU.add)
                last.then_inc(q["oa_done"], 1)

            dve.wait_ge(q["e_dt"], 2)
            for b in range(B):
                if b:
                    dve.wait_ge(q["oa_done"], 2 * NG * b)
                    dve.wait_ge(q["yb_done"], H * b)
                group_stage1(0, b)
                group_stage1(1, b)
                group_stage2(0, b)
                with dve.Fori(1, G - 1) as g:
                    group_stage1(g + 1, b)
                    group_stage2(g, b)
                group_stage2(G - 1, b)
                dve.wait_ge(q["c_cbm"], G * (b + 1))
                slots(dve, b, scan_slot)
            dve.wait_ge(q["oa_done"], 2 * NG * B)
            for b in range(B):
                part = slice(b * TB, (b + 1) * TB)
                link(nc.vector.tensor_tensor(acc[:, part, :], acc[:, part, :],
                                             gm[:, 0, 0, b, :].unsqueeze(1).to_broadcast([P, TB, D]), ALU.mult))
            nc.vector.tensor_tensor(x_sb[:], x_sb[:], acc[:], ALU.add).then_inc(q["x1_done"], 1)
            dve.wait_ge(q["x1_done"], 1)
            if stop == 0:
                return

            def experts(L):
                n0, nf = 2 * L + 1, FT[L]
                base = FT[0] * B if L else 0
                dve.wait_ge(q["d_sel"], 16 * (L + 1))
                nc.vector.tensor_copy(sel[:], selw).then_inc(q["sel_done"], 1)
                nc.vector.memset(zerob[:], 0.0).then_inc(q["zb_done"], 1)
                normalise(n0)
                if L == 0:
                    dve.wait_ge(q["rt_act"], 1)
                    link(nc.vector.tensor_scalar(pr[:], pr[:], 0.5, 0.5, ALU.mult, ALU.add))
                    link(nc.vector.tensor_tensor(prb[:], pr[:],
                                                 small[:, 2 * H:2 * H + E].unsqueeze(1).to_broadcast([P, NT, E]), ALU.add))
                    crit = prb
                else:
                    dve.wait_ge(q["rt_p"], 2)
                    z = bank[4][:, 0:NT * E].rearrange("p (t e) -> p t e", t=NT)
                    link(nc.vector.tensor_reduce(r1[:], z, mybir.AxisListType.X, ALU.max))
                    nc.vector.tensor_tensor(pr[:], z, r1[:].unsqueeze(2).to_broadcast([P, NT, E]), ALU.subtract)\
                        .then_inc(q["rt_dve"], 1)
                    dve.wait_ge(q["rt_act"], 2)
                    link(nc.vector.tensor_reduce(r1[:], pr[:], mybir.AxisListType.X, ALU.add))
                    link(nc.vector.reciprocal(r1[:], r1[:]))
                    link(nc.vector.tensor_tensor(pr[:], pr[:], r1[:].unsqueeze(2).to_broadcast([P, NT, E]), ALU.mult))
                    crit = pr
                theirs = crit[:].unsqueeze(2).to_broadcast([P, NT, E, E])
                own = crit[:].unsqueeze(3).to_broadcast([P, NT, E, E])
                lower = cst[:, C_LOWER:C_LOWER + E * E].rearrange("p (a c) -> p a c", a=E).unsqueeze(1)\
                    .to_broadcast([P, NT, E, E])
                nc.vector.tensor_tensor(cmpa[:], theirs, own, ALU.is_gt)
                link(nc.vector.tensor_tensor(cmpb[:], theirs, own, ALU.is_equal))
                link(nc.vector.tensor_tensor(cmpb[:], cmpb[:], lower, ALU.mult))
                link(nc.vector.tensor_tensor(cmpa[:], cmpa[:], cmpb[:], ALU.add))
                link(nc.vector.tensor_reduce(rank[:], cmpa[:], mybir.AxisListType.X, ALU.add))
                nc.vector.memset(comb[:, :, E:E1], 1.0)
                link(nc.vector.scalar_tensor_tensor(out=comb[:, :, 0:E], in0=rank[:], scalar=2.0, in1=pr[:],
                                                    op0=ALU.is_lt, op1=ALU.mult))
                if L:
                    link(nc.vector.tensor_reduce(r1[:], comb[:, :, 0:E], mybir.AxisListType.X, ALU.add))
                    link(nc.vector.reciprocal(r1[:], r1[:]))
                    link(nc.vector.tensor_tensor(comb[:, :, 0:E], comb[:, :, 0:E],
                                                 r1[:].unsqueeze(2).to_broadcast([P, NT, E]), ALU.mult))
                link(nc.vector.tensor_copy(cpb[:, :, 0, :], comb[:]))
                link(nc.vector.tensor_tensor(cpt[:], comb[:], cpb[:, :, 0, :], ALU.subtract))
                link(nc.vector.tensor_copy(cpb[:, :, 1, :], cpt[:]))
                nc.vector.tensor_tensor(cpb[:, :, 2, :], cpt[:], cpb[:, :, 1, :], ALU.subtract).then_inc(q["cp_done"], 1)
                split_rows(n0)
                dve.wait_ge(q["cpT_p"], L + 1)
                nc.vector.tensor_copy(cbT[:], bank[5][:, :].bitcast(bf16)[0:PIECES * E1, :]).then_inc(q["cbT_done"], 1)

                def hidden(f, b, buf):
                    n = base + nf * b + f
                    def since(name, m):
                        if type(m) is not int or m > 0:
                            dve.wait_ge(q[name], m)
                    if L == 0:
                        dve.wait_ge(q["fs_c"], n + 1)
                        since("fh_done", n - 1)
                        nc.vector.tensor_tensor(ua[:, buf, :], bank[0][:, :], sS[:, buf, :], ALU.mult)
                        nc.vector.scalar_tensor_tensor(out=uc[:, buf, :], in0=bank[1][:, :], scalar=0.5,
                                                       in1=sS[:, buf, :], op0=ALU.mult, op1=ALU.mult)\
                            .then_inc(q["fa_done"], 1)
                        since("fh_done", n)
                        dve.wait_ge(q["fth_done"], n + 1)
                        dve.wait_ge(q["fa_done"], n + 1)
                        nc.vector.scalar_tensor_tensor(out=fg[:], in0=fth[:, buf, :], scalar=1.0, in1=ua[:, buf, :],
                                                       op0=ALU.add, op1=ALU.mult).then_inc(q["zero_done"], 1)
                        since("fout", n - 1)
                        dve.wait_ge(q["zero_done"], n + 1)
                        nc.vector.tensor_tensor(hf[:, buf, :], fg[:], uc[:, buf, :], ALU.mult)\
                            .then_inc(q["fh_done"], 1)
                    else:
                        since("fh_done", n)
                        dve.wait_ge(q["fth_done"], n + 1)
                        nc.vector.scalar_tensor_tensor(out=fg[:], in0=fth[:, buf, :], scalar=1.0, in1=bank[0][:, :],
                                                       op0=ALU.add, op1=ALU.mult).then_inc(q["zero_done"], 1)
                        since("fout", n - 1)
                        dve.wait_ge(q["zero_done"], n + 1)
                        nc.vector.scalar_tensor_tensor(out=hf[:, buf, :], in0=fg[:], scalar=0.5, in1=bank[2][:, :],
                                                       op0=ALU.mult, op1=ALU.mult).then_inc(q["fa_done"], 1)
                        dve.wait_ge(q["fa_done"], n + 1)
                        dve.sem_inc(q["fh_done"], 1)

                for b in range(B):
                    for m in range(2):
                        hidden(m, b, m)
                    with dve.Fori(1, (nf - 1) // 2) as i:
                        for m in range(2):
                            hidden(2 * i + m, b, m)
                    hidden(nf - 1, b, 0)
                    dve.wait_ge(q["fout"], base + nf * (b + 1))
                    for m in range(2):
                        last = nc.vector.tensor_tensor(xo[:, 2 * m:2 * m + 2, :],
                                                       bank[6 + m][:, :].rearrange("p (t d) -> p t d", t=2),
                                                       gm[:, L, 1, b, :].unsqueeze(1).to_broadcast([P, 2, D]), ALU.mult)
                    link(last)
                    part = slice(b * TB, (b + 1) * TB)
                    nc.vector.tensor_tensor(x_sb[:, part, :], x_sb[:, part, :], xo[:], ALU.add).then_inc(q["xf_done"], 1)
                    dve.wait_ge(q["xf_done"], L * B + b + 1)

            experts(0)
            if stop == 1:
                return

            def heads():
                normalise(2)
                nc.vector.tensor_copy(iotak[:].rearrange("p s k h -> p (s k) h"),
                                      cst[:, C_IOTA:C_IOTA + 2 * K].unsqueeze(2).to_broadcast([P, 2 * K, QG]))
                nc.vector.tensor_copy(selQ[:], identb[:].rearrange("p (g h) -> p g h", h=QG).unsqueeze(2)
                                      .to_broadcast([P, NQ, K, QG]))
                block4 = cst[:, C_BLOCK:C_BLOCK + QG]
                link(nc.vector.tensor_copy(VW[:, :, :, 4], block4.unsqueeze(1).to_broadcast([P, NQ, QG])))
                for b in range(B):
                    dve.wait_ge(q["a_qkc"], b + 1)
                    link(nc.vector.tensor_copy(qp[:, 0, b, :], qs[:, b, :]))
                    link(nc.vector.tensor_tensor(rk[:], qs[:, b, :], qp[:, 0, b, :], ALU.subtract))
                    link(nc.vector.tensor_copy(qp[:, 1, b, :], rk[:]))
                    link(nc.vector.tensor_tensor(qp[:, 2, b, :], rk[:], qp[:, 1, b, :], ALU.subtract))
                nc.vector.memset(m8[:], 0.0).then_inc(q["a_qp"], B)
                dve.wait_ge(q["a_qp"], B)
                for b in range(B):
                    for side in range(2):
                        if side == 0:
                            link(nc.vector.tensor_copy(wk[:, 0, ::-1], ks[:, b, :]))
                        else:
                            link(nc.vector.tensor_scalar(wk[:, 0, :], ks[:, b, :], -1.0, None, ALU.mult))
                        src = 0
                        for r in range(K // 8):
                            link(nc.vector.max(m8[:, r % 2, :], wk[:, src, :]))
                            if r == 0:
                                link(nc.vector.tensor_scalar(ext[:, b, side:side + 1], m8[:, 0, 0:1],
                                                             1.0 - 2.0 * side, None, ALU.mult))
                            dst = 1 + r % 2
                            link(nc.vector.match_replace(wk[:, dst, :], m8[:, r % 2, :], wk[:, src, :], NEG))
                            src = dst
                        link(nc.vector.tensor_scalar(hit[:, 0, :], wk[:, src, :], NEG, None, ALU.is_equal))
                        link(nc.vector.tensor_tensor_scan(rk[:], hit[:, 0, :], hit[:, 0, :], 0.0, ALU.add, ALU.max))
                        link(nc.vector.scalar_tensor_tensor(out=code[:, side, :], in0=rk[:], scalar=float(side * K),
                                                            in1=hit[:, 0, :], op0=ALU.add, op1=ALU.mult))
                        if side == 0 and b:
                            dve.wait_ge(q["a_kT"], 2 * b)
                        link(nc.vector.tensor_scalar(kd[:, side, :], ks[:, b, :], ext[:, b, side:side + 1], None,
                                                     ALU.subtract))
                    nc.vector.tensor_tensor(code[:, 2, :], code[:, 0, ::-1], code[:, 1, :], ALU.add)\
                        .then_inc(q["a_code"], 1)
                    dve.wait_ge(q["a_code"], b + 1)
                    dve.sem_inc(q["a_kd"], 1)

                    dve.wait_ge(q["a_cT"], b + 1)
                    nc.vector.tensor_copy(cdT[:].rearrange("p t h -> p (t h)"),
                                          bank[2][:, :].bitcast(bf16)[:, 0:TB * P]).then_inc(q["a_cTc"], 1)
                    dve.wait_ge(q["a_cTc"], b + 1)
                    for t in range(TB):
                        for side in range(2):
                            last = nc.vector.tensor_tensor(
                                OH[:, t, side].rearrange("p g (k h) -> p g k h", h=QG),
                                cdT[:, t, :].rearrange("p (g h) -> p g h", h=QG).unsqueeze(2).to_broadcast([P, NQ, K, QG]),
                                iotak[:, side].unsqueeze(1).to_broadcast([P, NQ, K, QG]), ALU.is_equal)
                    last.then_inc(q["a_oh"], 1)

                    def pieces(src, qq, cnt):
                        out = lambda pc: PV[:, :, pc, :, qq]
                        rr = pvr[:].rearrange("p (t h) -> p t h", t=TB)
                        link(nc.vector.tensor_copy(out(0), src))
                        link(nc.vector.tensor_tensor(rr, src, out(0), ALU.subtract))
                        link(nc.vector.tensor_copy(out(1), rr))
                        link(nc.vector.tensor_tensor(out(2), rr, out(1), ALU.subtract))

                    for m in range(2):
                        dve.wait_ge(q["a_kT"], 2 * b + m + 1)
                        pieces(bank[3 + m][:, :].rearrange("p (t h) -> p t h", t=TB), m, None)
                    nc.vector.memset(m8[:, 0, :], 0.0).then_inc(q["a_pv"], 3)
                    dve.wait_ge(q["a_pv"], 3 * (b + 1))
                    dve.wait_ge(q["a_v"], b + 1)
                    for j in range(2):
                        for half in range(2):
                            src = bank[5 + half][:, :].rearrange("p (t j h) -> p t j h", t=2, j=2)[:, :, j, :]
                            out = lambda pc: PV[:, 2 * half:2 * half + 2, pc, :, 2 + j]
                            rr = pvr[:, 0:2 * P].rearrange("p (t h) -> p t h", t=2)
                            link(nc.vector.tensor_copy(out(0), src))
                            link(nc.vector.tensor_tensor(rr, src, out(0), ALU.subtract))
                            link(nc.vector.tensor_copy(out(1), rr))
                            link(nc.vector.tensor_tensor(out(2), rr, out(1), ALU.subtract))
                    nc.vector.memset(m8[:, 1, :], 0.0).then_inc(q["a_vp"], 1)
                    dve.wait_ge(q["a_vp"], b + 1)

                    st = q["a_iota"]
                    with dve.Fori(0, NQ // 4) as n:
                        c = NQ // 4 * b + n
                        s0 = 6 * c
                        dve.wait_ge(q["a_vw"], c + 1)
                        nc.vector.tensor_reduce(gat[:], bank[7][:, 0:384].rearrange("p (a c x) -> p a x c", a=8, c=3),
                                                mybir.AxisListType.X, ALU.add).then_inc(q["a_gat"], 1)
                        dve.wait_ge(q["a_gat"], c + 1)
                        nc.vector.tensor_tensor(gam[:].rearrange("p a (h x) -> p a h x", h=QG),
                                                gat[:].rearrange("p a (h x) -> p a h x", h=QG),
                                                block4.unsqueeze(1).unsqueeze(3).to_broadcast([P, 8, QG, 4]),
                                                ALU.mult).then_inc(st, 1)
                        dve.wait_ge(st, 5 * c + 1)
                        for side in range(2):
                            gv_ = gam[:].rearrange("p (a s) (h x) -> p a s h x", s=2, h=QG)[:, :, side]
                            nc.vector.tensor_reduce(scl[:, bass.ds(4 * n, 4), side], gv_[:, :, :, side],
                                                    mybir.AxisListType.X, ALU.add).then_inc(st, 1)
                            nc.vector.tensor_copy(VW[:, bass.ds(4 * n, 4), :, 2 * side:2 * side + 2], gv_[:, :, :, 2:4])\
                                .then_inc(st, 1)
                        dve.wait_ge(st, 5 * c + 5)
                    dve.sem_inc(q["a_tbr"], 1)

                    def least(i, n):
                        c = NQ * b + 4 * n + i
                        if not (type(c) is int and c < 2):
                            dve.wait_ge(q["a_E"], c - 1)
                        dve.wait_ge(q["a_tb"], c + 1)
                        nc.vector.scalar_tensor_tensor(out=arg[:, i % 2, :], in0=bank[i % 2][:, :],
                                                       scalar=scl[:, bass.ds(4 * n + i, 1), 0:1].squeeze(1),
                                                       in1=tb_[:, i % 2, :], op0=ALU.mult, op1=ALU.min)\
                            .then_inc(q["a_arg"], 1)

                    def collect(n):
                        c = NQ // 4 * b + n
                        dve.wait_ge(q["a_PV"], NQ * b + 4 * n + 4)
                        nc.vector.tensor_copy(
                            O5[:, :, bass.ds(16 * n, 16), :].rearrange("p t (g h) c -> p g t (h c)", g=4),
                            bank[2][:, 0:320].rearrange("p (g t x) -> p g t x", g=4, t=TB)).then_inc(q["a_O5"], 1)

                    for i in range(4):
                        least(i, 0)
                    with dve.Fori(1, NQ // 4) as n:
                        for i in range(4):
                            least(i, n)
                            if i == 1:
                                collect(n - 1)
                    collect(NQ // 4 - 1)
                    dve.wait_ge(q["a_O5"], NQ // 4 * (b + 1))
                    dve.wait_ge(q["a_qT"], b + 1)
                    link(nc.vector.tensor_scalar(qm.rearrange("p t h -> p (t h)"), bank[3][:, :], 0.0, None, ALU.is_gt))
                    link(nc.vector.reciprocal(rden, O5[:, :, :, 4]))
                    for j in range(2):
                        link(nc.vector.copy_predicated(O5[:, :, :, 2 + j], qm.bitcast(mybir.dt.uint32), O5[:, :, :, j]))
                    if b:
                        dve.wait_ge(q["a_attT"], b)
                    for j in range(2):
                        last = nc.vector.tensor_tensor(att[:, :, :, j], O5[:, :, :, 2 + j], rden, ALU.mult)
                    last.then_inc(q["a_att"], 1)
                    dve.wait_ge(q["a_out"], b + 1)
                    dve.wait_ge(q["a_att"], b + 1)
                    xo1 = wk[:, 0:2, :].rearrange("p a (t d) -> p (a t) d", t=2)
                    for m in range(2):
                        last = nc.vector.tensor_tensor(xo1[:, 2 * m:2 * m + 2, :],
                                                       bank[(6, 3)[m]][:, :].rearrange("p (t d) -> p t d", t=2),
                                                       gm[:, 1, 0, b, :].unsqueeze(1).to_broadcast([P, 2, D]), ALU.mult)
                    link(last)
                    part = slice(b * TB, (b + 1) * TB)
                    nc.vector.tensor_tensor(x_sb[:, part, :], x_sb[:, part, :], xo1, ALU.add).then_inc(q["a_x"], 1)
                    dve.wait_ge(q["a_x"], b + 1)

            heads()
            if stop == 2:
                return
            experts(1)

        @block.gpsimd
        def _(pool):
            count = [0]

            def link(ins):
                count[0] += 1
                ins.then_inc(q["pool_seq"], 1)
                pool.wait_ge(q["pool_seq"], count[0])

            pool.wait_ge(q["d_small"], 64)
            nc.gpsimd.tensor_scalar(bcp[:], bcp[:], 0.5, None, ALU.mult).then_inc(q["bcp_done"], 1)
            pool.wait_ge(q["d_wbc"], 16)
            link(nc.gpsimd.tensor_copy(wbs[:, 0], wbf))
            nc.gpsimd.tensor_tensor(wbs[:, 1], wbf, wbs[:, 0], ALU.subtract).then_inc(q["wbs_done"], 1)
            pool.wait_ge(q["whi_done"], 1)
            nc.gpsimd.tensor_tensor(whl[:, 0, 1, :], wA[:, 0, :], whl[:, 0, 0, :], ALU.subtract)\
                .then_inc(q["wsplit"], 1)

            def scan_slot(i, it, b):
                head = stages(i, it)
                h1, h2, h3, h4 = head(0), head(1), head(2), head(3)
                n1, n2, n3, n4 = (H * b + 8 * h[1] + h[0] if h else None for h in (h1, h2, h3, h4))

                def since(name, n):
                    if type(n) is not int or n > 0:
                        pool.wait_ge(q[name], n)

                if h1:
                    nx = (i + 1) % 2
                    pool.wait_ge(q["whi_done"], n1 + 2)
                    nc.gpsimd.tensor_tensor(whl[:, nx, 1, :], wA[:, nx, :], whl[:, nx, 0, :],
                                            ALU.subtract).then_inc(q["wsplit"], 1)
                    pool.wait_ge(d_wB[i], 16 * (H // 8 * b + h1[1] + 1))
                    nc.gpsimd.tensor_tensor(wB[:, i, 0:D], wB[:, i, 0:D],
                                            wB[:, i, D + 6:D + 7].to_broadcast([P, D]), ALU.mult)\
                        .then_inc(q["wo_done"], 1)
                if h2:
                    j = h2[0]
                    hcol = 8 * h2[1] + h2[0]
                    since("ps", n2 - 1)
                    pool.wait_ge(q["xdt_done"], n2 + 1)
                    nc.gpsimd.tensor_tensor(
                        Xw[:, j % 2, :].rearrange("p (t n) -> p t n", n=P),
                        Xdt[:, j % 2, 0:S - P].rearrange("p (t n) -> p t n", n=P),
                        dec[:, b * TB:b * TB + TB - 1, bass.ds(hcol, 1)].to_broadcast([P, TB - 1, P]),
                        ALU.mult).then_inc(q["xw_done"], 1)
                if h2:
                    since("py", n2 - 1)
                    pool.wait_ge(q["e_done"], n2 + 1)
                    nc.gpsimd.tensor_tensor(CE[:, j % 2, :], CT[:, j, P:S], Em[:, j % 2, :], ALU.mult)\
                        .then_inc(q["ce_done"], 1)
                if h4:
                    j = h4[0]
                    jj = NG * b + 2 * h4[1] + j // 4
                    m = j % HG
                    if m:
                        if m > 1:
                            pool.wait_ge(q["sq_add"], 3 * jj + m - 1)
                        pool.wait_ge(q["ysq_done"], n4 + 1)
                        nc.gpsimd.tensor_tensor(sqa[:, j // 4, :], sqa[:, j // 4, :], ysq[:], ALU.add)\
                            .then_inc(q["sq_add"], 1)
                if h3:
                    j = h3[0]
                    jj = NG * b + 2 * h3[1] + j // 4
                    since("out_done", 2 * jj - 2)
                    pool.wait_ge(q["gs_done"], n3 + 1)
                    pool.wait_ge(q["yc_done"], n3 + 1)
                    nc.gpsimd.tensor_tensor(yb[:, j, :], yv[:, j % 2, :], gs[:, j % 4, :], ALU.mult)\
                        .then_inc(q["yb_done"], 1)

            for b in range(B):
                pool.wait_ge(q["c_btok"], G * (b + 1))
                pool.wait_ge(q["c_cbm"], G * (b + 1))
                slots(pool, b, scan_slot)

            for L in range(2):
                if stop is not None and stop < 2 * L + 1:
                    return
                w = 512 if L == 0 else 256
                for f in range(FT[L]):
                    pool.wait_ge(q["fw_hi"], (FT[0] if L else 0) + f + 1)
                    nc.gpsimd.tensor_tensor(w13s[:, 1, f, 0:w], w13[:, f, 0:w], w13s[:, 0, f, 0:w], ALU.subtract)\
                        .then_inc(q["fw_done"], 1)


def out_event(i, it):
    for half, back in ((0, 4), (1, 5)):
        j, n = i - back, it
        if j < 0:
            j, n = j + 8, it - 1
        if j % 4 == 3:
            if type(n) is int and not 0 <= n < H // 8:
                return None
            return half, j // 4, 2 * n + j // 4
    return None


def kernel(**inputs):
    import numpy as np
    import concourse.bacc as bacc
    from concourse.bass_utils import run_bass_kernel_spmd

    def a(name):
        return np.asarray(inputs[name])

    f32 = np.float32
    I, GN = H * P, G * P
    rows = a("L0_attn_in_proj_w")

    def km(w):
        n, m, _ = w.shape
        return w.reshape(n, m, KT, P).transpose(3, 0, 2, 1)

    gate = km(rows[0:I].reshape(H, P, D))
    xs = km(rows[I:2 * I].reshape(H, P, D))
    win = np.stack([xs, gate], axis=2).transpose(1, 0, 2, 3, 4).reshape(H, P, 512)
    Bw = km(rows[2 * I:2 * I + GN].reshape(G, P, D))
    Cw = km(rows[2 * I + GN:2 * I + 2 * GN].reshape(G, P, D))
    wbc = np.stack([Bw, Cw], axis=2).reshape(P, G, 512)
    wdt = rows[2 * I + 2 * GN:].reshape(H, KT, P).transpose(2, 1, 0)
    cw, cb = a("L0_attn_conv_w")[:, 0, :], a("L0_attn_conv_b")
    chan = np.concatenate([cw, cb[:, None]], axis=1)
    wob = np.concatenate([
        a("L0_attn_out_proj_w").T.reshape(H, P, D),
        chan[0:I].reshape(H, P, 5),
        np.broadcast_to(a("L0_attn_D")[:, None, None], (H, P, 1)),
        a("L0_attn_norm_w").reshape(H, P, 1),
        np.zeros((H, P, 1), f32)], axis=2)
    bcp = np.stack([chan[I:I + GN].reshape(G, P, 5), chan[I + GN:].reshape(G, P, 5)], axis=2).transpose(1, 0, 2, 3)
    eye = np.eye(P, dtype=f32)
    stack = np.concatenate([np.tile(np.eye(H, dtype=f32), (PIECES, 1)), np.zeros((P - PIECES * H, H), f32)])
    k1 = np.arange(P)[:, None]
    lower = np.tril(np.ones((E, E), f32), -1).reshape(1, E * E)
    iota = np.arange(1, 2 * K + 1, dtype=f32)[None]
    consts = np.concatenate([
        eye, np.triu(np.ones((P, P), f32)), np.ones((P, P), f32), stack,
        np.broadcast_to(lower, (P, E * E)), (k1 % QG == np.arange(QG)).astype(f32),
        np.broadcast_to(iota, (P, 2 * K))], axis=1)
    expert = [np.arange(FT[0] * P) // P, np.minimum(np.arange(FT[1] * P) // HID1, E)]
    sel = np.concatenate([(e[None] == np.arange(E1)[:, None]).astype(f32) for e in expert], axis=1)
    w13_0 = np.stack([km(np.concatenate([a("L0_ffn_w1"), a("L0_ffn_sw1")[None]])),
                      km(np.concatenate([a("L0_ffn_w3"), a("L0_ffn_sw3")[None]]))], axis=2).reshape(P, E1, 512)
    w2_0 = np.concatenate([a("L0_ffn_w2"), a("L0_ffn_sw2")[None]]).transpose(2, 0, 1)
    pad = FT[1] * P - E1 * HID1
    in1 = np.concatenate([a("L1_ffn_w1"), a("L1_ffn_w_shared1")[None]]).transpose(1, 0, 2).reshape(D, E1 * HID1)
    in1 = np.concatenate([in1, np.zeros((D, pad), f32)], axis=1)
    w13_1 = in1.reshape(KT, P, FT[1], P).transpose(1, 2, 0, 3).reshape(P, FT[1], 256)
    out1 = np.concatenate([a("L1_ffn_w2"), a("L1_ffn_w_shared2")[None]]).reshape(E1 * HID1, D)
    w2_1 = np.concatenate([out1, np.zeros((pad, D), f32)]).reshape(FT[1], P, D).transpose(1, 0, 2)
    router = np.stack([a("L0_ffn_gate_w").T, a("L1_ffn_w_router")]).reshape(2, KT, P, E).transpose(2, 0, 1, 3)
    wqk = np.stack([a("L1_attn_Wq").T, a("L1_attn_Wk").T]).reshape(2, KT, P, P).transpose(2, 0, 1, 3)
    wv = a("L1_attn_Wv").reshape(P, 2, D).transpose(2, 1, 0).reshape(KT, P, D).transpose(1, 0, 2)
    wo = a("L1_attn_Wo").T.reshape(KT, P, D).transpose(1, 0, 2)
    feeds = {
        "sel": np.tile(sel, (PIECES, 1)), "w13_0": w13_0, "w2_0": w2_0, "w13_1": w13_1, "w2_1": w2_1,
        "router": router, "wqk": wqk, "wv": wv, "wo": wo,
        "x": a("L0_attn_x").reshape(T, D),
        "cst": consts,
        "cT": np.stack([a("L0_c"), a("L1_c")]).reshape(2, B, KT, P).transpose(3, 0, 2, 1).reshape(P, 2 * KT * B),
        "wmod": np.stack([a("L0_wmod"), a("L1_wmod")]).reshape(2, KT, P, 6 * D).transpose(0, 2, 1, 3),
        "small": np.concatenate([a("L0_attn_dt_bias"), a("L0_attn_A_log"), a("L0_ffn_expert_bias")]),
        "wdt": wdt, "bcp": bcp, "wbc": wbc, "win": win, "wob": wob,
    }
    nc = bacc.Bacc("TRN2", target_bir_lowering=False, num_devices=1)
    feeds = {n: np.ascontiguousarray(v) for n, v in feeds.items()}
    io = {n: nc.dram_tensor(f"in_{n}", v.shape, mybir.dt.from_np(v.dtype), kind="ExternalInput").ap()
          for n, v in feeds.items()}
    io["out"] = nc.dram_tensor("out", (T, D), mybir.dt.float32, kind="ExternalOutput").ap()
    build_block(nc, io)
    r = run_bass_kernel_spmd(nc, [{f"in_{n}": v for n, v in feeds.items()}], core_ids=[0])
    return r.results[0]["out"].reshape(B, S, D)
```

```python
from contextlib import ExitStack

import concourse.bass as bass
from concourse import mybir

B, S, D = 2, 512, 256
T = B * S
P = 128
KT = D // P
NT = T // P
TB = S // P
H = 32
G = 8
NG = 8
HG = H // NG
LN_EPS = 1e-5
RMS_EPS = 1e-6
E = 8
E1 = E + 1
HID1 = 176
FT = (E1, -(-E1 * HID1 // P))
K = 32
QG = 4
NQ = P // QG
NEG = -3.0e38
CST = 3 * P + H + E * E + QG + 2 * K
C_STACK = 3 * P
C_LOWER = C_STACK + H
C_BLOCK = C_LOWER + E * E
C_IOTA = C_BLOCK + QG
CH = 8
MASKED = -1.0e30
PIECES = 3


def build_block(nc, io, stop=None):
    fp32, bf16, i32 = mybir.dt.float32, mybir.dt.bfloat16, mybir.dt.int32
    ALU = mybir.AluOpType
    ACT = mybir.ActivationFunctionType
    ctx = ExitStack()
    with ctx:
        def sb(name, shape, dt=fp32):
            return ctx.enter_context(nc.sbuf_tensor(name, shape, dt))

        def sem(name):
            return ctx.enter_context(nc.semaphore(name))

        bank = [ctx.enter_context(nc.psum_tensor(f"bank{n}", [P, 512], fp32)) for n in range(8)]

        x_sb = sb("x_sb", [P, NT, D])
        acc = sb("acc", [P, NT, D])
        xT = sb("xT", [P, 4, S])
        hT = xT[:, :, :].rearrange("p (k c) s -> p k (c s)", k=KT)
        hTs = sb("hTs", [P, 2, KT, T], bf16)
        cst = sb("cst", [P, CST])
        ident, tri, ones = cst[:, 0:P], cst[:, P:2 * P], cst[:, 2 * P:3 * P]
        identb = sb("identb", [P, P], bf16)
        identb96 = sb("identb96", [PIECES * H, 2, H], bf16)
        maskb = sb("maskb", [P, P], bf16)
        cT = sb("cT", [P, 2 * KT * B])
        sc = sb("sc", [P, 2 * KT * B])
        mods = sb("mods", [P, 2, 4, KT, B])
        gm = sb("gm", [P, 2, 2, B, D])
        small = sb("small", [P, 2 * H + E])
        wdt = sb("wdt", [P, KT, H])
        bcp = sb("bcp", [P, G, 2, 5])
        stats = sb("stats", [P, NT, 6])
        mv = sb("mv", [P, NT, 2])
        rstd = sb("rstd", [P, NT])
        nwt = sb("nwt", [P, 3, NT])
        router = sb("router", [P, 2, KT, E])
        later = ExitStack()
        resident_sb = sb
        scan = ctx.enter_context(ExitStack())

        def sb(name, shape, dt=fp32):
            return scan.enter_context(nc.sbuf_tensor(name, shape, dt))

        dtv = sb("dtv", [P, NT, H])
        cs = sb("cs", [P, NT, H])
        dec = sb("dec", [P, NT, H])
        etot = sb("etot", [P, NT, H])
        csp = sb("csp", [P, NT, PIECES, H], bf16)
        csT = sb("csT", [PIECES * H, T], bf16)
        wbs = sb("wbs", [P, 2, G, 512], bf16)
        CB = sb("CB", [P, G, TB, P])
        Btok = sb("Btok", [P, G, TB, P])
        CT = sb("CT", [P, G, S])
        BT = sb("BT", [P, S])
        wA = sb("wA", [P, 2, 512])
        whl = sb("whl", [P, 2, 2, 512], bf16)
        wB = sb("wB", [P, 8, D])
        chn = sb("chn", [P, H, CH])
        raw = sb("raw", [P, 2, S + 3])
        u = sb("u", [P, 2, S])
        thx = sb("thx", [P, S])
        thg = sb("thg", [P, S])
        gs = sb("gs", [P, 4, S])
        Lm = sb("Lm", [P, 2, S])
        scb = Lm[:, :, :].rearrange("p a (b n) -> p (a b) n", n=P)
        Em = sb("Em", [P, 2, S - P])
        Mm = sb("Mm", [P, 2, S])
        dtmp = Mm[:, :, :].rearrange("p a (b t h) -> p (a b) t h", t=NT, h=H)
        xbuf = sb("xbuf", [P, 2 * S + 6 * (S - P)])
        Xdt = xbuf[:, 0:2 * S].rearrange("p (a n) -> p a n", a=2)
        Xw, CE, St = (xbuf[:, 2 * S + 2 * m * (S - P):2 * S + 2 * (m + 1) * (S - P)].rearrange("p (a n) -> p a n", a=2)
                      for m in range(3))
        yv = sb("yv", [P, 2, S])
        yb = sb("yb", [P, 8, S])
        ysq = sb("ysq", [P, S])
        sqa = sb("sqa", [P, 2, S])
        ssv = sb("ssv", [P, TB])
        rg = sb("rg", [P, TB])
        wm = yb[:, :, :].rearrange("p a b -> p (a b)")[:, 0:KT * 6 * D].rearrange(
            "p (k n) -> p k n", k=KT)
        rawg = xbuf[:, 0:4 * (S + 3)].rearrange("p (a n) -> p a n", a=4)
        wm1 = Btok[:, :, :, :].rearrange("p a b c -> p (a b c)")[:, 0:KT * 6 * D].rearrange(
            "p (k n) -> p k n", k=KT)
        wbf = CB[:, :, :, :].rearrange("p a b c -> p a (b c)")

        yv_sign = yb[:, 0:4, :].rearrange("p a b -> p (a b)")

        scan.close()
        def sb(name, shape, dt=fp32):
            return later.enter_context(nc.sbuf_tensor(name, shape, dt))

        sel = sb("sel", [PIECES * E1, sum(FT) * P], bf16)
        F1 = max(FT)
        w13 = sb("w13", [P, F1, 512])
        w13s = sb("w13s", [P, 2, F1, 512], bf16)
        w2 = sb("w2", [P, F1, D])
        selw = w2[0:PIECES * E1, :, :].rearrange("p f d -> p (f d)")[:, 0:sum(FT) * P]
        pr = sb("pr", [P, NT, E])
        prb = sb("prb", [P, NT, E])
        rank = sb("rank", [P, NT, E])
        cmpa = sb("cmpa", [P, NT, E, E])
        cmpb = sb("cmpb", [P, NT, E, E])
        comb = sb("comb", [P, NT, E1])
        cpt = sb("cpt", [P, NT, E1])
        cpb = sb("cpb", [P, NT, PIECES, E1], bf16)
        cbT = sb("cbT", [PIECES * E1, T], bf16)
        r1 = sb("r1", [P, NT])
        sS = sb("sS", [P, 2, S])
        ua = sb("ua", [P, 2, S])
        uc = sb("uc", [P, 2, S])
        fth = sb("fth", [P, 2, S])
        fg = sb("fg", [P, S])
        hf = sb("hf", [P, 2, S])
        xo = sb("xo", [P, TB, D])
        zerob = sb("zerob", [P, P + S], bf16)
        later.close()
        def sb(name, shape, dt=fp32):
            return ctx.enter_context(nc.sbuf_tensor(name, shape, dt))

        wqk = sb("wqk", [P, 2, KT, P])
        wv = sb("wv", [P, KT, D])
        wo = sb("wo", [P, KT, D])
        qs = sb("qs", [P, B, S])
        qp = sb("qp", [P, PIECES, B, S], bf16)
        ks = sb("ks", [P, B, S])
        wk = sb("wk", [P, 3, S])
        m8 = sb("m8", [P, 2, 8])
        ext = sb("ext", [P, B, 2])
        hit = sb("hit", [P, 2, S])
        rk = sb("rk", [P, S])
        code = sb("code", [P, 3, S], bf16)
        cdT = sb("cdT", [P, TB, P], bf16)
        kd = sb("kd", [P, 2, S])
        PV = sb("PV", [P, TB, PIECES, P, 4], bf16)
        pvr = sb("pvr", [P, TB * P])
        iotak = sb("iotak", [P, 2, K, QG], bf16)
        selQ = sb("selQ", [P, NQ, K, QG], bf16)
        OH = sb("OH", [P, TB, 2, NQ, P], bf16)
        gat = sb("gat", [P, 8, 16])
        gam = sb("gam", [P, 8, 16])
        scl = sb("scl", [P, NQ, 2])
        VW = sb("VW", [P, NQ, QG, 5])
        tb_ = sb("tb", [P, 2, S])
        arg = sb("arg", [P, 2, S])
        Ex = sb("Ex", [P, 4, S])
        ohf = OH[:, :, :, :, :].rearrange("p t s g m -> p (t s g m)").bitcast(fp32)
        O5 = ohf[:, 0:2560].rearrange("p (t h c) -> p t h c", t=TB, c=5)
        qm = ohf[:, 2560:3072].rearrange("p (t h) -> p t h", t=TB)
        rden = ohf[:, 3072:3584].rearrange("p (t h) -> p t h", t=TB)
        att = ohf[:, 3584:4608].rearrange("p (t h j) -> p t h j", t=TB, j=2)
        attT = ohf[:, 4608:5632].rearrange("p (k s) -> p k s", k=KT)
        attf = att.rearrange("p t h j -> p t (h j)")

        names = ("d_cst d_x d_c d_wm0 d_wm1 d_small d_wbc d_out "
                 "modp_done gmod_done sc_done mods_done gm_done thc_done scb_done "
                 "dve_seq pool_seq act_seq xh_done tr_done hT_done hts_done "
                 "dtp_done dtz_done dta_done dcs_done dex_done csp_done cspT_done csT_done e_dt "
                 "bcp_done wbs_hi wbs_done idb_done "
                 "c_proj c_raw c_step c_th c_bc c_mm c_evac d_chn pad_done "
                 "wsplit whi_done wo_done px raw_done tr_x xdt_done pg thg_done gs_done pc pc2 e_done L_done "
                 "M_done c0_done cv_step thx_done xT_done xw_done ce_done ps rc_step py yc_done "
                 "yb_done ysq_done sq_add ssq_done out_done rg_step oa_done "
                 "x1_done "
                 "d_sel d_w13 d_w2 d_attn sel_done zb_done "
                 "rt_p rt_act rt_dve cp_done cpT_p cbT_done fw_hi fw_done "
                 "fu fs_c fa_done fth_done fh_done fout zero_done xf_done "
                 "a_qk a_v a_qkc a_code a_cT a_cTc a_kd a_kT a_pv a_vp a_oh a_gat a_vw a_iota "
                 "a_qp a_Q a_tb a_arg a_E a_PV a_O5 a_qT a_qm a_att a_attT a_attc a_out a_x a_tbr").split()
        q = {n: sem(n) for n in names}
        d_wA = [sem(f"d_wA{n}") for n in range(2)]
        d_wB = [sem(f"d_wB{n}") for n in range(8)]

        block = ctx.enter_context(nc.Block())

        NWT = 13
        ROOT = 12

        def rsqrt_steps(dve, out, v, tmp, step, first):
            n = first
            nc.vector.tensor_scalar(tmp[0].bitcast(i32), v.bitcast(i32), 1, None,
                                    ALU.logical_shift_right).then_inc(step, 1)
            dve.wait_ge(step, n + 1)
            nc.vector.tensor_scalar(out.bitcast(i32), tmp[0].bitcast(i32), -1.0, float(0x5f3759df),
                                    ALU.mult, ALU.add).then_inc(step, 1)
            n = 2
            for _ in range(3):
                dve.wait_ge(step, first + n)
                nc.vector.tensor_tensor(tmp[0], out, out, ALU.mult).then_inc(step, 1)
                dve.wait_ge(step, first + n + 1)
                nc.vector.scalar_tensor_tensor(out=tmp[1], in0=tmp[0], scalar=-0.5, in1=v, op0=ALU.mult,
                                               op1=ALU.mult).then_inc(step, 1)
                dve.wait_ge(step, first + n + 2)
                nc.vector.scalar_tensor_tensor(out=out, in0=tmp[1], scalar=1.5, in1=out, op0=ALU.add,
                                               op1=ALU.mult).then_inc(step, 1)
                n += 3
            dve.wait_ge(step, first + n)
            nc.vector.tensor_tensor(tmp[0], out, out, ALU.mult).then_inc(step, 1)
            dve.wait_ge(step, first + n + 1)
            nc.vector.scalar_tensor_tensor(out=tmp[1], in0=tmp[0], scalar=-0.5, in1=v, op0=ALU.mult,
                                           op1=ALU.mult).then_inc(step, 1)
            dve.wait_ge(step, first + n + 2)

        def slots(eng, b, slot):
            for i in range(8):
                slot(i, 0, b)
            with eng.Fori(1, 4) as it:
                for i in range(8):
                    slot(i, it, b)
            for i in range(7):
                slot(i, 4, b)

        def stages(i, it):
            def head(back):
                j, n = i - back, it
                if j < 0:
                    j, n = j + 8, it - 1
                if type(n) is int and not 0 <= n < H // 8:
                    return None
                return j, n
            return head

        @block.sync
        def _(sp):
            sp.dma_start(cT[:], io["cT"][:, :]).then_inc(q["d_c"], 16)
            sp.dma_start(x_sb[:], io["x"].rearrange("(t p) d -> p t d", p=P)).then_inc(q["d_x"], 16)
            sp.dma_start(wm, io["wmod"][0]).then_inc(q["d_wm0"], 16)
            sp.dma_start(cst[:], io["cst"][:, :]).then_inc(q["d_cst"], 16)
            sp.dma_start(small[:], io["small"].partition_broadcast(P)).then_inc(q["d_small"], 16)
            sp.dma_start(wdt[:], io["wdt"]).then_inc(q["d_small"], 16)
            sp.dma_start(bcp[:], io["bcp"]).then_inc(q["d_small"], 16)
            sp.dma_start(router[:], io["router"]).then_inc(q["d_small"], 16)
            sp.dma_start(wbf, io["wbc"]).then_inc(q["d_wbc"], 16)
            sp.dma_start(chn[:], io["chn"]).then_inc(q["d_chn"], 16)
            sp.dma_start(wm1, io["wmod"][1]).then_inc(q["d_wm1"], 16)

            def load_slot(i, it, b):
                def number(h):
                    k = 8 * h[1] + h[0]
                    return k if type(k) is int else sp.snap(k)

                head = stages(i, it)
                h0, h3 = head(0), head(3)
                if h0:
                    kk = number(h0)
                    split = H * b + kk - 1
                    if type(split) is not int:
                        split = sp.snap(split)
                    if type(split) is not int or split > 0:
                        sp.wait_ge(q["wsplit"], split)
                    sp.dma_start(wA[:, i % 2, :], io["win"][bass.ds(kk, 1)].squeeze(0)).then_inc(d_wA[i % 2], 16)
                if h3:
                    j, n = h3
                    kk = number(h3)
                    outs = TB * (NG * b + 2 * n + j // HG - 1)
                    if type(outs) is not int:
                        outs = sp.snap(outs)
                    if type(outs) is not int or outs > 0:
                        sp.wait_ge(q["out_done"], outs)
                    sp.dma_start(wB[:, j, :], io["wob"][bass.ds(kk, 1)].squeeze(0)).then_inc(d_wB[j], 16)

            for b in range(B):
                slots(sp, b, load_slot)
            sp.wait_ge(q["wsplit"], B * H - 1)
            sp.dma_start(wA[:, 0, :], io["win"][0]).then_inc(d_wA[0], 16)

            def experts_load(L):
                n = FT[L]
                if L == 0:
                    sp.wait_ge(q["x1_done"], 1)
                else:
                    sp.wait_ge(q["a_x"], B)
                sp.dma_start(selw, io["sel"]).then_inc(q["d_sel"], 16)
                sp.wait_ge(q["sel_done"], L + 1)
                sp.dma_start(w13[:, 0:n, 0:io[f"w13_{L}"].shape[2]], io[f"w13_{L}"]).then_inc(q["d_w13"], 16)
                sp.dma_start(w2[:, 0:n, :], io[f"w2_{L}"]).then_inc(q["d_w2"], 16)

            def store():
                sp.dma_start(io["out"].rearrange("(t p) d -> p t d", p=P), x_sb[:]).then_inc(q["d_out"], 16)
                sp.wait_ge(q["d_out"], 16)

            if stop == 0:
                sp.wait_ge(q["x1_done"], 1)
                return store()
            experts_load(0)
            sp.wait_ge(q["xf_done"], B)
            if stop == 1:
                return store()
            sp.dma_start(wqk[:], io["wqk"]).then_inc(q["d_attn"], 16)
            sp.dma_start(wv[:], io["wv"]).then_inc(q["d_attn"], 16)
            sp.dma_start(wo[:], io["wo"]).then_inc(q["d_attn"], 16)
            sp.wait_ge(q["a_x"], B)
            if stop == 2:
                return store()
            experts_load(1)
            sp.wait_ge(q["xf_done"], 2 * B)
            store()

        @block.tensor
        def _(pe):
            def modulation(L):
                w = (wm, wm1)[L]
                pe.wait_ge(q[f"d_wm{L}"], 16)
                for n, m in enumerate((0, 1, 3, 4)):
                    for ft in range(KT):
                        o = (n * KT + ft) * B
                        for kt in range(KT):
                            last = nc.tensor.matmul(
                                bank[4 - L][:, o:o + B], w[:, kt, m * D + ft * P:m * D + (ft + 1) * P],
                                sc[:, (L * KT + kt) * B:(L * KT + kt + 1) * B],
                                start=kt == 0, stop=kt == KT - 1)
                last.then_inc(q["modp_done"], 1)

            def gates():
                for L in range(2):
                    w = (wm, wm1)[L]
                    for n, m in enumerate((2, 5)):
                        for b in range(B):
                            o = (L * 2 + n) * B + b
                            for kt in range(KT):
                                last = nc.tensor.matmul(
                                    bank[4 + o // 2][:, (o % 2) * D:(o % 2 + 1) * D],
                                    scb[:, (L * KT + kt) * B + b, :], w[:, kt, m * D:(m + 1) * D],
                                    start=kt == 0, stop=kt == KT - 1)
                last.then_inc(q["gmod_done"], 1)

            pe.wait_ge(q["sc_done"], 1)
            modulation(0)

            def transposed_rows(n):
                for b in range(B):
                    pe.wait_ge(q["xh_done"], n * B + b + 1)
                    for ft in range(KT):
                        for t in range(TB):
                            last = nc.tensor.transpose(
                                bank[b * KT + ft][:, t * P:(t + 1) * P],
                                acc[:, b * TB + t, ft * P:(ft + 1) * P], ident)
                        last.then_inc(q["tr_done"], 1)

            pe.wait_ge(q["d_cst"], 16)
            transposed_rows(0)

            pe.wait_ge(q["hT_done"], 4)
            pe.wait_ge(q["d_small"], 64)
            for t in range(NT):
                for kt in range(KT):
                    last = nc.tensor.matmul(bank[4][:, t * H:(t + 1) * H], hT[:, kt, t * P:(t + 1) * P],
                                            wdt[:, kt, :], start=kt == 0, stop=kt == KT - 1)
            last.then_inc(q["dtp_done"], 1)
            pe.wait_ge(q["dta_done"], 1)
            ab = dtmp[:, 2, :, :].rearrange("p t h -> p (t h)")
            nc.tensor.matmul(bank[5][:, 0:NT * H], tri, ab, start=True, stop=True)
            nc.tensor.matmul(bank[6][:, 0:NT * H], ones, ab, start=True, stop=True).then_inc(q["dcs_done"], 1)
            pe.wait_ge(q["csp_done"], 1)
            pe.wait_ge(q["idb_done"], 2)
            cspT = bank[7][:, :].bitcast(bf16)
            for t in range(NT):
                last = nc.tensor.transpose(cspT[0:PIECES * H, t * P:(t + 1) * P],
                                           csp[:, t, :, :].rearrange("p a h -> p (a h)"), identb[:])
            last.then_inc(q["cspT_done"], 1)

            def split_product(out, wpart, hpart):
                n = 0
                for a, c in ((0, 0), (0, 1), (1, 0)):
                    for kt in range(KT):
                        last = nc.tensor.matmul(out, wpart(a, kt), hpart(c, kt), start=n == 0, stop=n == 5)
                        n += 1
                return last

            def group_rows(g, b):
                if not (type(g) is int and G * b + g == 0):
                    pe.wait_ge(q["c_raw"], G * b + g)
                for n in range(2):
                    last = split_product(
                        bank[n][:, :],
                        lambda a, kt: wbs[:, a, bass.ds(g, 1), (n * KT + kt) * P:(n * KT + kt + 1) * P].squeeze(1),
                        lambda a, kt: hTs[:, a, kt, b * S:(b + 1) * S])
                last.then_inc(q["c_proj"], 1)

            def group_products(g, b):
                pe.wait_ge(q["c_bc"], 2 * (G * b + g) + 2)
                if not (type(g) is int and G * b + g == 0):
                    pe.wait_ge(q["c_evac"], G * b + g)
                for t in range(TB):
                    last = nc.tensor.matmul(bank[2][:, t * P:(t + 1) * P], BT[:, t * P:(t + 1) * P],
                                            CT[:, bass.ds(g, 1), t * P:(t + 1) * P].squeeze(1), start=True, stop=True)
                for t in range(TB):
                    last = nc.tensor.transpose(bank[3][:, t * P:(t + 1) * P], BT[:, t * P:(t + 1) * P], ident)
                last.then_inc(q["c_mm"], 1)

            def scan_slot(i, it, b):
                head = stages(i, it)
                h0, h1, h2 = head(0), head(1), head(2)
                n0, n1, n2 = (H * b + 8 * h[1] + h[0] if h else None for h in (h0, h1, h2))

                def since(name, n):
                    if type(n) is not int or n > 0:
                        pe.wait_ge(q[name], n)

                if h0:
                    w = whl[:, i % 2, :, :]
                    pe.wait_ge(q["wsplit"], n0 + 1)
                    since("raw_done", n0)
                    split_product(bank[0][:, :], lambda a, kt: w[:, a, kt * P:(kt + 1) * P],
                                  lambda a, kt: hTs[:, a, kt, b * S:(b + 1) * S]).then_inc(q["px"], 1)
                if h1:
                    j = h1[0]
                    pe.wait_ge(q["xT_done"], n1 + 1)
                    since("xdt_done", n1)
                    for t in range(TB):
                        last = nc.tensor.transpose(bank[2][:, t * P:(t + 1) * P],
                                                   xT[:, j % 4, t * P:(t + 1) * P], ident)
                    last.then_inc(q["tr_x"], 1)
                if h2:
                    j = h2[0]
                    pe.wait_ge(q["rc_step"], 3 * n2 + 3)
                    pe.wait_ge(q["ce_done"], n2 + 1)
                    for c in range(1, TB):
                        last = nc.tensor.matmul(bank[5][:, c * P:(c + 1) * P], St[:, j % 2, (c - 1) * P:c * P],
                                                CE[:, j % 2, (c - 1) * P:c * P], start=False, stop=True,
                                                skip_group_check=True)
                    last.then_inc(q["py"], 1)
                if h0:
                    hcol = 8 * h0[1] + h0[0]
                    since("L_done", n0)
                    if type(n0) is int and n0 == 0:
                        pe.wait_ge(q["csT_done"], 1)
                    nc.tensor.matmul(
                        bank[3][:, :], identb96[:, 0, bass.ds(hcol, 1)].to_broadcast([PIECES * H, P]),
                        csT[:, b * S:(b + 1) * S], start=True, stop=True, skip_group_check=True)\
                        .then_inc(q["pc"], 1)
                out_slot(i, it, b)
                if h0:
                    pe.wait_ge(q["e_done"], n0 + 1)
                    for t in range(TB):
                        nc.tensor.matmul(bank[3][:, t * P:(t + 1) * P], csT[:, b * S + t * P:b * S + (t + 1) * P],
                                         identb96[:, 1, bass.ds(hcol, 1)].to_broadcast([PIECES * H, P]),
                                         start=False, stop=True, skip_group_check=True)
                    nc.tensor.matmul(bank[3][:, :], identb[:], maskb[:].unsqueeze(1).to_broadcast([P, TB, P]),
                                     start=False, stop=True, skip_group_check=True).then_inc(q["pc2"], 1)
                if h1:
                    since("rc_step", 3 * n1)
                if (e := out_event(i, it, 7)) and e[0] == 0:
                    pe.wait_ge(q["rg_step"], ROOT * (NG * b + e[2]) + 1)
                sums_slot(i, it, b)
                if h1:
                    j = h1[0]
                    pe.wait_ge(q["xw_done"], n1 + 1)
                    for c in range(TB - 1):
                        last = nc.tensor.matmul(bank[4][:, c * P:(c + 1) * P], Btok[:, j, c, :],
                                                Xw[:, j % 2, c * P:(c + 1) * P], start=True, stop=True)
                    last.then_inc(q["ps"], 1)
                    pe.wait_ge(q["M_done"], n1 + 1)
                    since("yc_done", n1)
                    for c in range(TB):
                        nc.tensor.matmul(bank[5][:, c * P:(c + 1) * P], Xdt[:, j % 2, c * P:(c + 1) * P],
                                         Mm[:, j % 2, c * P:(c + 1) * P], start=c == 0, stop=c == 0,
                                         skip_group_check=True)
                if h0:
                    since("gs_done", n0)
                    split_product(bank[1][:, :], lambda a, kt: w[:, a, (KT + kt) * P:(KT + kt + 1) * P],
                                  lambda a, kt: hTs[:, a, kt, b * S:(b + 1) * S]).then_inc(q["pg"], 1)

            def sums_slot(i, it, b):
                e = out_event(i, it, 6)
                if not e or e[0]:
                    return
                _, j, gi = e
                jj = NG * b + gi
                if not stages(i, it)(1):
                    pe.wait_ge(q["rc_step"], 3 * H * (b + 1))
                pe.wait_ge(q["sq_add"], 3 * (jj + 1))
                for t in range(TB):
                    last = nc.tensor.matmul(bank[4][:, S - P + t:S - P + t + 1], sqa[:, j, t * P:(t + 1) * P], ones[:, 0:1],
                                            start=True, stop=True)
                last.then_inc(q["ssq_done"], 1)

            def out_slot(i, it, b):
                e = out_event(i, it, 6)
                if not e:
                    return
                t, j, gi = e
                jj = NG * b + gi
                y0 = HG * j
                if t == 0:
                    pe.wait_ge(q["wo_done"], HG * (jj + 1))
                    pe.wait_ge(q["yb_done"], HG * (jj + 1))
                if type(jj) is not int or TB * jj + t > 1:
                    pe.wait_ge(q["oa_done"], TB * jj + t - 1)
                for m in range(HG):
                    last = nc.tensor.matmul(bank[6 + t % 2][:, 0:D], yb[:, y0 + m, t * P:(t + 1) * P],
                                            wB[:, y0 + m, :], start=m == 0, stop=m == HG - 1)
                last.then_inc(q["out_done"], 1)

            for b in range(B):
                if b == 0:
                    pe.wait_ge(q["wbs_done"], 1)
                    pe.wait_ge(q["hts_done"], 4)
                else:
                    pe.wait_ge(q["oa_done"], TB * NG * b)
                group_rows(0, b)
                group_rows(1, b)
                if b == 0:
                    pe.wait_ge(q["scb_done"], 1)
                    pe.wait_ge(q["csT_done"], 1)
                    modulation(1)
                    gates()
                    pe.wait_ge(q["mods_done"], 2)
                group_rows(2, b)
                group_products(0, b)
                with pe.Fori(1, G - 2) as g:
                    group_rows(g + 2, b)
                    group_products(g, b)
                group_products(G - 2, b)
                group_products(G - 1, b)
                pe.wait_ge(q["c_evac"], G * (b + 1))
                pe.wait_ge(q["gm_done"], 4)
                slots(pe, b, scan_slot)
            if stop == 0:
                return

            def experts(L):
                n0, nf = 2 * L + 1, FT[L]
                w13n = 2 if L == 0 else 1
                transposed_rows(n0)
                pe.wait_ge(q["hT_done"], 4 * (n0 + 1))
                for t in range(NT):
                    for kt in range(KT):
                        last = nc.tensor.matmul(bank[4][:, t * E:(t + 1) * E], hT[:, kt, t * P:(t + 1) * P],
                                                router[:, L, kt, :], start=kt == 0, stop=kt == KT - 1)
                last.then_inc(q["rt_p"], 1)
                pe.wait_ge(q["cp_done"], L + 1)
                cT_ = bank[5][:, :].bitcast(bf16)
                for t in range(NT):
                    last = nc.tensor.transpose(cT_[0:PIECES * E1, t * P:(t + 1) * P],
                                               cpb[:, t, :, :].rearrange("p a e -> p (a e)"), identb[:])
                last.then_inc(q["cpT_p"], 1)
                pe.wait_ge(q["cbT_done"], L + 1)
                pe.wait_ge(q["hts_done"], 4 * (L + 2))
                pe.wait_ge(q["zb_done"], L + 1)
                pe.wait_ge(q["sel_done"], L + 1)

                def rows_in(f, b, first):
                    n = (FT[0] * B if L else 0) + nf * b + f
                    if not (type(f) is int and f == 0):
                        pe.wait_ge(q["fa_done"], n)
                    pe.wait_ge(q["fw_done"], (FT[0] if L else 0) + f + 1)
                    for m in range(w13n):
                        split_product(bank[m][:, :],
                                      lambda a, kt: w13s[:, a, bass.ds(f, 1), (m * KT + kt) * P:(m * KT + kt + 1) * P].squeeze(1),
                                      lambda a, kt: hTs[:, a, kt, b * S:(b + 1) * S])
                    nc.tensor.matmul(bank[2][:, :], sel[:, bass.ds((FT[0] * P if L else 0) + f * P, P)],
                                     cbT[:, b * S:(b + 1) * S], start=True, stop=True).then_inc(q["fu"], 1)

                def rows_out(f, b, buf):
                    n = (FT[0] * B if L else 0) + nf * b + f
                    pe.wait_ge(q["fh_done"], n + 1)
                    for t in range(TB):
                        last = nc.tensor.matmul(bank[6 + t // 2][:, (t % 2) * D:(t % 2 + 1) * D],
                                                hf[:, buf, t * P:(t + 1) * P], w2[:, bass.ds(f, 1), :].squeeze(1),
                                                start=False, stop=False, skip_group_check=True)
                    last.then_inc(q["fout"], 1)

                pe.wait_ge(q["d_w2"], 16 * (L + 1))
                for b in range(B):
                    if b:
                        pe.wait_ge(q["xf_done"], L * B + b)
                        pe.wait_ge(q["fa_done"], (FT[0] * B if L else 0) + nf * b)
                    for m in (6, 7):
                        nc.tensor.matmul(bank[m][:, :], zerob[:, 0:P], zerob[:, P:], start=True, stop=False,
                                         skip_group_check=True)
                    rows_in(0, b, True)
                    for m in range(2):
                        rows_in(m + 1, b, False)
                        rows_out(m, b, m)
                    with pe.Fori(1, (nf - 1) // 2) as i:
                        for m in range(2):
                            rows_in(2 * i + m + 1, b, False)
                            rows_out(2 * i + m, b, m)
                    rows_out(nf - 1, b, 0)

            pe.wait_ge(q["x1_done"], 1)
            experts(0)
            if stop == 1:
                return

            def heads():
                transposed_rows(2)
                pe.wait_ge(q["hT_done"], 12)
                pe.wait_ge(q["d_attn"], 48)
                for b in range(B):
                    hb = slice(b * S, (b + 1) * S)
                    if b:
                        pe.wait_ge(q["a_qkc"], b)
                    for m in range(2):
                        for kt in range(KT):
                            last = nc.tensor.matmul(bank[m][:, :], wqk[:, m, kt, :], hT[:, kt, hb],
                                                    start=kt == 0, stop=kt == KT - 1)
                    last.then_inc(q["a_qk"], 1)
                for b in range(B):
                    pe.wait_ge(q["a_kd"], b + 1)
                    pe.wait_ge(q["a_code"], b + 1)
                    cT_ = bank[2][:, :].bitcast(bf16)
                    for t in range(TB):
                        last = nc.tensor.transpose(cT_[:, t * P:(t + 1) * P], code[:, 2, t * P:(t + 1) * P], identb[:])
                    last.then_inc(q["a_cT"], 1)
                    if b:
                        pe.wait_ge(q["a_pv"], 3 * b)
                    for m in range(2):
                        for t in range(TB):
                            last = nc.tensor.transpose(bank[3 + m][:, t * P:(t + 1) * P],
                                                       kd[:, m, t * P:(t + 1) * P], ident)
                        last.then_inc(q["a_kT"], 1)
                    for t in range(TB):
                        for kt in range(KT):
                            last = nc.tensor.matmul(bank[5 + t // 2][:, (t % 2) * D:(t % 2 + 1) * D],
                                                    hT[:, kt, (b * TB + t) * P:(b * TB + t + 1) * P], wv[:, kt, :],
                                                    start=kt == 0, stop=kt == KT - 1)
                    last.then_inc(q["a_v"], 1)

                    pe.wait_ge(q["a_oh"], b + 1)
                    pe.wait_ge(q["a_pv"], 3 * (b + 1))
                    pe.wait_ge(q["a_vp"], b + 1)

                    def gather(n):
                        c = NQ // 4 * b + n
                        if not (type(n) is int and c == 0):
                            pe.wait_ge(q["a_gat"], c)
                        for g4 in range(4):
                            for side in range(2):
                                o = (g4 * 2 + side) * 48
                                for t in range(TB):
                                    last = nc.tensor.matmul(
                                        bank[7][:, o:o + 48],
                                        OH[:, t, side, bass.ds(4 * n + g4, 1), :].squeeze(1),
                                        PV[:, t, :, bass.ds(16 * n + 4 * g4, 4), :],
                                        start=t == 0, stop=t == TB - 1)
                        last.then_inc(q["a_vw"], 1)

                    gather(0)
                    with pe.Fori(1, NQ // 4) as n:
                        gather(n)
                    pe.wait_ge(q["a_qp"], b + 1)
                    pe.wait_ge(q["a_gat"], NQ // 4 * (b + 1))
                    pe.wait_ge(q["a_cTc"], b + 1)
                    pe.wait_ge(q["a_qkc"], B)

                    def spread(i, n):
                        c = NQ * b + 4 * n + i
                        if not (type(c) is int and c < 2):
                            pe.wait_ge(q["a_arg"], c - 1)
                        for pc in range(PIECES):
                            last = nc.tensor.matmul(
                                bank[i % 2][:, :],
                                selQ[:, bass.ds(4 * n + i, 1), :, :].squeeze(1).rearrange("p k h -> p (k h)"),
                                qp[:, pc, b, :], start=pc == 0, stop=pc == PIECES - 1)
                        last.then_inc(q["a_Q"], 1)

                    def weigh(i, n):
                        c = NQ * b + 4 * n + i
                        if i == 0 and not (type(n) is int and NQ // 4 * b + n == 0):
                            pe.wait_ge(q["a_O5"], NQ // 4 * b + n)
                        pe.wait_ge(q["a_E"], c + 1)
                        for t in range(TB):
                            last = nc.tensor.matmul(bank[2][:, (i * TB + t) * 20:(i * TB + t + 1) * 20],
                                                    Ex[:, i, t * P:(t + 1) * P],
                                                    VW[:, bass.ds(4 * n + i, 1), :, :].squeeze(1).rearrange("p h c -> p (h c)"),
                                                    start=True, stop=True)
                        last.then_inc(q["a_PV"], 1)

                    for i in range(4):
                        spread(i, 0)
                        if i > 1:
                            weigh(i - 2, 0)
                    with pe.Fori(1, NQ // 4) as n:
                        for i in range(4):
                            spread(i, n)
                            weigh((i - 2) % 4, n if i > 1 else n - 1)
                    weigh(2, NQ // 4 - 1)
                    weigh(3, NQ // 4 - 1)
                    for t in range(TB):
                        last = nc.tensor.transpose(bank[3][:, t * P:(t + 1) * P], qs[:, b, t * P:(t + 1) * P], ident)
                    last.then_inc(q["a_qT"], 1)
                    pe.wait_ge(q["a_att"], b + 1)
                    for kt in range(KT):
                        for t in range(TB):
                            last = nc.tensor.transpose(bank[4 + kt][:, t * P:(t + 1) * P],
                                                       attf[:, t, kt * P:(kt + 1) * P], ident)
                    last.then_inc(q["a_attT"], 1)
                    pe.wait_ge(q["a_attc"], b + 1)
                    for t in range(TB):
                        for kt in range(KT):
                            last = nc.tensor.matmul(bank[(6, 3)[t // 2]][:, (t % 2) * D:(t % 2 + 1) * D],
                                                    attT[:, kt, t * P:(t + 1) * P], wo[:, kt, :],
                                                    start=kt == 0, stop=kt == KT - 1)
                    last.then_inc(q["a_out"], 1)

            heads()
            if stop == 2:
                return
            pe.wait_ge(q["a_x"], B)
            experts(1)

        @block.scalar
        def _(act):
            act.wait_ge(q["d_c"], 16)
            nc.scalar.activation(sc[:], cT[:], ACT.Tanh, scale=0.5).then_inc(q["thc_done"], 1)

            def modulate(n, L):
                act.wait_ge(q["mods_done"], L + 1)
                for b in range(B):
                    for ft in range(KT):
                        act.wait_ge(q["tr_done"], 4 * n + b * KT + ft + 1)
                        nc.scalar.activation(hT[:, ft, b * S:(b + 1) * S], bank[b * KT + ft][:, :], ACT.Identity,
                                             bias=mods[:, L, 2 * (n % 2), ft, b:b + 1],
                                             scale=mods[:, L, 2 * (n % 2) + 1, ft, b:b + 1]).then_inc(q["hT_done"], 1)

            modulate(0, 0)
            act.wait_ge(q["d_wbc"], 16)
            nc.scalar.activation(wbs[:, 0], wbf, ACT.Copy).then_inc(q["wbs_hi"], 1)
            act.wait_ge(q["dtz_done"], 2)
            nc.scalar.activation(dtmp[:, 1], dtmp[:, 1], ACT.Exp).then_inc(q["act_seq"], 1)
            act.wait_ge(q["act_seq"], 1)
            nc.scalar.activation(dtmp[:, 1], dtmp[:, 1], ACT.Ln, bias=1.0).then_inc(q["act_seq"], 1)
            nc.scalar.activation(small[:, H:2 * H], small[:, H:2 * H], ACT.Exp).then_inc(q["act_seq"], 1)
            act.wait_ge(q["dex_done"], 1)
            nc.scalar.activation(dec[:], dec[:], ACT.Exp).then_inc(q["e_dt"], 1)
            nc.scalar.activation(etot[:], etot[:], ACT.Exp).then_inc(q["e_dt"], 1)

            def group_rows(g, par, b):
                n = G * b + g
                if not (type(n) is int and n < 2):
                    act.wait_ge(q["c_step"], 6 * n - 6)
                    act.wait_ge(q["c_bc"], 2 * n - 2)
                act.wait_ge(q["c_proj"], n + 1)
                for m in range(2):
                    w = lambda tap: bcp[:, bass.ds(g, 1), m, tap:tap + 1].squeeze(1)
                    nc.scalar.activation(rawg[:, 2 * par + m, 3:], bank[m][:, :], ACT.Copy)
                    last = nc.scalar.activation(gs[:, 2 * par + m, :], bank[m][:, :], ACT.Identity, scale=w(3),
                                                bias=w(4))
                last.then_inc(q["c_raw"], 1)

            def group_tanh(g, par, b):
                n = G * b + g
                for m, th in enumerate((thx, thg)):
                    if not (type(n) is int and n == 0):
                        act.wait_ge(q["c_bc"], 2 * n - 1 + m)
                    act.wait_ge(q["c_step"], 6 * n + 5 + m)
                    nc.scalar.activation(th[:], gs[:, 2 * par + m, :], ACT.Tanh).then_inc(q["c_th"], 1)

            def group_evac(g, b):
                act.wait_ge(q["c_mm"], G * b + g + 1)
                nc.scalar.activation(CB[:, bass.ds(g, 1), :, :].squeeze(1).rearrange("p t n -> p (t n)"),
                                     bank[2][:, :], ACT.Copy)
                nc.scalar.activation(Btok[:, bass.ds(g, 1), :, :].squeeze(1).rearrange("p t n -> p (t n)"),
                                     bank[3][:, :], ACT.Copy).then_inc(q["c_evac"], 1)

            def scan_slot(i, it, b):
                head = stages(i, it)
                h0, h1, h2 = head(0), head(1), head(2)
                n0, n1, n2 = (H * b + 8 * h[1] + h[0] if h else None for h in (h0, h1, h2))

                def since(name, n):
                    if type(n) is not int or n > 0:
                        act.wait_ge(q[name], n)

                if h1:
                    j = h1[0]
                    since("gs_done", n1)
                    act.wait_ge(q["pg"], n1 + 1)
                    nc.scalar.activation(thg[:], bank[1][:, :], ACT.Tanh, scale=0.5).then_inc(q["thg_done"], 1)
                if h0:
                    hcol = 8 * h0[1] + h0[0]
                    since("cv_step", 3 * n0 - 3)
                    since("xT_done", n0 - 1)
                    act.wait_ge(q["px"], n0 + 1)
                    nc.scalar.activation(raw[:, i % 2, 3:], bank[0][:, :], ACT.Copy)
                    nc.scalar.activation(u[:, i % 2, :], bank[0][:, :], ACT.Identity,
                                         scale=chn[:, bass.ds(hcol, 1), 3:4].squeeze(1),
                                         bias=chn[:, bass.ds(hcol, 1), 4:5].squeeze(1)).then_inc(q["raw_done"], 1)
                if h1:
                    hcol = 8 * h1[1] + h1[0]
                    since("py", n1 - 1)
                    since("xw_done", n1 - 1)
                    act.wait_ge(q["tr_x"], n1 + 1)
                    for t in range(TB):
                        last = nc.scalar.activation(Xdt[:, j % 2, t * P:(t + 1) * P], bank[2][:, t * P:(t + 1) * P],
                                                    ACT.Copy, scale=dtv[:, b * TB + t, bass.ds(hcol, 1)])
                    last.then_inc(q["xdt_done"], 1)
                if h0:
                    j = h0[0]
                    since("ce_done", n0 - 1)
                    act.wait_ge(q["pc"], n0 + 1)
                    nc.scalar.activation(Em[:, j % 2, :], bank[3][:, P:S], ACT.Exp).then_inc(q["e_done"], 1)
                    since("pg", n0)
                    since("wsplit", n0)
                    act.wait_ge(d_wA[(i + 1) % 2], 16 * (H // 2 * b + 4 * it + (i + 1) // 2 + 1))
                    nc.scalar.activation(whl[:, (i + 1) % 2, 0, :], wA[:, (i + 1) % 2, :], ACT.Copy)\
                        .then_inc(q["whi_done"], 1)
                    since("M_done", n0 - 1)
                    act.wait_ge(q["pc2"], n0 + 1)
                    nc.scalar.activation(Lm[:, j % 2, :], bank[3][:, :], ACT.Exp).then_inc(q["L_done"], 1)
                if h2:
                    j = h2[0]
                    jj = NG * b + 2 * h2[1] + j // 4
                    if j % HG == 0:
                        since("ssq_done", jj - 1)
                    elif j % HG > 1 or type(jj) is not int or jj > 0:
                        act.wait_ge(q["sq_add"], 3 * jj + j % HG - 1)
                    act.wait_ge(q["yb_done"], n2 + 1)
                    nc.scalar.activation(ysq[:] if j % HG else sqa[:, j // HG, :], yb[:, j, :], ACT.Square)\
                        .then_inc(q["ysq_done"], 1)
                if h0:
                    since("xT_done", n0)
                    act.wait_ge(q["cv_step"], 3 * n0 + 3)
                    nc.scalar.activation(thx[:], u[:, i % 2, :], ACT.Tanh, scale=0.5).then_inc(q["thx_done"], 1)

            act.wait_ge(d_wA[0], 16)
            nc.scalar.activation(whl[:, 0, 0, :], wA[:, 0, :], ACT.Copy).then_inc(q["whi_done"], 1)
            act.wait_ge(q["bcp_done"], 1)
            act.wait_ge(q["d_chn"], 16)
            for b in range(B):
                if b:
                    act.wait_ge(q["oa_done"], TB * NG * b)
                group_rows(0, 0, b)
                group_rows(1, 1, b)
                group_tanh(0, 0, b)
                with act.Fori(1, G // 2) as g2:
                    for m in range(2):
                        g = 2 * g2 - 1 + m
                        group_rows(g + 1, m, b)
                        group_tanh(g, 1 - m, b)
                        group_evac(g - 1, b)
                group_tanh(G - 1, 1, b)
                group_evac(G - 2, b)
                group_evac(G - 1, b)
                act.wait_ge(q["c_bc"], 2 * G * (b + 1))
                slots(act, b, scan_slot)
            if stop == 0:
                return

            def experts(L):
                n0, nf = 2 * L + 1, FT[L]
                w = 512 if L == 0 else 256
                base = FT[0] * B if L else 0
                modulate(n0, L)
                act.wait_ge(q["d_w13"], 16 * (L + 1))
                if L:
                    act.wait_ge(q["a_x"], B)
                for f in range(nf):
                    nc.scalar.activation(w13s[:, 0, f, 0:w], w13[:, f, 0:w], ACT.Copy).then_inc(q["fw_hi"], 1)
                if L == 0:
                    act.wait_ge(q["rt_p"], 1)
                    nc.scalar.activation(pr[:].rearrange("p t e -> p (t e)"), bank[4][:, 0:NT * E], ACT.Tanh,
                                         scale=0.5).then_inc(q["rt_act"], 1)
                else:
                    act.wait_ge(q["rt_dve"], 1)
                    nc.scalar.activation(pr[:], pr[:], ACT.Exp).then_inc(q["rt_act"], 1)

                def hidden(f, b, buf):
                    n = base + nf * b + f
                    def since(name, m):
                        if type(m) is not int or m > 0:
                            act.wait_ge(q[name], m)
                    if L == 0:
                        since("fh_done", n - 1)
                        act.wait_ge(q["fu"], n + 1)
                        nc.scalar.activation(sS[:, buf, :], bank[2][:, :], ACT.Copy).then_inc(q["fs_c"], 1)
                        act.wait_ge(q["fa_done"], n + 1)
                        nc.scalar.activation(fth[:, buf, :], ua[:, buf, :], ACT.Tanh, scale=0.5)\
                            .then_inc(q["fth_done"], 1)
                    else:
                        since("fh_done", n - 1)
                        act.wait_ge(q["fu"], n + 1)
                        nc.scalar.activation(fth[:, buf, :], bank[0][:, :], ACT.Tanh, scale=0.5)\
                            .then_inc(q["fth_done"], 1)

                for b in range(B):
                    for m in range(2):
                        hidden(m, b, m)
                    with act.Fori(1, (nf - 1) // 2) as i:
                        for m in range(2):
                            hidden(2 * i + m, b, m)
                    hidden(nf - 1, b, 0)

            experts(0)
            if stop == 1:
                return

            def heads():
                modulate(2, 1)
                for b in range(B):
                    act.wait_ge(q["a_qk"], b + 1)
                    nc.scalar.activation(qs[:, b, :], bank[0][:, :], ACT.Copy)
                    nc.scalar.activation(ks[:, b, :], bank[1][:, :], ACT.Copy).then_inc(q["a_qkc"], 1)
                for b in range(B):
                    def part(i, n):
                        c = NQ * b + 4 * n + i
                        if not (type(c) is int and c < 2):
                            act.wait_ge(q["a_arg"], c - 1)
                        act.wait_ge(q["a_Q"], c + 1)
                        nc.scalar.activation(tb_[:, i % 2, :], bank[i % 2][:, :], ACT.Identity,
                                             scale=scl[:, bass.ds(4 * n + i, 1), 1:2].squeeze(1)).then_inc(q["a_tb"], 1)

                    def grow(i, n):
                        c = NQ * b + 4 * n + i
                        if not (type(c) is int and c < 4):
                            act.wait_ge(q["a_PV"], c - 3)
                        act.wait_ge(q["a_arg"], c + 1)
                        nc.scalar.activation(Ex[:, i, :], arg[:, i % 2, :], ACT.Exp).then_inc(q["a_E"], 1)

                    act.wait_ge(q["a_gat"], NQ // 4 * (b + 1))
                    for i in range(4):
                        part(i, 0)
                        if i:
                            grow(i - 1, 0)
                    with act.Fori(1, NQ // 4) as n:
                        for i in range(4):
                            part(i, n)
                            grow((i - 1) % 4, n if i else n - 1)
                    grow(3, NQ // 4 - 1)
                    act.wait_ge(q["a_attT"], b + 1)
                    for kt in range(KT):
                        last = nc.scalar.activation(attT[:, kt, :], bank[4 + kt][:, :], ACT.Copy)
                    last.then_inc(q["a_attc"], 1)

            heads()
            if stop == 2:
                return
            experts(1)

        @block.vector
        def _(dve):
            count = [0]

            def link(ins):
                count[0] += 1
                ins.then_inc(q["dve_seq"], 1)
                dve.wait_ge(q["dve_seq"], count[0])

            link(nc.vector.memset(raw[:, :, 0:3], 0.0))
            dve.wait_ge(q["thc_done"], 1)
            link(nc.vector.scalar_tensor_tensor(out=sc[:], in0=sc[:], scalar=1.0, in1=cT[:], op0=ALU.add, op1=ALU.mult))
            nc.vector.tensor_scalar(sc[:], sc[:], 0.5, None, ALU.mult).then_inc(q["sc_done"], 1)
            dve.wait_ge(q["sc_done"], 1)
            nc.vector.tensor_copy(scb, sc[:].unsqueeze(2).to_broadcast([P, 2 * KT * B, P])).then_inc(q["scb_done"], 1)
            dve.wait_ge(q["d_cst"], 16)
            nc.vector.tensor_copy(identb[:], ident).then_inc(q["idb_done"], 1)
            nc.vector.tensor_copy(identb96[:, 0, :], cst[0:PIECES * H, C_STACK:C_STACK + H])
            nc.vector.tensor_scalar(identb96[:, 1, :], cst[0:PIECES * H, C_STACK:C_STACK + H], -1.0, None, ALU.mult)
            nc.vector.tensor_scalar(maskb[:], tri, 1.0, -MASKED, ALU.subtract, ALU.mult).then_inc(q["idb_done"], 1)
            def normalise(n):
                for t in range(NT):
                    last = nc.vector.bn_stats(stats[:, t, :], x_sb[:, t, :])
                link(last)
                for t in range(NT):
                    last = nc.vector.bn_aggr(mv[:, t, :], stats[:, t, :])
                link(last)
                link(nc.vector.tensor_scalar(nwt[:, 2, :], mv[:, :, 1], LN_EPS, None, ALU.add))
                rsqrt_steps(dve, rstd[:], nwt[:, 2, :], (nwt[:, 0, :], nwt[:, 1, :]), q["dve_seq"], count[0])
                count[0] += NWT
                for b in range(B):
                    for t in range(b * TB, (b + 1) * TB):
                        last = nc.vector.tensor_scalar(acc[:, t, :], x_sb[:, t, :], mv[:, t, 0:1], rstd[:, t:t + 1],
                                                       ALU.subtract, ALU.mult)
                    last.then_inc(q["xh_done"], 1)

            def split_rows(n):
                for b in range(B):
                    for ft in range(KT):
                        dve.wait_ge(q["hT_done"], 4 * n + b * KT + ft + 1)
                        part = slice(b * S, (b + 1) * S)
                        link(nc.vector.tensor_copy(hTs[:, 0, ft, part], hT[:, ft, part]))
                        nc.vector.tensor_tensor(hTs[:, 1, ft, part], hT[:, ft, part], hTs[:, 0, ft, part],
                                                ALU.subtract).then_inc(q["hts_done"], 1)

            def take_modulation(L):
                dve.wait_ge(q["modp_done"], L + 1)
                link(nc.vector.tensor_copy(mods[:, L].rearrange("p b c d -> p (b c d)"), bank[4 - L][:, 0:16]))
                for m in (1, 3):
                    last = nc.vector.tensor_scalar(mods[:, L, m], mods[:, L, m], 1.0, None, ALU.add)
                last.then_inc(q["mods_done"], 1)

            dve.wait_ge(q["d_x"], 16)
            normalise(0)
            take_modulation(0)
            split_rows(0)
            dve.wait_ge(q["tr_done"], 4)
            link(nc.vector.memset(acc[:], 0.0))

            dve.wait_ge(q["dtp_done"], 1)
            dve.wait_ge(q["d_small"], 64)
            z, az, adt = dtmp[:, 0], dtmp[:, 1], dtmp[:, 2]
            nc.vector.tensor_tensor(z, bank[4][:, 0:NT * H].rearrange("p (t h) -> p t h", t=NT),
                                    small[:, 0:H].unsqueeze(1).to_broadcast([P, NT, H]), ALU.add)\
                .then_inc(q["dtz_done"], 1)
            dve.wait_ge(q["dtz_done"], 1)
            nc.vector.scalar_tensor_tensor(out=az, in0=z, scalar=-1.0, in1=z, op0=ALU.mult, op1=ALU.min).then_inc(q["dtz_done"], 1)
            dve.wait_ge(q["act_seq"], 3)
            link(nc.vector.scalar_tensor_tensor(out=dtv[:], in0=z, scalar=0.0, in1=az, op0=ALU.max, op1=ALU.add))
            link(nc.vector.tensor_scalar(dtv[:], dtv[:], 0.0, None, ALU.max))
            nc.vector.scalar_tensor_tensor(out=adt, in0=dtv[:], scalar=-1.0,
                                           in1=small[:, H:2 * H].unsqueeze(1).to_broadcast([P, NT, H]),
                                           op0=ALU.mult, op1=ALU.mult).then_inc(q["dta_done"], 1)
            dve.wait_ge(q["dcs_done"], 1)
            fl = "p t h -> p (t h)"
            link(nc.vector.tensor_copy(cs[:].rearrange(fl), bank[5][:, 0:NT * H]))
            nc.vector.tensor_copy(etot[:].rearrange(fl), bank[6][:, 0:NT * H])
            link(nc.vector.tensor_tensor(dec[:].rearrange(fl), bank[6][:, 0:NT * H], cs[:].rearrange(fl), ALU.subtract))
            link(nc.vector.tensor_copy(csp[:, :, 0, :], cs[:]))
            dve.wait_ge(q["dve_seq"], count[0])
            nc.vector.tensor_tensor(dtmp[:, 0], cs[:], csp[:, :, 0, :], ALU.subtract).then_inc(q["dex_done"], 1)
            dve.wait_ge(q["dex_done"], 1)
            link(nc.vector.tensor_copy(csp[:, :, 1, :], dtmp[:, 0]))
            nc.vector.tensor_tensor(csp[:, :, 2, :], dtmp[:, 0], csp[:, :, 1, :], ALU.subtract).then_inc(q["csp_done"], 1)
            dve.wait_ge(q["cspT_done"], 1)
            nc.vector.tensor_copy(csT[:], bank[7][:, :].bitcast(bf16)[0:PIECES * H, :]).then_inc(q["csT_done"], 1)

            def take_gates():
                dve.wait_ge(q["gmod_done"], 1)
                for o in range(4):
                    last = nc.vector.tensor_copy(gm[:, o // 2, o % 2].rearrange("p b d -> p (b d)"), bank[4 + o][:, :])
                last.then_inc(q["gm_done"], 4)
                dve.wait_ge(q["gm_done"], 4)
                gv = gm[:].rearrange("p a b c d -> p (a b c d)")
                sg = yv_sign[:]
                link(nc.vector.tensor_scalar(sg, gv, 0.0, 2.0, ALU.is_ge, ALU.mult))
                link(nc.vector.scalar_tensor_tensor(out=gv, in0=gv, scalar=-1.0, in1=gv, op0=ALU.mult, op1=ALU.max))
                link(nc.vector.tensor_scalar(gv, gv, 0.25, None, ALU.max))
                link(nc.vector.scalar_tensor_tensor(out=gv, in0=sg, scalar=-1.0, in1=gv, op0=ALU.add, op1=ALU.mult))

            def group(g, par, b):
                n = G * b + g
                dve.wait_ge(q["c_raw"], n + 1)
                w = lambda m, tap: bcp[:, bass.ds(g, 1), m, tap:tap + 1].squeeze(1)
                for d in (1, 2, 3):
                    for m in range(2):
                        if d > 1:
                            dve.wait_ge(q["c_step"], 6 * n + 2 * (d - 2) + m + 1)
                        o = gs[:, 2 * par + m, :]
                        nc.vector.scalar_tensor_tensor(out=o, in0=rawg[:, 2 * par + m, 3 - d:3 - d + S],
                                                       scalar=w(m, 3 - d), in1=o, op0=ALU.mult, op1=ALU.add)\
                            .then_inc(q["c_step"], 1)
                if not (type(g) is int and n == 0):
                    dve.wait_ge(q["c_mm"], n)
                dve.wait_ge(q["c_step"], 6 * n + 6)
                dve.wait_ge(q["c_th"], 2 * n + 1)
                nc.vector.scalar_tensor_tensor(out=BT[:], in0=thx[:], scalar=1.0, in1=gs[:, 2 * par, :],
                                               op0=ALU.add, op1=ALU.mult).then_inc(q["c_bc"], 1)
                dve.wait_ge(q["c_th"], 2 * n + 2)
                nc.vector.scalar_tensor_tensor(out=CT[:, bass.ds(g, 1), :].squeeze(1), in0=thg[:], scalar=1.0,
                                               in1=gs[:, 2 * par + 1, :], op0=ALU.add, op1=ALU.mult)\
                    .then_inc(q["c_bc"], 1)

            def scan_slot(i, it, b):
                head = stages(i, it)
                h0, h1, h2 = head(0), head(1), head(2)
                n0, n1, n2 = (H * b + 8 * h[1] + h[0] if h else None for h in (h0, h1, h2))

                def since(name, n):
                    if type(n) is not int or n > 0:
                        dve.wait_ge(q[name], n)

                late, early = out_event(i, it, 6), out_event(i, it, 7)

                def rms_link(k):
                    e = late if k < 2 else early
                    if e and e[0] == 0:
                        root_step(k, NG * b + e[2])

                if h1:
                    j = h1[0]
                    since("py", n1 - 1)
                    dve.wait_ge(q["L_done"], n1 + 1)
                    nc.vector.tensor_tensor(Mm[:, j % 2, :], CB[:, j, :, :].rearrange("p t n -> p (t n)"),
                                            Lm[:, j % 2, :], ALU.mult).then_inc(q["M_done"], 1)
                rms_link(2)
                if h1:
                    since("yb_done", n1 - 3)
                    dve.wait_ge(q["thg_done"], n1 + 1)
                    nc.vector.scalar_tensor_tensor(out=gs[:, j % 4, :], in0=thg[:], scalar=1.0, in1=bank[1][:, :],
                                                   op0=ALU.add, op1=ALU.mult).then_inc(q["gs_done"], 1)
                rms_link(3)
                def tap(d):
                    if h0:
                        hcol = 8 * h0[1] + h0[0]
                        dve.wait_ge(q["cv_step"], 3 * n0 + d - 1) if d > 1 else dve.wait_ge(q["raw_done"], n0 + 1)
                        nc.vector.scalar_tensor_tensor(out=u[:, i % 2, :], in0=raw[:, i % 2, 3 - d:3 - d + S],
                                                       scalar=chn[:, bass.ds(hcol, 1), 3 - d:4 - d].squeeze(1),
                                                       in1=u[:, i % 2, :],
                                                       op0=ALU.mult, op1=ALU.add).then_inc(q["cv_step"], 1)
                    rms_link(3 + d)

                def state(c):
                    if h1:
                        j = h1[0]
                        hcol = 8 * h1[1] + h1[0]
                        s_of = lambda c: St[:, j % 2, c * P:(c + 1) * P]
                        if c == 0:
                            since("py", n1 - 1)
                            dve.wait_ge(q["ps"], n1 + 1)
                            nc.vector.tensor_copy(s_of(0), bank[4][:, 0:P]).then_inc(q["rc_step"], 1)
                        else:
                            dve.wait_ge(q["rc_step"], 3 * n1 + c)
                            nc.vector.scalar_tensor_tensor(out=s_of(c), in0=s_of(c - 1),
                                                           scalar=etot[:, b * TB + c, bass.ds(hcol, 1)],
                                                           in1=bank[4][:, c * P:(c + 1) * P],
                                                           op0=ALU.mult, op1=ALU.add).then_inc(q["rc_step"], 1)
                    rms_link(8 + c)

                tap(1)
                if h2:
                    j = h2[0]
                    hcol = 8 * h2[1] + h2[0]
                    since("yb_done", n2 - 1)
                    dve.wait_ge(q["xT_done"], n2 + 1)
                    dve.wait_ge(q["py"], n2 + 1)
                    nc.vector.scalar_tensor_tensor(out=yv[:, j % 2, :], in0=xT[:, j % 4, :],
                                                   scalar=chn[:, bass.ds(hcol, 1), 5:6].squeeze(1), in1=bank[5][:, :],
                                                   op0=ALU.mult, op1=ALU.add).then_inc(q["yc_done"], 1)
                tap(2)
                tap(3)
                rms_link(7)
                state(0)
                state(1)
                if early and early[0]:
                    add_tile(early, b)
                state(2)
                rms_link(11)
                rms_link(0)
                if h0:
                    since("yc_done", n0 - 3)
                    dve.wait_ge(q["thx_done"], n0 + 1)
                    dve.wait_ge(q["cv_step"], 3 * n0 + 3)
                    nc.vector.scalar_tensor_tensor(out=xT[:, i % 4, :], in0=thx[:], scalar=1.0, in1=u[:, i % 2, :],
                                                   op0=ALU.add, op1=ALU.mult).then_inc(q["xT_done"], 1)
                rms_link(1)
                if early and not early[0]:
                    add_tile(early, b)

            def add_tile(event, b):
                t, j, gi = event
                jj = NG * b + gi
                if t == 0:
                    dve.wait_ge(q["rg_step"], ROOT * (jj + 1))
                if type(jj) is not int or TB * jj + t > 0:
                    dve.wait_ge(q["oa_done"], TB * jj + t)
                dve.wait_ge(q["out_done"], TB * jj + t + 1)
                nc.vector.scalar_tensor_tensor(out=acc[:, b * TB + t, :], in0=bank[6 + t % 2][:, 0:D],
                                               scalar=rg[:, t:t + 1], in1=acc[:, b * TB + t, :],
                                               op0=ALU.mult, op1=ALU.add).then_inc(q["oa_done"], 1)

            def root_step(k, jj):
                step, base = q["rg_step"], ROOT * jj
                if type(jj) is not int or jj > 0 or k:
                    dve.wait_ge(step, base + k)
                t0, t1 = nwt[:, 0, 0:TB], nwt[:, 1, 0:TB]
                if k == 0:
                    dve.wait_ge(q["ssq_done"], jj + 1)
                    ins = nc.vector.tensor_scalar(ssv[:], bank[4][:, S - P:S - P + TB], 1.0 / (HG * P), 16 * RMS_EPS,
                                                  ALU.mult, ALU.add)
                elif k == 1:
                    ins = nc.vector.tensor_scalar(t0.bitcast(i32), ssv[:].bitcast(i32), 1, None,
                                                  ALU.logical_shift_right)
                elif k == 2:
                    if type(jj) is not int or jj > 0:
                        dve.wait_ge(q["oa_done"], TB * jj)
                    ins = nc.vector.tensor_scalar(rg[:].bitcast(i32), t0.bitcast(i32), -1.0, float(0x5f3759df),
                                                  ALU.mult, ALU.add)
                elif k % 3 == 0:
                    ins = nc.vector.tensor_tensor(t0, rg[:], rg[:], ALU.mult)
                elif k % 3 == 1:
                    ins = nc.vector.scalar_tensor_tensor(out=t1, in0=t0, scalar=-0.5, in1=ssv[:], op0=ALU.mult,
                                                         op1=ALU.mult)
                else:
                    ins = nc.vector.scalar_tensor_tensor(out=rg[:], in0=t1, scalar=1.5, in1=rg[:], op0=ALU.add,
                                                         op1=ALU.mult)
                ins.then_inc(step, 1)

            dve.wait_ge(q["e_dt"], 2)
            for b in range(B):
                if b:
                    dve.wait_ge(q["oa_done"], TB * NG * b)
                    dve.wait_ge(q["yb_done"], H * b)
                else:
                    dve.wait_ge(q["bcp_done"], 1)
                nc.vector.memset(rawg[:, :, 0:3], 0.0).then_inc(q["pad_done"], 1)
                dve.wait_ge(q["pad_done"], b + 1)
                group(0, 0, b)
                if b == 0:
                    take_modulation(1)
                    take_gates()
                group(1, 1, b)
                with dve.Fori(1, G // 2) as g2:
                    for m in range(2):
                        group(2 * g2 + m, m, b)
                dve.wait_ge(q["c_evac"], G * (b + 1))
                slots(dve, b, scan_slot)
            dve.wait_ge(q["oa_done"], TB * NG * B)
            for b in range(B):
                part = slice(b * TB, (b + 1) * TB)
                link(nc.vector.tensor_tensor(acc[:, part, :], acc[:, part, :],
                                             gm[:, 0, 0, b, :].unsqueeze(1).to_broadcast([P, TB, D]), ALU.mult))
            nc.vector.tensor_tensor(x_sb[:], x_sb[:], acc[:], ALU.add).then_inc(q["x1_done"], 1)
            dve.wait_ge(q["x1_done"], 1)
            if stop == 0:
                return

            def experts(L):
                n0, nf = 2 * L + 1, FT[L]
                base = FT[0] * B if L else 0
                dve.wait_ge(q["d_sel"], 16 * (L + 1))
                nc.vector.tensor_copy(sel[:], selw).then_inc(q["sel_done"], 1)
                nc.vector.memset(zerob[:], 0.0).then_inc(q["zb_done"], 1)
                normalise(n0)
                if L == 0:
                    dve.wait_ge(q["rt_act"], 1)
                    link(nc.vector.tensor_scalar(pr[:], pr[:], 0.5, 0.5, ALU.mult, ALU.add))
                    link(nc.vector.tensor_tensor(prb[:], pr[:],
                                                 small[:, 2 * H:2 * H + E].unsqueeze(1).to_broadcast([P, NT, E]), ALU.add))
                    crit = prb
                else:
                    dve.wait_ge(q["rt_p"], 2)
                    z = bank[4][:, 0:NT * E].rearrange("p (t e) -> p t e", t=NT)
                    link(nc.vector.tensor_reduce(r1[:], z, mybir.AxisListType.X, ALU.max))
                    nc.vector.tensor_tensor(pr[:], z, r1[:].unsqueeze(2).to_broadcast([P, NT, E]), ALU.subtract)\
                        .then_inc(q["rt_dve"], 1)
                    dve.wait_ge(q["rt_act"], 2)
                    link(nc.vector.tensor_reduce(r1[:], pr[:], mybir.AxisListType.X, ALU.add))
                    link(nc.vector.reciprocal(r1[:], r1[:]))
                    link(nc.vector.tensor_tensor(pr[:], pr[:], r1[:].unsqueeze(2).to_broadcast([P, NT, E]), ALU.mult))
                    crit = pr
                theirs = crit[:].unsqueeze(2).to_broadcast([P, NT, E, E])
                own = crit[:].unsqueeze(3).to_broadcast([P, NT, E, E])
                lower = cst[:, C_LOWER:C_LOWER + E * E].rearrange("p (a c) -> p a c", a=E).unsqueeze(1)\
                    .to_broadcast([P, NT, E, E])
                nc.vector.tensor_tensor(cmpa[:], theirs, own, ALU.is_gt)
                link(nc.vector.tensor_tensor(cmpb[:], theirs, own, ALU.is_equal))
                link(nc.vector.tensor_tensor(cmpb[:], cmpb[:], lower, ALU.mult))
                link(nc.vector.tensor_tensor(cmpa[:], cmpa[:], cmpb[:], ALU.add))
                link(nc.vector.tensor_reduce(rank[:], cmpa[:], mybir.AxisListType.X, ALU.add))
                nc.vector.memset(comb[:, :, E:E1], 1.0)
                link(nc.vector.scalar_tensor_tensor(out=comb[:, :, 0:E], in0=rank[:], scalar=2.0, in1=pr[:],
                                                    op0=ALU.is_lt, op1=ALU.mult))
                if L:
                    link(nc.vector.tensor_reduce(r1[:], comb[:, :, 0:E], mybir.AxisListType.X, ALU.add))
                    link(nc.vector.reciprocal(r1[:], r1[:]))
                    link(nc.vector.tensor_tensor(comb[:, :, 0:E], comb[:, :, 0:E],
                                                 r1[:].unsqueeze(2).to_broadcast([P, NT, E]), ALU.mult))
                link(nc.vector.tensor_copy(cpb[:, :, 0, :], comb[:]))
                link(nc.vector.tensor_tensor(cpt[:], comb[:], cpb[:, :, 0, :], ALU.subtract))
                link(nc.vector.tensor_copy(cpb[:, :, 1, :], cpt[:]))
                nc.vector.tensor_tensor(cpb[:, :, 2, :], cpt[:], cpb[:, :, 1, :], ALU.subtract).then_inc(q["cp_done"], 1)
                split_rows(n0)
                dve.wait_ge(q["cpT_p"], L + 1)
                nc.vector.tensor_copy(cbT[:], bank[5][:, :].bitcast(bf16)[0:PIECES * E1, :]).then_inc(q["cbT_done"], 1)

                def hidden(f, b, buf):
                    n = base + nf * b + f
                    def since(name, m):
                        if type(m) is not int or m > 0:
                            dve.wait_ge(q[name], m)
                    if L == 0:
                        dve.wait_ge(q["fs_c"], n + 1)
                        since("fh_done", n - 1)
                        nc.vector.tensor_tensor(ua[:, buf, :], bank[0][:, :], sS[:, buf, :], ALU.mult)
                        nc.vector.scalar_tensor_tensor(out=uc[:, buf, :], in0=bank[1][:, :], scalar=0.5,
                                                       in1=sS[:, buf, :], op0=ALU.mult, op1=ALU.mult)\
                            .then_inc(q["fa_done"], 1)
                        since("fh_done", n)
                        dve.wait_ge(q["fth_done"], n + 1)
                        dve.wait_ge(q["fa_done"], n + 1)
                        nc.vector.scalar_tensor_tensor(out=fg[:], in0=fth[:, buf, :], scalar=1.0, in1=ua[:, buf, :],
                                                       op0=ALU.add, op1=ALU.mult).then_inc(q["zero_done"], 1)
                        since("fout", n - 1)
                        dve.wait_ge(q["zero_done"], n + 1)
                        nc.vector.tensor_tensor(hf[:, buf, :], fg[:], uc[:, buf, :], ALU.mult)\
                            .then_inc(q["fh_done"], 1)
                    else:
                        since("fh_done", n)
                        dve.wait_ge(q["fth_done"], n + 1)
                        nc.vector.scalar_tensor_tensor(out=fg[:], in0=fth[:, buf, :], scalar=1.0, in1=bank[0][:, :],
                                                       op0=ALU.add, op1=ALU.mult).then_inc(q["zero_done"], 1)
                        since("fout", n - 1)
                        dve.wait_ge(q["zero_done"], n + 1)
                        nc.vector.scalar_tensor_tensor(out=hf[:, buf, :], in0=fg[:], scalar=0.5, in1=bank[2][:, :],
                                                       op0=ALU.mult, op1=ALU.mult).then_inc(q["fa_done"], 1)
                        dve.wait_ge(q["fa_done"], n + 1)
                        dve.sem_inc(q["fh_done"], 1)

                for b in range(B):
                    for m in range(2):
                        hidden(m, b, m)
                    with dve.Fori(1, (nf - 1) // 2) as i:
                        for m in range(2):
                            hidden(2 * i + m, b, m)
                    hidden(nf - 1, b, 0)
                    dve.wait_ge(q["fout"], base + nf * (b + 1))
                    for m in range(2):
                        last = nc.vector.tensor_tensor(xo[:, 2 * m:2 * m + 2, :],
                                                       bank[6 + m][:, :].rearrange("p (t d) -> p t d", t=2),
                                                       gm[:, L, 1, b, :].unsqueeze(1).to_broadcast([P, 2, D]), ALU.mult)
                    link(last)
                    part = slice(b * TB, (b + 1) * TB)
                    nc.vector.tensor_tensor(x_sb[:, part, :], x_sb[:, part, :], xo[:], ALU.add).then_inc(q["xf_done"], 1)
                    dve.wait_ge(q["xf_done"], L * B + b + 1)

            experts(0)
            if stop == 1:
                return

            def heads():
                normalise(2)
                nc.vector.tensor_copy(iotak[:].rearrange("p s k h -> p (s k) h"),
                                      cst[:, C_IOTA:C_IOTA + 2 * K].unsqueeze(2).to_broadcast([P, 2 * K, QG]))
                nc.vector.tensor_copy(selQ[:], identb[:].rearrange("p (g h) -> p g h", h=QG).unsqueeze(2)
                                      .to_broadcast([P, NQ, K, QG]))
                block4 = cst[:, C_BLOCK:C_BLOCK + QG]
                link(nc.vector.tensor_copy(VW[:, :, :, 4], block4.unsqueeze(1).to_broadcast([P, NQ, QG])))
                for b in range(B):
                    dve.wait_ge(q["a_qkc"], b + 1)
                    link(nc.vector.tensor_copy(qp[:, 0, b, :], qs[:, b, :]))
                    link(nc.vector.tensor_tensor(rk[:], qs[:, b, :], qp[:, 0, b, :], ALU.subtract))
                    link(nc.vector.tensor_copy(qp[:, 1, b, :], rk[:]))
                    link(nc.vector.tensor_tensor(qp[:, 2, b, :], rk[:], qp[:, 1, b, :], ALU.subtract))
                nc.vector.memset(m8[:], 0.0).then_inc(q["a_qp"], B)
                dve.wait_ge(q["a_qp"], B)
                for b in range(B):
                    for side in range(2):
                        if side == 0:
                            link(nc.vector.tensor_copy(wk[:, 0, ::-1], ks[:, b, :]))
                        else:
                            link(nc.vector.tensor_scalar(wk[:, 0, :], ks[:, b, :], -1.0, None, ALU.mult))
                        src = 0
                        for r in range(K // 8):
                            link(nc.vector.max(m8[:, r % 2, :], wk[:, src, :]))
                            if r == 0:
                                link(nc.vector.tensor_scalar(ext[:, b, side:side + 1], m8[:, 0, 0:1],
                                                             1.0 - 2.0 * side, None, ALU.mult))
                            dst = 1 + r % 2
                            link(nc.vector.match_replace(wk[:, dst, :], m8[:, r % 2, :], wk[:, src, :], NEG))
                            src = dst
                        link(nc.vector.tensor_scalar(hit[:, 0, :], wk[:, src, :], NEG, None, ALU.is_equal))
                        link(nc.vector.tensor_tensor_scan(rk[:], hit[:, 0, :], hit[:, 0, :], 0.0, ALU.add, ALU.max))
                        link(nc.vector.scalar_tensor_tensor(out=code[:, side, :], in0=rk[:], scalar=float(side * K),
                                                            in1=hit[:, 0, :], op0=ALU.add, op1=ALU.mult))
                        if side == 0 and b:
                            dve.wait_ge(q["a_kT"], 2 * b)
                        link(nc.vector.tensor_scalar(kd[:, side, :], ks[:, b, :], ext[:, b, side:side + 1], None,
                                                     ALU.subtract))
                    nc.vector.tensor_tensor(code[:, 2, :], code[:, 0, ::-1], code[:, 1, :], ALU.add)\
                        .then_inc(q["a_code"], 1)
                    dve.wait_ge(q["a_code"], b + 1)
                    dve.sem_inc(q["a_kd"], 1)

                    dve.wait_ge(q["a_cT"], b + 1)
                    nc.vector.tensor_copy(cdT[:].rearrange("p t h -> p (t h)"),
                                          bank[2][:, :].bitcast(bf16)[:, 0:TB * P]).then_inc(q["a_cTc"], 1)
                    dve.wait_ge(q["a_cTc"], b + 1)
                    for t in range(TB):
                        for side in range(2):
                            last = nc.vector.tensor_tensor(
                                OH[:, t, side].rearrange("p g (k h) -> p g k h", h=QG),
                                cdT[:, t, :].rearrange("p (g h) -> p g h", h=QG).unsqueeze(2).to_broadcast([P, NQ, K, QG]),
                                iotak[:, side].unsqueeze(1).to_broadcast([P, NQ, K, QG]), ALU.is_equal)
                    last.then_inc(q["a_oh"], 1)

                    def pieces(src, qq, cnt):
                        out = lambda pc: PV[:, :, pc, :, qq]
                        rr = pvr[:].rearrange("p (t h) -> p t h", t=TB)
                        link(nc.vector.tensor_copy(out(0), src))
                        link(nc.vector.tensor_tensor(rr, src, out(0), ALU.subtract))
                        link(nc.vector.tensor_copy(out(1), rr))
                        link(nc.vector.tensor_tensor(out(2), rr, out(1), ALU.subtract))

                    for m in range(2):
                        dve.wait_ge(q["a_kT"], 2 * b + m + 1)
                        pieces(bank[3 + m][:, :].rearrange("p (t h) -> p t h", t=TB), m, None)
                    nc.vector.memset(m8[:, 0, :], 0.0).then_inc(q["a_pv"], 3)
                    dve.wait_ge(q["a_pv"], 3 * (b + 1))
                    dve.wait_ge(q["a_v"], b + 1)
                    for j in range(2):
                        for half in range(2):
                            src = bank[5 + half][:, :].rearrange("p (t j h) -> p t j h", t=2, j=2)[:, :, j, :]
                            out = lambda pc: PV[:, 2 * half:2 * half + 2, pc, :, 2 + j]
                            rr = pvr[:, 0:2 * P].rearrange("p (t h) -> p t h", t=2)
                            link(nc.vector.tensor_copy(out(0), src))
                            link(nc.vector.tensor_tensor(rr, src, out(0), ALU.subtract))
                            link(nc.vector.tensor_copy(out(1), rr))
                            link(nc.vector.tensor_tensor(out(2), rr, out(1), ALU.subtract))
                    nc.vector.memset(m8[:, 1, :], 0.0).then_inc(q["a_vp"], 1)
                    dve.wait_ge(q["a_vp"], b + 1)

                    st = q["a_iota"]
                    with dve.Fori(0, NQ // 4) as n:
                        c = NQ // 4 * b + n
                        s0 = 6 * c
                        dve.wait_ge(q["a_vw"], c + 1)
                        nc.vector.tensor_reduce(gat[:], bank[7][:, 0:384].rearrange("p (a c x) -> p a x c", a=8, c=3),
                                                mybir.AxisListType.X, ALU.add).then_inc(q["a_gat"], 1)
                        dve.wait_ge(q["a_gat"], c + 1)
                        nc.vector.tensor_tensor(gam[:].rearrange("p a (h x) -> p a h x", h=QG),
                                                gat[:].rearrange("p a (h x) -> p a h x", h=QG),
                                                block4.unsqueeze(1).unsqueeze(3).to_broadcast([P, 8, QG, 4]),
                                                ALU.mult).then_inc(st, 1)
                        dve.wait_ge(st, 5 * c + 1)
                        for side in range(2):
                            gv_ = gam[:].rearrange("p (a s) (h x) -> p a s h x", s=2, h=QG)[:, :, side]
                            nc.vector.tensor_reduce(scl[:, bass.ds(4 * n, 4), side], gv_[:, :, :, side],
                                                    mybir.AxisListType.X, ALU.add).then_inc(st, 1)
                            nc.vector.tensor_copy(VW[:, bass.ds(4 * n, 4), :, 2 * side:2 * side + 2], gv_[:, :, :, 2:4])\
                                .then_inc(st, 1)
                        dve.wait_ge(st, 5 * c + 5)
                    dve.sem_inc(q["a_tbr"], 1)

                    def least(i, n):
                        c = NQ * b + 4 * n + i
                        if not (type(c) is int and c < 2):
                            dve.wait_ge(q["a_E"], c - 1)
                        dve.wait_ge(q["a_tb"], c + 1)
                        nc.vector.scalar_tensor_tensor(out=arg[:, i % 2, :], in0=bank[i % 2][:, :],
                                                       scalar=scl[:, bass.ds(4 * n + i, 1), 0:1].squeeze(1),
                                                       in1=tb_[:, i % 2, :], op0=ALU.mult, op1=ALU.min)\
                            .then_inc(q["a_arg"], 1)

                    def collect(n):
                        c = NQ // 4 * b + n
                        dve.wait_ge(q["a_PV"], NQ * b + 4 * n + 4)
                        nc.vector.tensor_copy(
                            O5[:, :, bass.ds(16 * n, 16), :].rearrange("p t (g h) c -> p g t (h c)", g=4),
                            bank[2][:, 0:320].rearrange("p (g t x) -> p g t x", g=4, t=TB)).then_inc(q["a_O5"], 1)

                    for i in range(4):
                        least(i, 0)
                    with dve.Fori(1, NQ // 4) as n:
                        for i in range(4):
                            least(i, n)
                            if i == 1:
                                collect(n - 1)
                    collect(NQ // 4 - 1)
                    dve.wait_ge(q["a_O5"], NQ // 4 * (b + 1))
                    dve.wait_ge(q["a_qT"], b + 1)
                    link(nc.vector.tensor_scalar(qm.rearrange("p t h -> p (t h)"), bank[3][:, :], 0.0, None, ALU.is_gt))
                    link(nc.vector.reciprocal(rden, O5[:, :, :, 4]))
                    for j in range(2):
                        link(nc.vector.copy_predicated(O5[:, :, :, 2 + j], qm.bitcast(mybir.dt.uint32), O5[:, :, :, j]))
                    if b:
                        dve.wait_ge(q["a_attT"], b)
                    for j in range(2):
                        last = nc.vector.tensor_tensor(att[:, :, :, j], O5[:, :, :, 2 + j], rden, ALU.mult)
                    last.then_inc(q["a_att"], 1)
                    dve.wait_ge(q["a_out"], b + 1)
                    dve.wait_ge(q["a_att"], b + 1)
                    xo1 = wk[:, 0:2, :].rearrange("p a (t d) -> p (a t) d", t=2)
                    for m in range(2):
                        last = nc.vector.tensor_tensor(xo1[:, 2 * m:2 * m + 2, :],
                                                       bank[(6, 3)[m]][:, :].rearrange("p (t d) -> p t d", t=2),
                                                       gm[:, 1, 0, b, :].unsqueeze(1).to_broadcast([P, 2, D]), ALU.mult)
                    link(last)
                    part = slice(b * TB, (b + 1) * TB)
                    nc.vector.tensor_tensor(x_sb[:, part, :], x_sb[:, part, :], xo1, ALU.add).then_inc(q["a_x"], 1)
                    dve.wait_ge(q["a_x"], b + 1)

            heads()
            if stop == 2:
                return
            experts(1)

        @block.gpsimd
        def _(pool):
            count = [0]

            def link(ins):
                count[0] += 1
                ins.then_inc(q["pool_seq"], 1)
                pool.wait_ge(q["pool_seq"], count[0])

            pool.wait_ge(q["d_small"], 64)
            nc.gpsimd.tensor_scalar(bcp[:], bcp[:], 0.5, None, ALU.mult).then_inc(q["bcp_done"], 1)
            pool.wait_ge(q["wbs_hi"], 1)
            nc.gpsimd.tensor_tensor(wbs[:, 1], wbf, wbs[:, 0], ALU.subtract).then_inc(q["wbs_done"], 1)
            pool.wait_ge(q["whi_done"], 1)
            nc.gpsimd.tensor_tensor(whl[:, 0, 1, :], wA[:, 0, :], whl[:, 0, 0, :], ALU.subtract)\
                .then_inc(q["wsplit"], 1)

            def scan_slot(i, it, b):
                head = stages(i, it)
                h0, h1, h2 = head(0), head(1), head(2)
                n0, n1, n2 = (H * b + 8 * h[1] + h[0] if h else None for h in (h0, h1, h2))

                def since(name, n):
                    if type(n) is not int or n > 0:
                        pool.wait_ge(q[name], n)

                if h1:
                    j = h1[0]
                    hcol = 8 * h1[1] + h1[0]
                    since("ps", n1 - 1)
                    pool.wait_ge(q["xdt_done"], n1 + 1)
                    nc.gpsimd.tensor_tensor(
                        Xw[:, j % 2, :].rearrange("p (t n) -> p t n", n=P),
                        Xdt[:, j % 2, 0:S - P].rearrange("p (t n) -> p t n", n=P),
                        dec[:, b * TB:b * TB + TB - 1, bass.ds(hcol, 1)].to_broadcast([P, TB - 1, P]),
                        ALU.mult).then_inc(q["xw_done"], 1)
                if h2:
                    j = h2[0]
                    jj = NG * b + 2 * h2[1] + j // 4
                    since("out_done", TB * (jj - 1))
                    pool.wait_ge(q["gs_done"], n2 + 1)
                    pool.wait_ge(q["yc_done"], n2 + 1)
                    nc.gpsimd.tensor_tensor(yb[:, j, :], yv[:, j % 2, :], gs[:, j % 4, :], ALU.mult)\
                        .then_inc(q["yb_done"], 1)
                if h0:
                    nx = (i + 1) % 2
                    pool.wait_ge(q["whi_done"], n0 + 2)
                    nc.gpsimd.tensor_tensor(whl[:, nx, 1, :], wA[:, nx, :], whl[:, nx, 0, :],
                                            ALU.subtract).then_inc(q["wsplit"], 1)
                    since("py", n0 - 1)
                    pool.wait_ge(q["e_done"], n0 + 1)
                    nc.gpsimd.tensor_tensor(CE[:, i % 2, :], CT[:, i, P:S], Em[:, i % 2, :], ALU.mult)\
                        .then_inc(q["ce_done"], 1)
                if h2:
                    hcol = 8 * h2[1] + j
                    pool.wait_ge(d_wB[j], 16 * (H // 8 * b + h2[1] + 1))
                    nc.gpsimd.tensor_tensor(wB[:, j, :], wB[:, j, :],
                                            chn[:, bass.ds(hcol, 1), 6:7].squeeze(1).to_broadcast([P, D]), ALU.mult)\
                        .then_inc(q["wo_done"], 1)
                    m = j % HG
                    if m:
                        if m > 1:
                            pool.wait_ge(q["sq_add"], 3 * jj + m - 1)
                        pool.wait_ge(q["ysq_done"], n2 + 1)
                        nc.gpsimd.tensor_tensor(sqa[:, j // 4, :], sqa[:, j // 4, :], ysq[:], ALU.add)\
                            .then_inc(q["sq_add"], 1)

            pool.wait_ge(q["d_chn"], 16)
            for b in range(B):
                pool.wait_ge(q["c_evac"], G * (b + 1))
                slots(pool, b, scan_slot)

            for L in range(2):
                if stop is not None and stop < 2 * L + 1:
                    return
                w = 512 if L == 0 else 256
                for f in range(FT[L]):
                    pool.wait_ge(q["fw_hi"], (FT[0] if L else 0) + f + 1)
                    nc.gpsimd.tensor_tensor(w13s[:, 1, f, 0:w], w13[:, f, 0:w], w13s[:, 0, f, 0:w], ALU.subtract)\
                        .then_inc(q["fw_done"], 1)


def out_event(i, it, back):
    j, n = i - back, it
    if j < 0:
        j, n = j + 8, it - 1
    if type(n) is int and not 0 <= n < H // 8:
        return None
    return j % TB, j // HG, 2 * n + j // HG


def kernel(**inputs):
    import numpy as np
    import concourse.bacc as bacc
    from concourse.bass_utils import run_bass_kernel_spmd

    def a(name):
        return np.asarray(inputs[name])

    f32 = np.float32
    I, GN = H * P, G * P
    rows = a("L0_attn_in_proj_w")

    def km(w):
        n, m, _ = w.shape
        return w.reshape(n, m, KT, P).transpose(3, 0, 2, 1)

    gate = km(rows[0:I].reshape(H, P, D))
    xs = km(rows[I:2 * I].reshape(H, P, D))
    win = np.stack([xs, gate], axis=2).transpose(1, 0, 2, 3, 4).reshape(H, P, 512)
    Bw = km(rows[2 * I:2 * I + GN].reshape(G, P, D))
    Cw = km(rows[2 * I + GN:2 * I + 2 * GN].reshape(G, P, D))
    wbc = np.stack([Bw, Cw], axis=2).reshape(P, G, 512)
    wdt = rows[2 * I + 2 * GN:].reshape(H, KT, P).transpose(2, 1, 0)
    cw, cb = a("L0_attn_conv_w")[:, 0, :], a("L0_attn_conv_b")
    chan = np.concatenate([cw, cb[:, None]], axis=1)
    wob = a("L0_attn_out_proj_w").T.reshape(H, P, D)
    chn = np.concatenate([
        chan[0:I].reshape(H, P, 5),
        np.broadcast_to(a("L0_attn_D")[:, None, None], (H, P, 1)),
        a("L0_attn_norm_w").reshape(H, P, 1),
        np.zeros((H, P, CH - 7), f32)], axis=2).transpose(1, 0, 2)
    bcp = np.stack([chan[I:I + GN].reshape(G, P, 5), chan[I + GN:].reshape(G, P, 5)], axis=2).transpose(1, 0, 2, 3)
    eye = np.eye(P, dtype=f32)
    stack = np.concatenate([np.tile(np.eye(H, dtype=f32), (PIECES, 1)), np.zeros((P - PIECES * H, H), f32)])
    k1 = np.arange(P)[:, None]
    lower = np.tril(np.ones((E, E), f32), -1).reshape(1, E * E)
    iota = np.arange(1, 2 * K + 1, dtype=f32)[None]
    consts = np.concatenate([
        eye, np.triu(np.ones((P, P), f32)), np.ones((P, P), f32), stack,
        np.broadcast_to(lower, (P, E * E)), (k1 % QG == np.arange(QG)).astype(f32),
        np.broadcast_to(iota, (P, 2 * K))], axis=1)
    expert = [np.arange(FT[0] * P) // P, np.minimum(np.arange(FT[1] * P) // HID1, E)]
    sel = np.concatenate([(e[None] == np.arange(E1)[:, None]).astype(f32) for e in expert], axis=1)
    w13_0 = np.stack([km(np.concatenate([a("L0_ffn_w1"), a("L0_ffn_sw1")[None]])),
                      km(np.concatenate([a("L0_ffn_w3"), a("L0_ffn_sw3")[None]]))], axis=2).reshape(P, E1, 512)
    w2_0 = np.concatenate([a("L0_ffn_w2"), a("L0_ffn_sw2")[None]]).transpose(2, 0, 1)
    pad = FT[1] * P - E1 * HID1
    in1 = np.concatenate([a("L1_ffn_w1"), a("L1_ffn_w_shared1")[None]]).transpose(1, 0, 2).reshape(D, E1 * HID1)
    in1 = np.concatenate([in1, np.zeros((D, pad), f32)], axis=1)
    w13_1 = in1.reshape(KT, P, FT[1], P).transpose(1, 2, 0, 3).reshape(P, FT[1], 256)
    out1 = np.concatenate([a("L1_ffn_w2"), a("L1_ffn_w_shared2")[None]]).reshape(E1 * HID1, D)
    w2_1 = np.concatenate([out1, np.zeros((pad, D), f32)]).reshape(FT[1], P, D).transpose(1, 0, 2)
    router = np.stack([a("L0_ffn_gate_w").T, a("L1_ffn_w_router")]).reshape(2, KT, P, E).transpose(2, 0, 1, 3)
    wqk = np.stack([a("L1_attn_Wq").T, a("L1_attn_Wk").T]).reshape(2, KT, P, P).transpose(2, 0, 1, 3)
    wv = a("L1_attn_Wv").reshape(P, 2, D).transpose(2, 1, 0).reshape(KT, P, D).transpose(1, 0, 2)
    wo = a("L1_attn_Wo").T.reshape(KT, P, D).transpose(1, 0, 2)
    feeds = {
        "sel": np.tile(sel, (PIECES, 1)), "w13_0": w13_0, "w2_0": w2_0, "w13_1": w13_1, "w2_1": w2_1,
        "router": router, "wqk": wqk, "wv": wv, "wo": wo,
        "x": a("L0_attn_x").reshape(T, D),
        "cst": consts,
        "cT": np.stack([a("L0_c"), a("L1_c")]).reshape(2, B, KT, P).transpose(3, 0, 2, 1).reshape(P, 2 * KT * B),
        "wmod": np.stack([a("L0_wmod"), a("L1_wmod")]).reshape(2, KT, P, 6 * D).transpose(0, 2, 1, 3),
        "small": np.concatenate([a("L0_attn_dt_bias"), a("L0_attn_A_log"), a("L0_ffn_expert_bias")]),
        "wdt": wdt, "bcp": bcp, "chn": chn, "wbc": wbc, "win": win, "wob": wob,
    }
    nc = bacc.Bacc("TRN2", target_bir_lowering=False, num_devices=1)
    feeds = {n: np.ascontiguousarray(v) for n, v in feeds.items()}
    io = {n: nc.dram_tensor(f"in_{n}", v.shape, mybir.dt.from_np(v.dtype), kind="ExternalInput").ap()
          for n, v in feeds.items()}
    io["out"] = nc.dram_tensor("out", (T, D), mybir.dt.float32, kind="ExternalOutput").ap()
    build_block(nc, io)
    r = run_bass_kernel_spmd(nc, [{f"in_{n}": v for n, v in feeds.items()}], core_ids=[0])
    return r.results[0]["out"].reshape(B, S, D)
```

```python
from contextlib import ExitStack

import concourse.bass as bass
from concourse import mybir

B, S, D = 2, 512, 256
T = B * S
P = 128
KT = D // P
NT = T // P
TB = S // P
H = 32
G = 8
NG = 8
HG = H // NG
LN_EPS = 1e-5
RMS_EPS = 1e-6
E = 8
E1 = E + 1
HID1 = 176
FT = (E1, -(-E1 * HID1 // P))
K = 32
QG = 4
NQ = P // QG
OC = 4 * QG * 5
NEG = -3.0e38
CST = 3 * P + H + E * E + QG + 2 * K
C_STACK = 3 * P
C_LOWER = C_STACK + H
C_BLOCK = C_LOWER + E * E
C_IOTA = C_BLOCK + QG
CH = 8
PIECES = 3


def build_block(nc, io):
    fp32, bf16, i32 = mybir.dt.float32, mybir.dt.bfloat16, mybir.dt.int32
    ALU = mybir.AluOpType
    ACT = mybir.ActivationFunctionType
    ctx = ExitStack()
    with ctx:
        def sb(name, shape, dt=fp32):
            return ctx.enter_context(nc.sbuf_tensor(name, shape, dt))

        def sem(name):
            return ctx.enter_context(nc.semaphore(name))

        bank = [ctx.enter_context(nc.psum_tensor(f"bank{n}", [P, 512], fp32)) for n in range(8)]

        x_sb = sb("x_sb", [P, NT, D])
        acc = sb("acc", [P, NT, D])
        xT = sb("xT", [P, 4, S])
        hT = xT[:, :, :].rearrange("p (k c) s -> p k (c s)", k=KT)
        hTs = sb("hTs", [P, 2, KT, T], bf16)
        cst = sb("cst", [P, CST])
        ident, tri, ones = cst[:, 0:P], cst[:, P:2 * P], cst[:, 2 * P:3 * P]
        identb = sb("identb", [P, P], bf16)
        identb96 = sb("identb96", [PIECES * H, 2, H], bf16)
        cT = sb("cT", [P, 2 * KT * B])
        sc = sb("sc", [P, 2 * KT * B])
        mods = sb("mods", [P, 2, 4, KT, B])
        gm = sb("gm", [P, 2, 2, B, D])
        small = sb("small", [P, 2 * H + E])
        wdt = sb("wdt", [P, KT, H])
        bcp = sb("bcp", [P, G, 2, 5])
        stats = sb("stats", [P, NT, 6])
        mv = sb("mv", [P, NT, 2])
        rstd = sb("rstd", [P, NT])
        nwt = sb("nwt", [P, 3, NT])
        router = sb("router", [P, 2, KT, E])
        later = ExitStack()
        scan = ctx.enter_context(ExitStack())

        def sb(name, shape, dt=fp32):
            return scan.enter_context(nc.sbuf_tensor(name, shape, dt))

        dtv = sb("dtv", [P, NT, H])
        cs = sb("cs", [P, NT, H])
        dec = sb("dec", [P, NT, H])
        etot = sb("etot", [P, NT, H])
        csp = sb("csp", [P, NT, PIECES, H], bf16)
        csT = sb("csT", [PIECES * H, T], bf16)
        wbs = sb("wbs", [P, 2, G, 512], bf16)
        CB = sb("CB", [P, G, TB, P])
        Btok = sb("Btok", [P, G, TB, P])
        CT = sb("CT", [P, G, S])
        BT = sb("BT", [P, S])
        wA = sb("wA", [P, 2, 512])
        whl = sb("whl", [P, 2, 2, 512], bf16)
        wB = sb("wB", [P, 8, D])
        chn = sb("chn", [P, H, CH])
        raw = sb("raw", [P, 2, S + 3])
        u = sb("u", [P, 2, S])
        thx = sb("thx", [P, S])
        thg = sb("thg", [P, S])
        gs = sb("gs", [P, 4, S])
        rel = sb("rel", [P, S])
        Lm = sb("Lm", [P, 2, S])
        scb = Lm[:, :, :].rearrange("p a (b n) -> p (a b) n", n=P)
        Em = sb("Em", [P, 2, S - P])
        Mm = sb("Mm", [P, 2, S])
        dtmp = Mm[:, :, :].rearrange("p a (b t h) -> p (a b) t h", t=NT, h=H)
        xbuf = sb("xbuf", [P, 2 * S + 6 * (S - P)])
        Xdt = xbuf[:, 0:2 * S].rearrange("p (a n) -> p a n", a=2)
        Xw, CE, St = (xbuf[:, 2 * S + 2 * m * (S - P):2 * S + 2 * (m + 1) * (S - P)].rearrange("p (a n) -> p a n", a=2)
                      for m in range(3))
        yv = sb("yv", [P, 2, S])
        yb = sb("yb", [P, 8, S])
        ysq = sb("ysq", [P, S])
        sqa = sb("sqa", [P, 2, S])
        ssv = sb("ssv", [P, TB])
        rg = sb("rg", [P, TB])
        wm = yb[:, :, :].rearrange("p a b -> p (a b)")[:, 0:KT * 6 * D].rearrange(
            "p (k n) -> p k n", k=KT)
        rawg = xbuf[:, 0:4 * (S + 3)].rearrange("p (a n) -> p a n", a=4)
        wm1 = Btok[:, :, :, :].rearrange("p a b c -> p (a b c)")[:, 0:KT * 6 * D].rearrange(
            "p (k n) -> p k n", k=KT)
        wbf = CB[:, :, :, :].rearrange("p a b c -> p a (b c)")

        scb_sign = Lm[:, :, :].rearrange("p a b -> p (a b)")

        scan.close()
        def sb(name, shape, dt=fp32):
            return later.enter_context(nc.sbuf_tensor(name, shape, dt))

        sel = sb("sel", [PIECES * E1, sum(FT) * P], bf16)
        F1 = max(FT)
        w13 = sb("w13", [P, F1, 512])
        w13s = sb("w13s", [P, 2, F1, 512], bf16)
        w2 = sb("w2", [P, F1, D])
        selw = w2[0:PIECES * E1, :, :].rearrange("p f d -> p (f d)")[:, 0:sum(FT) * P]
        pr = sb("pr", [P, NT, E])
        prb = sb("prb", [P, NT, E])
        rank = sb("rank", [P, NT, E])
        cmpa = sb("cmpa", [P, NT, E, E])
        cmpb = sb("cmpb", [P, NT, E, E])
        comb = sb("comb", [P, NT, E1])
        cpt = sb("cpt", [P, NT, E1])
        cpb = sb("cpb", [P, NT, PIECES, E1], bf16)
        cbT = sb("cbT", [PIECES * E1, T], bf16)
        r1 = sb("r1", [P, NT])
        sS = sb("sS", [P, 2, S])
        ua = sb("ua", [P, 2, S])
        uc = sb("uc", [P, 2, S])
        fth = sb("fth", [P, 2, S])
        fg = sb("fg", [P, S])
        hf = sb("hf", [P, 2, S])
        xo = sb("xo", [P, TB, D])
        zerob = sb("zerob", [P, P + S], bf16)
        later.close()
        def sb(name, shape, dt=fp32):
            return ctx.enter_context(nc.sbuf_tensor(name, shape, dt))

        wqk = sb("wqk", [P, 2, KT, P])
        wv = sb("wv", [P, KT, D])
        wo = sb("wo", [P, KT, D])
        qs = sb("qs", [P, B, S])
        qp = sb("qp", [P, PIECES, B, S], bf16)
        ks = sb("ks", [P, B, S])
        aw = sb("aw", [P, 8, S])
        tb_, arg = aw[:, 0:4, :], aw[:, 4:8, :]
        wk = acc[:, :, :].rearrange("p t d -> p (t d)").rearrange("p (s n k) -> p s n k", s=2, n=2)
        hit = wk[:, :, 1, :]
        m8 = sb("m8", [P, 2, 2, 8])
        e8 = sb("e8", [P, 2, 8])
        ext = sb("ext", [P, B, 2])
        rk = hTs[:, 0].rearrange("p k t -> p (k t)").bitcast(fp32)[:, 0:2 * S].rearrange("p (a s) -> p a s", a=2)
        code = sb("code", [P, 3, S], bf16)
        cdT = sb("cdT", [P, TB, P], bf16)
        kd = sb("kd", [P, 2, S])
        PV = sb("PV", [P, TB, PIECES, P, 4], bf16)
        pvr = sb("pvr", [P, 4, TB * P])
        iotak = sb("iotak", [P, 2, K, QG], bf16)
        selQ = sb("selQ", [P, NQ, K, QG], bf16)
        OH = sb("OH", [P, TB, 2, NQ, P], bf16)
        gat = pvr[:, 0:2, :].rearrange("p a (g x) -> p (a g) x", x=16)
        gam = hTs[:, 1].rearrange("p k t -> p (k t)").bitcast(fp32).rearrange("p (g x) -> p g x", x=16)
        scl = sb("scl", [P, NQ, 2])
        VW = sb("VW", [P, 2, 4 * (OC + QG * 5)])
        VWd = VW[:, :, :].rearrange("p a (i x) -> p a i x", i=4)[:, :, :, 0:QG * 5].rearrange(
            "p a i (h c) -> p a i h c", h=QG)
        oc = pvr[0:OC, 2:4, :]
        Ex = sb("Ex", [P, 4, S])
        O5 = sb("O5", [P, TB, P, 5])
        ex_sign = Ex[:, 0:2, :].rearrange("p a b -> p (a b)")
        qm = aw[:, 0, :].rearrange("p (t h) -> p t h", t=TB)
        rden = aw[:, 1, :].rearrange("p (t h) -> p t h", t=TB)
        att = aw[:, 2:4, :].rearrange("p a (t h j) -> p (a t) h j", t=2, j=2)
        attT = aw[:, 4:6, :]
        attf = att.rearrange("p t h j -> p t (h j)")
        xo1 = aw[:, 6:8, :].rearrange("p a (t d) -> p (a t) d", t=2)

        names = ("d_cst d_x d_c d_wm0 d_wm1 d_small d_wbc d_out modp_done gmod_done sc_done "
                 "mods_done gm_done thc_done scb_done dve_seq pool_seq act_seq xh_done tr_done "
                 "hT_done hts_done dtp_done dtz_done dta_done dcs_done dex_done csp_done "
                 "cspT_done csT_done e_dt bcp_done wbs_hi wbs_done idb_done c_proj c_raw "
                 "c_step c_th c_bc c_mm c_evac c_cbm d_chn pad_done wsplit whi_done wo_done px "
                 "raw_done tr_x xdt_done pg thg_done gs_done pc pc2 e_done rel_done L_done "
                 "M_done cv_step thx_done xT_done xw_done ce_done ps rc_step py yc_done "
                 "yb_done ysq_done sq_add ssq_done out_done rg_step oa_done x1_done d_sel "
                 "d_w13 d_w2 d_attn sel_done zb_done rt_p rt_act rt_dve cp_done cpT_p cbT_done "
                 "fw_hi fw_done fu fs_c fa_done fth_done fh_done fout fg_done xf_done a_qk a_v "
                 "a_qkc a_q0 a_q1 a_q2 a_qp tk0 tk1 a_e8 a_ext a_kd a_kT a_pvs a_p0 a_p1 a_p2 "
                 "a_pv a_code a_cT a_cTc a_oh a_gat a_vw a_iota a_vwt a_oc a_oT a_mask a_Q "
                 "a_tb a_arg a_E a_PV a_O5 a_qT a_att a_attT a_attc a_out a_x").split()
        q = {n: sem(n) for n in names}
        d_wA = [sem(f"d_wA{n}") for n in range(2)]
        d_wB = [sem(f"d_wB{n}") for n in range(8)]

        QB, VB = (0, 1, 3, 4), (2, 5)

        block = ctx.enter_context(nc.Block())

        NWT = 11
        ROOT = 12

        def rsqrt_steps(dve, out, v, tmp, step, first):
            n = first
            nc.vector.tensor_scalar(tmp[0].bitcast(i32), v.bitcast(i32), 1, None,
                                    ALU.logical_shift_right).then_inc(step, 1)
            dve.wait_ge(step, n + 1)
            nc.vector.tensor_scalar(out.bitcast(i32), tmp[0].bitcast(i32), -1.0, float(0x5f3759df),
                                    ALU.mult, ALU.add).then_inc(step, 1)
            n = 2
            for _ in range(3):
                dve.wait_ge(step, first + n)
                nc.vector.tensor_tensor(tmp[0], out, out, ALU.mult).then_inc(step, 1)
                dve.wait_ge(step, first + n + 1)
                nc.vector.scalar_tensor_tensor(out=tmp[1], in0=tmp[0], scalar=-0.5, in1=v, op0=ALU.mult,
                                               op1=ALU.mult).then_inc(step, 1)
                dve.wait_ge(step, first + n + 2)
                nc.vector.scalar_tensor_tensor(out=out, in0=tmp[1], scalar=1.5, in1=out, op0=ALU.add,
                                               op1=ALU.mult).then_inc(step, 1)
                n += 3
            dve.wait_ge(step, first + n)

        def slots(eng, b, slot, ahead=None):
            for i in range(8):
                slot(i, 0, b)
            with eng.Fori(1, 4) as it:
                for i in range(8):
                    slot(i, it, b)
            for i in range(7):
                slot(i, 4, b)
                if ahead and i == 1 and b + 1 < B:
                    ahead(b + 1)

        def stages(i, it):
            def head(back):
                j, n = i - back, it
                if j < 0:
                    j, n = j + 8, it - 1
                if type(n) is int and not 0 <= n < H // 8:
                    return None
                return j, n
            return head

        @block.sync
        def _(sp):
            sp.dma_start(cT[:], io["cT"][:, :]).then_inc(q["d_c"], 16)
            sp.dma_start(x_sb[:], io["x"].rearrange("(t p) d -> p t d", p=P)).then_inc(q["d_x"], 16)
            sp.dma_start(wm, io["wmod"][0]).then_inc(q["d_wm0"], 16)
            sp.dma_start(cst[:], io["cst"][:, :]).then_inc(q["d_cst"], 16)
            sp.dma_start(small[:], io["small"].partition_broadcast(P)).then_inc(q["d_small"], 16)
            sp.dma_start(wdt[:], io["wdt"]).then_inc(q["d_small"], 16)
            sp.dma_start(bcp[:], io["bcp"]).then_inc(q["d_small"], 16)
            sp.dma_start(router[:], io["router"]).then_inc(q["d_small"], 16)
            sp.dma_start(wbf, io["wbc"]).then_inc(q["d_wbc"], 16)
            sp.dma_start(chn[:], io["chn"]).then_inc(q["d_chn"], 16)
            sp.dma_start(wm1, io["wmod"][1]).then_inc(q["d_wm1"], 16)

            def load_slot(i, it, b):
                def number(h):
                    k = 8 * h[1] + h[0]
                    return k if type(k) is int else sp.snap(k)

                head = stages(i, it)
                h0, h3 = head(0), head(3)
                if h0:
                    kk = number(h0)
                    split = H * b + kk - 1
                    if type(split) is not int:
                        split = sp.snap(split)
                    if type(split) is not int or split > 0:
                        sp.wait_ge(q["wsplit"], split)
                    sp.dma_start(wA[:, i % 2, :], io["win"][bass.ds(kk, 1)].squeeze(0)).then_inc(d_wA[i % 2], 16)
                if h3:
                    j, n = h3
                    kk = number(h3)
                    outs = TB * (NG * b + 2 * n + j // HG - 1)
                    if type(outs) is not int:
                        outs = sp.snap(outs)
                    if type(outs) is not int or outs > 0:
                        sp.wait_ge(q["out_done"], outs)
                    sp.dma_start(wB[:, j, :], io["wob"][bass.ds(kk, 1)].squeeze(0)).then_inc(d_wB[j], 16)

            for b in range(B):
                slots(sp, b, load_slot)
            sp.wait_ge(q["wsplit"], B * H - 1)
            sp.dma_start(wA[:, 0, :], io["win"][0]).then_inc(d_wA[0], 16)

            def experts_load(L):
                n = FT[L]
                if L == 0:
                    sp.wait_ge(q["x1_done"], 1)
                else:
                    sp.wait_ge(q["a_x"], B)
                sp.dma_start(selw, io["sel"]).then_inc(q["d_sel"], 16)
                sp.dma_start(w13[:, 0:n, 0:io[f"w13_{L}"].shape[2]], io[f"w13_{L}"]).then_inc(q["d_w13"], 16)
                sp.wait_ge(q["sel_done"], L + 1)
                sp.dma_start(w2[:, 0:n, :], io[f"w2_{L}"]).then_inc(q["d_w2"], 16)

            def store():
                sp.dma_start(io["out"].rearrange("(t p) d -> p t d", p=P), x_sb[:]).then_inc(q["d_out"], 16)
                sp.wait_ge(q["d_out"], 16)

            experts_load(0)
            sp.wait_ge(q["xf_done"], B)
            sp.dma_start(wqk[:], io["wqk"]).then_inc(q["d_attn"], 16)
            sp.dma_start(wv[:], io["wv"]).then_inc(q["d_attn"], 16)
            sp.dma_start(wo[:], io["wo"]).then_inc(q["d_attn"], 16)
            sp.wait_ge(q["a_x"], B)
            experts_load(1)
            sp.wait_ge(q["xf_done"], 2 * B)
            store()

        @block.tensor
        def _(pe):
            def modulation(L):
                w = (wm, wm1)[L]
                pe.wait_ge(q[f"d_wm{L}"], 16)
                for n, m in enumerate((0, 1, 3, 4)):
                    for ft in range(KT):
                        o = (n * KT + ft) * B
                        for kt in range(KT):
                            last = nc.tensor.matmul(
                                bank[4][:, o:o + B], w[:, kt, m * D + ft * P:m * D + (ft + 1) * P],
                                sc[:, (L * KT + kt) * B:(L * KT + kt + 1) * B],
                                start=kt == 0, stop=kt == KT - 1)
                last.then_inc(q["modp_done"], 1)

            def gates():
                for L in range(2):
                    w = (wm, wm1)[L]
                    for n, m in enumerate((2, 5)):
                        for b in range(B):
                            o = (L * 2 + n) * B + b
                            for kt in range(KT):
                                last = nc.tensor.matmul(
                                    bank[o // 2][:, (o % 2) * D:(o % 2 + 1) * D],
                                    scb[:, (L * KT + kt) * B + b, :], w[:, kt, m * D:(m + 1) * D],
                                    start=kt == 0, stop=kt == KT - 1)
                last.then_inc(q["gmod_done"], 1)

            pe.wait_ge(q["sc_done"], 1)
            modulation(0)

            def transposed_rows(n):
                for b in range(B):
                    pe.wait_ge(q["xh_done"], n * B + b + 1)
                    for ft in range(KT):
                        for t in range(TB):
                            last = nc.tensor.transpose(
                                bank[b * KT + ft][:, t * P:(t + 1) * P],
                                acc[:, b * TB + t, ft * P:(ft + 1) * P], ident)
                        last.then_inc(q["tr_done"], 1)

            pe.wait_ge(q["d_cst"], 16)
            transposed_rows(0)

            pe.wait_ge(q["hT_done"], 4)
            pe.wait_ge(q["d_small"], 64)
            for t in range(NT):
                for kt in range(KT):
                    last = nc.tensor.matmul(bank[4][:, t * H:(t + 1) * H], hT[:, kt, t * P:(t + 1) * P],
                                            wdt[:, kt, :], start=kt == 0, stop=kt == KT - 1)
            last.then_inc(q["dtp_done"], 1)
            pe.wait_ge(q["scb_done"], 1)
            pe.wait_ge(q["d_wm1"], 16)
            gates()
            pe.wait_ge(q["dta_done"], 1)
            ab = dtmp[:, 2, :, :].rearrange("p t h -> p (t h)")
            nc.tensor.matmul(bank[5][:, 0:NT * H], tri, ab, start=True, stop=True)
            nc.tensor.matmul(bank[6][:, 0:NT * H], ones, ab, start=True, stop=True).then_inc(q["dcs_done"], 1)
            modulation(1)
            pe.wait_ge(q["csp_done"], 1)
            pe.wait_ge(q["idb_done"], 2)
            cspT = bank[7][:, :].bitcast(bf16)
            for t in range(NT):
                last = nc.tensor.transpose(cspT[0:PIECES * H, t * P:(t + 1) * P],
                                           csp[:, t, :, :].rearrange("p a h -> p (a h)"), identb[:])
            last.then_inc(q["cspT_done"], 1)

            def split_product(out, wpart, hpart):
                n = 0
                for a, c in ((0, 0), (0, 1), (1, 0)):
                    for kt in range(KT):
                        last = nc.tensor.matmul(out, wpart(a, kt), hpart(c, kt), start=n == 0, stop=n == 5)
                        n += 1
                return last

            def group_rows(g, b):
                if b and type(g) is int and g == 0:
                    pe.wait_ge(q["gs_done"], H * b)
                    pe.wait_ge(q["raw_done"], H * b)
                if not (type(g) is int and G * b + g == 0):
                    pe.wait_ge(q["c_raw"], G * b + g)
                for n in range(2):
                    last = split_product(
                        bank[n][:, :],
                        lambda a, kt: wbs[:, a, bass.ds(g, 1), (n * KT + kt) * P:(n * KT + kt + 1) * P].squeeze(1),
                        lambda a, kt: hTs[:, a, kt, b * S:(b + 1) * S])
                last.then_inc(q["c_proj"], 1)

            def group_products(g, b):
                pe.wait_ge(q["c_bc"], 2 * (G * b + g) + 2)
                if not (type(g) is int and G * b + g == 0):
                    pe.wait_ge(q["c_evac"], G * b + g)
                for t in range(TB):
                    last = nc.tensor.matmul(bank[2][:, t * P:(t + 1) * P], BT[:, t * P:(t + 1) * P],
                                            CT[:, bass.ds(g, 1), t * P:(t + 1) * P].squeeze(1), start=True, stop=True)
                for t in range(TB):
                    last = nc.tensor.transpose(bank[3][:, t * P:(t + 1) * P], BT[:, t * P:(t + 1) * P], ident)
                last.then_inc(q["c_mm"], 1)

            def scan_slot(i, it, b):
                head = stages(i, it)
                h0, h1, h2 = head(0), head(1), head(2)
                n0, n1, n2 = (H * b + 8 * h[1] + h[0] if h else None for h in (h0, h1, h2))

                def since(name, n):
                    if type(n) is not int or n > 0:
                        pe.wait_ge(q[name], n)

                if h0:
                    w = whl[:, i % 2, :, :]
                    pe.wait_ge(q["wsplit"], n0 + 1)
                    since("raw_done", n0)
                    split_product(bank[0][:, :], lambda a, kt: w[:, a, kt * P:(kt + 1) * P],
                                  lambda a, kt: hTs[:, a, kt, b * S:(b + 1) * S]).then_inc(q["px"], 1)
                if h1:
                    j = h1[0]
                    pe.wait_ge(q["xT_done"], n1 + 1)
                    since("xdt_done", n1)
                    for t in range(TB):
                        last = nc.tensor.transpose(bank[2][:, t * P:(t + 1) * P],
                                                   xT[:, j % 4, t * P:(t + 1) * P], ident)
                    last.then_inc(q["tr_x"], 1)
                if h2:
                    j = h2[0]
                    pe.wait_ge(q["rc_step"], 3 * n2 + 3)
                    pe.wait_ge(q["ce_done"], n2 + 1)
                    for c in range(1, TB):
                        last = nc.tensor.matmul(bank[5][:, c * P:(c + 1) * P], St[:, j % 2, (c - 1) * P:c * P],
                                                CE[:, j % 2, (c - 1) * P:c * P], start=False, stop=True,
                                                skip_group_check=True)
                    last.then_inc(q["py"], 1)
                if h0:
                    hcol = 8 * h0[1] + h0[0]
                    since("rel_done", n0)
                    if type(it) is int and 8 * it + i == 0:
                        pe.wait_ge(q["c_evac"], G * (b + 1))
                        pe.wait_ge(q["csT_done"], 1)
                        pe.wait_ge(q["mods_done"], 2)
                    nc.tensor.matmul(
                        bank[3][:, :], identb96[:, 0, bass.ds(hcol, 1)].to_broadcast([PIECES * H, P]),
                        csT[:, b * S:(b + 1) * S], start=True, stop=True, skip_group_check=True)\
                        .then_inc(q["pc"], 1)
                out_slot(i, it, b)
                if h0:
                    pe.wait_ge(q["e_done"], n0 + 1)
                    for t in range(TB):
                        last = nc.tensor.matmul(bank[3][:, t * P:(t + 1) * P], csT[:, b * S + t * P:b * S + (t + 1) * P],
                                                identb96[:, 1, bass.ds(hcol, 1)].to_broadcast([PIECES * H, P]),
                                                start=False, stop=True, skip_group_check=True)
                    last.then_inc(q["pc2"], 1)
                if h1:
                    j = h1[0]
                    pe.wait_ge(q["xdt_done"], n1 + 1)
                    pe.wait_ge(q["M_done"], n1 + 1)
                    since("yc_done", n1)
                    for c in range(TB):
                        nc.tensor.matmul(bank[5][:, c * P:(c + 1) * P], Xdt[:, j % 2, c * P:(c + 1) * P],
                                         Mm[:, j % 2, c * P:(c + 1) * P], start=c == 0, stop=c == 0,
                                         skip_group_check=True)
                if h1:
                    since("rc_step", 3 * n1)
                if (e := out_event(i, it, 7)) and e[0] == 0:
                    pe.wait_ge(q["rg_step"], ROOT * (NG * b + e[2]) + 1)
                sums_slot(i, it, b)
                if h1:
                    j = h1[0]
                    pe.wait_ge(q["xw_done"], n1 + 1)
                    for c in range(TB - 1):
                        last = nc.tensor.matmul(bank[4][:, c * P:(c + 1) * P], Btok[:, j, c, :],
                                                Xw[:, j % 2, c * P:(c + 1) * P], start=True, stop=True)
                    last.then_inc(q["ps"], 1)
                if h0:
                    since("gs_done", n0)
                    split_product(bank[1][:, :], lambda a, kt: w[:, a, (KT + kt) * P:(KT + kt + 1) * P],
                                  lambda a, kt: hTs[:, a, kt, b * S:(b + 1) * S]).then_inc(q["pg"], 1)

            def sums_slot(i, it, b):
                e = out_event(i, it, 6)
                if not e or e[0]:
                    return
                _, j, gi = e
                jj = NG * b + gi
                if not stages(i, it)(1):
                    pe.wait_ge(q["rc_step"], 3 * H * (b + 1))
                pe.wait_ge(q["sq_add"], 3 * (jj + 1))
                for t in range(TB):
                    last = nc.tensor.matmul(bank[4][:, S - P + t:S - P + t + 1], sqa[:, j, t * P:(t + 1) * P], ones[:, 0:1],
                                            start=True, stop=True)
                last.then_inc(q["ssq_done"], 1)

            def out_slot(i, it, b):
                e = out_event(i, it, 6)
                if not e:
                    return
                t, j, gi = e
                jj = NG * b + gi
                y0 = HG * j
                if t == 0:
                    pe.wait_ge(q["wo_done"], HG * (jj + 1))
                    pe.wait_ge(q["yb_done"], HG * (jj + 1))
                if type(jj) is not int or TB * jj + t > 1:
                    pe.wait_ge(q["oa_done"], TB * jj + t - 1)
                for m in range(HG):
                    last = nc.tensor.matmul(bank[6 + t % 2][:, 0:D], yb[:, y0 + m, t * P:(t + 1) * P],
                                            wB[:, y0 + m, :], start=m == 0, stop=m == HG - 1)
                last.then_inc(q["out_done"], 1)

            for b in range(B):
                if b == 0:
                    pe.wait_ge(q["wbs_done"], 1)
                    pe.wait_ge(q["hts_done"], 4)
                    pe.wait_ge(q["gm_done"], 4)
                    group_rows(0, b)
                else:
                    pe.wait_ge(q["oa_done"], TB * NG * b)
                group_rows(1, b)
                group_rows(2, b)
                group_products(0, b)
                with pe.Fori(1, G - 2) as g:
                    group_rows(g + 2, b)
                    group_products(g, b)
                group_products(G - 2, b)
                group_products(G - 1, b)
                pe.wait_ge(q["c_raw"], G * (b + 1))
                slots(pe, b, scan_slot, lambda b: group_rows(0, b))

            def experts(L):
                n0, nf = 2 * L + 1, FT[L]
                w13n = 2 if L == 0 else 1
                transposed_rows(n0)
                for t in range(NT):
                    if t % TB == 0:
                        pe.wait_ge(q["hT_done"], 4 * n0 + KT * (t // TB + 1))
                    for kt in range(KT):
                        last = nc.tensor.matmul(bank[6][:, t * E:(t + 1) * E], hT[:, kt, t * P:(t + 1) * P],
                                                router[:, L, kt, :], start=kt == 0, stop=kt == KT - 1)
                last.then_inc(q["rt_p"], 1)

                def number(f, b):
                    return (FT[0] * B if L else 0) + nf * b + f

                def products(f, b, par):
                    n = number(f, b)
                    if not (type(n) is int and n < 2):
                        pe.wait_ge(q["fa_done"], n - 1)
                    pe.wait_ge(q["fw_done"], (FT[0] if L else 0) + f + 1)
                    for m in range(w13n):
                        split_product(bank[3 * par + m][:, :],
                                      lambda a, kt: w13s[:, a, bass.ds(f, 1), (m * KT + kt) * P:(m * KT + kt + 1) * P].squeeze(1),
                                      lambda a, kt: hTs[:, a, kt, b * S:(b + 1) * S])

                def select(f, b, par):
                    nc.tensor.matmul(bank[3 * par + 2][:, :], sel[:, bass.ds((FT[0] * P if L else 0) + f * P, P)],
                                     cbT[:, b * S:(b + 1) * S], start=True, stop=True).then_inc(q["fu"], 1)

                def rows_in(f, b, par):
                    products(f, b, par)
                    select(f, b, par)

                def rows_out(f, b, par):
                    pe.wait_ge(q["fh_done"], number(f, b) + 1)
                    for t in range(TB):
                        last = nc.tensor.matmul(bank[6 + t // 2][:, (t % 2) * D:(t % 2 + 1) * D],
                                                hf[:, par, t * P:(t + 1) * P], w2[:, bass.ds(f, 1), :].squeeze(1),
                                                start=False, stop=False, skip_group_check=True)
                    last.then_inc(q["fout"], 1)

                pe.wait_ge(q["hts_done"], 4 * (L + 2))
                products(0, 0, 0)
                products(1, 0, 1)
                pe.wait_ge(q["cp_done"], L + 1)
                cT_ = bank[7][:, :].bitcast(bf16)
                for t in range(NT):
                    last = nc.tensor.transpose(cT_[0:PIECES * E1, t * P:(t + 1) * P],
                                               cpb[:, t, :, :].rearrange("p a e -> p (a e)"), identb[:])
                last.then_inc(q["cpT_p"], 1)
                pe.wait_ge(q["cbT_done"], L + 1)
                pe.wait_ge(q["zb_done"], L + 1)
                pe.wait_ge(q["sel_done"], L + 1)
                select(0, 0, 0)
                select(1, 0, 1)
                pe.wait_ge(q["d_w2"], 16 * (L + 1))
                for b in range(B):
                    if b:
                        rows_in(1, b, 1 - b)
                        pe.wait_ge(q["xf_done"], L * B + b)
                    for m in (6, 7):
                        nc.tensor.matmul(bank[m][:, :], zerob[:, 0:P], zerob[:, P:], start=True, stop=False,
                                         skip_group_check=True)
                    rows_out(0, b, b)
                    rows_in(2, b, b)
                    rows_out(1, b, 1 - b)
                    with pe.Fori(1, (nf - 1) // 2) as i:
                        for m in range(2):
                            rows_in(2 * i + m + 1, b, (b + m + 1) % 2)
                            rows_out(2 * i + m, b, (b + m) % 2)
                    if b + 1 < B:
                        rows_in(0, b + 1, b + 1)
                    rows_out(nf - 1, b, b)

            pe.wait_ge(q["x1_done"], 1)
            experts(0)

            def heads():
                transposed_rows(2)
                pe.wait_ge(q["d_attn"], 48)
                for b in range(B):
                    pe.wait_ge(q["hT_done"], 8 + KT * (b + 1))
                    hb = slice(b * S, (b + 1) * S)
                    if b:
                        pe.wait_ge(q["a_qkc"], 2 * b)
                    for m in (1, 0):
                        for kt in range(KT):
                            last = nc.tensor.matmul(bank[m][:, :], wqk[:, m, kt, :], hT[:, kt, hb],
                                                    start=kt == 0, stop=kt == KT - 1)
                        last.then_inc(q["a_qk"], 1)

                def tokens_first(b):
                    if b:
                        pe.wait_ge(q["a_O5"], NQ // 4 * b)
                    for t in range(TB):
                        for kt in range(KT):
                            last = nc.tensor.matmul(bank[5 + t // 2][:, (t % 2) * D:(t % 2 + 1) * D],
                                                    hT[:, kt, (b * TB + t) * P:(b * TB + t + 1) * P], wv[:, kt, :],
                                                    start=kt == 0, stop=kt == KT - 1)
                    last.then_inc(q["a_v"], 1)
                    for m in range(2):
                        pe.wait_ge(q["a_kd"], 2 * b + m + 1)
                        for t in range(TB):
                            last = nc.tensor.transpose(bank[3 + m][:, t * P:(t + 1) * P],
                                                       kd[:, m, t * P:(t + 1) * P], ident)
                        last.then_inc(q["a_kT"], 1)
                    pe.wait_ge(q["a_code"], b + 1)
                    cT_ = bank[2][:, :].bitcast(bf16)
                    for t in range(TB):
                        last = nc.tensor.transpose(cT_[:, t * P:(t + 1) * P], code[:, 2, t * P:(t + 1) * P], identb[:])
                    last.then_inc(q["a_cT"], 1)

                tokens_first(0)
                for b in range(B):
                    def spread(i, n):
                        c = NQ * b + 4 * n + i
                        if not (type(c) is int and c < 4):
                            pe.wait_ge(q["a_arg"], c - 3)
                        for pc in range(PIECES):
                            last = nc.tensor.matmul(
                                bank[QB[i]][:, :],
                                selQ[:, bass.ds(4 * n + i, 1), :, :].squeeze(1).rearrange("p k h -> p (k h)"),
                                qp[:, pc, b, :], start=pc == 0, stop=pc == PIECES - 1)
                        last.then_inc(q["a_Q"], 1)

                    def weigh(i, n, par):
                        c = NQ * b + 4 * n + i
                        if i == 0:
                            m = NQ // 4 * b + n
                            pe.wait_ge(q["a_vwt"], m + 1)
                            if not (type(m) is int and m < 2):
                                pe.wait_ge(q["a_oc"], m - 1)
                        pe.wait_ge(q["a_E"], c + 1)
                        nc.tensor.matmul(bank[VB[par]][0:OC, :], VW[:, par, i * OC:(i + 1) * OC], Ex[:, i, :],
                                         start=i == 0, stop=i == 3).then_inc(q["a_PV"], 1)

                    def turn(n, par):
                        m = NQ // 4 * b + n
                        if not (type(m) is int and m == 0):
                            pe.wait_ge(q["a_O5"], m)
                        pe.wait_ge(q["a_oc"], m + 1)
                        for t in range(TB):
                            last = nc.tensor.transpose(bank[6][:, t * OC:(t + 1) * OC],
                                                       oc[:, par, t * P:(t + 1) * P], ident[0:OC, 0:OC])
                        last.then_inc(q["a_oT"], 1)

                    def attend(n, par):
                        for i in range(4):
                            spread(i, n)
                            if i == 3:
                                weigh(0, n, par)
                            elif type(n) is not int or n:
                                weigh(i + 1, n - 1, 1 - par)
                            if i == 0 and (type(n) is not int or n > 1):
                                turn(n - 2, par)

                    pe.wait_ge(q["a_pv"], 4 * (b + 1))
                    pe.wait_ge(q["a_cTc"], b + 1)
                    pe.wait_ge(q["a_pvs"], 4 * (b + 1))
                    pe.wait_ge(q["a_qkc"], 2 * B)
                    if b:
                        pe.wait_ge(q["a_x"], b)
                    for t in range(TB):
                        pe.wait_ge(q["a_oh"], TB * b + t + 1)
                        for n in range(NQ // 4):
                            for g4 in range(4):
                                for side in range(2):
                                    o = (g4 * 2 + side) * 48
                                    last = nc.tensor.matmul(
                                        bank[n][:, o:o + 48], OH[:, t, side, 4 * n + g4, :],
                                        PV[:, t, :, 16 * n + 4 * g4:16 * n + 4 * g4 + 4, :],
                                        start=t == 0 and o == 0, stop=t == TB - 1, skip_group_check=True)
                            if t == TB - 1:
                                last.then_inc(q["a_vw"], 1)
                    pe.wait_ge(q["a_qp"], b + 1)
                    pe.wait_ge(q["a_gat"], NQ // 4 * (b + 1))
                    for n in range(3):
                        attend(n, n % 2)
                    with pe.Fori(0, (NQ // 4 - 4) // 2) as r:
                        for m in range(2):
                            attend(2 * r + 3 + m, 1 - m)
                    attend(NQ // 4 - 1, 1)
                    turn(NQ // 4 - 2, 0)
                    for i in range(1, 4):
                        weigh(i, NQ // 4 - 1, 1)
                    turn(NQ // 4 - 1, 1)
                    pe.wait_ge(q["a_arg"], NQ * (b + 1))
                    for t in range(TB):
                        last = nc.tensor.transpose(bank[7][:, t * P:(t + 1) * P], qs[:, b, t * P:(t + 1) * P], ident)
                    last.then_inc(q["a_qT"], 1)
                    if b + 1 < B:
                        tokens_first(b + 1)
                    pe.wait_ge(q["a_att"], b + 1)
                    for kt in range(KT):
                        for t in range(TB):
                            last = nc.tensor.transpose(bank[kt][:, t * P:(t + 1) * P],
                                                       attf[:, t, kt * P:(kt + 1) * P], ident)
                    last.then_inc(q["a_attT"], 1)
                    pe.wait_ge(q["a_attc"], b + 1)
                    for t in range(TB):
                        for kt in range(KT):
                            last = nc.tensor.matmul(bank[t // 2][:, (t % 2) * D:(t % 2 + 1) * D],
                                                    attT[:, kt, t * P:(t + 1) * P], wo[:, kt, :],
                                                    start=kt == 0, stop=kt == KT - 1)
                    last.then_inc(q["a_out"], 1)

            heads()
            pe.wait_ge(q["a_x"], B)
            experts(1)

        @block.scalar
        def _(act):
            act.wait_ge(q["d_c"], 16)
            nc.scalar.activation(sc[:], cT[:], ACT.Tanh, scale=0.5).then_inc(q["thc_done"], 1)

            def modulate(n, L):
                act.wait_ge(q["mods_done"], L + 1)
                for b in range(B):
                    for ft in range(KT):
                        act.wait_ge(q["tr_done"], 4 * n + b * KT + ft + 1)
                        nc.scalar.activation(hT[:, ft, b * S:(b + 1) * S], bank[b * KT + ft][:, :], ACT.Identity,
                                             bias=mods[:, L, 2 * (n % 2), ft, b:b + 1],
                                             scale=mods[:, L, 2 * (n % 2) + 1, ft, b:b + 1]).then_inc(q["hT_done"], 1)

            modulate(0, 0)
            act.wait_ge(q["d_wbc"], 16)
            nc.scalar.activation(wbs[:, 0], wbf, ACT.Copy).then_inc(q["wbs_hi"], 1)
            act.wait_ge(q["dtz_done"], 2)
            nc.scalar.activation(dtmp[:, 1], dtmp[:, 1], ACT.Exp).then_inc(q["act_seq"], 1)
            act.wait_ge(q["act_seq"], 1)
            nc.scalar.activation(dtmp[:, 1], dtmp[:, 1], ACT.Ln, bias=1.0).then_inc(q["act_seq"], 1)
            nc.scalar.activation(small[:, H:2 * H], small[:, H:2 * H], ACT.Exp).then_inc(q["act_seq"], 1)
            act.wait_ge(q["dex_done"], 1)
            nc.scalar.activation(dec[:], dec[:], ACT.Exp).then_inc(q["e_dt"], 1)
            nc.scalar.activation(etot[:], etot[:], ACT.Exp).then_inc(q["e_dt"], 1)

            def group_rows(g, par, b):
                n = G * b + g
                if b and type(g) is int and g == 0:
                    act.wait_ge(q["yb_done"], H * b)
                    act.wait_ge(q["py"], H * b)
                if b and type(g) is int and g == 0:
                    act.wait_ge(q["pad_done"], b + 1)
                if not (type(n) is int and n < 2):
                    act.wait_ge(q["c_step"], 6 * n - 6)
                    act.wait_ge(q["c_bc"], 2 * n - 2)
                act.wait_ge(q["c_proj"], n + 1)
                for m in range(2):
                    w = lambda tap: bcp[:, bass.ds(g, 1), m, tap:tap + 1].squeeze(1)
                    nc.scalar.activation(rawg[:, 2 * par + m, 3:], bank[m][:, :], ACT.Copy)
                    last = nc.scalar.activation(gs[:, 2 * par + m, :], bank[m][:, :], ACT.Identity, scale=w(3),
                                                bias=w(4))
                last.then_inc(q["c_raw"], 1)

            def group_tanh(g, par, b):
                n = G * b + g
                for m, th in enumerate((thx, thg)):
                    if not (type(n) is int and n == 0):
                        act.wait_ge(q["c_bc"], 2 * n - 1 + m)
                    act.wait_ge(q["c_step"], 6 * n + 5 + m)
                    nc.scalar.activation(th[:], gs[:, 2 * par + m, :], ACT.Tanh).then_inc(q["c_th"], 1)

            def group_evac(g, b):
                act.wait_ge(q["c_mm"], G * b + g + 1)
                nc.scalar.activation(CB[:, bass.ds(g, 1), :, :].squeeze(1).rearrange("p t n -> p (t n)"),
                                     bank[2][:, :], ACT.Copy)
                nc.scalar.activation(Btok[:, bass.ds(g, 1), :, :].squeeze(1).rearrange("p t n -> p (t n)"),
                                     bank[3][:, :], ACT.Copy).then_inc(q["c_evac"], 1)

            def scan_slot(i, it, b):
                head = stages(i, it)
                h0, h1, h2 = head(0), head(1), head(2)
                n0, n1, n2 = (H * b + 8 * h[1] + h[0] if h else None for h in (h0, h1, h2))

                def since(name, n):
                    if type(n) is not int or n > 0:
                        act.wait_ge(q[name], n)

                if h1:
                    j = h1[0]
                    since("gs_done", n1)
                    act.wait_ge(q["pg"], n1 + 1)
                    nc.scalar.activation(thg[:], bank[1][:, :], ACT.Tanh, scale=0.5).then_inc(q["thg_done"], 1)
                if h0:
                    hcol = 8 * h0[1] + h0[0]
                    since("cv_step", 3 * n0 - 3)
                    since("xT_done", n0 - 1)
                    act.wait_ge(q["px"], n0 + 1)
                    nc.scalar.activation(raw[:, i % 2, 3:], bank[0][:, :], ACT.Copy)
                    nc.scalar.activation(u[:, i % 2, :], bank[0][:, :], ACT.Identity,
                                         scale=chn[:, bass.ds(hcol, 1), 3:4].squeeze(1),
                                         bias=chn[:, bass.ds(hcol, 1), 4:5].squeeze(1)).then_inc(q["raw_done"], 1)
                if h1:
                    hcol = 8 * h1[1] + h1[0]
                    since("py", n1 - 1)
                    since("xw_done", n1 - 1)
                    act.wait_ge(q["tr_x"], n1 + 1)
                    for t in range(TB):
                        last = nc.scalar.activation(Xdt[:, j % 2, t * P:(t + 1) * P], bank[2][:, t * P:(t + 1) * P],
                                                    ACT.Copy, scale=dtv[:, b * TB + t, bass.ds(hcol, 1)])
                    last.then_inc(q["xdt_done"], 1)
                if h0:
                    j = h0[0]
                    since("ce_done", n0 - 1)
                    act.wait_ge(q["pc"], n0 + 1)
                    nc.scalar.activation(Em[:, j % 2, :], bank[3][:, P:S], ACT.Exp).then_inc(q["e_done"], 1)
                    since("pg", n0)
                    since("wsplit", n0)
                    act.wait_ge(d_wA[(i + 1) % 2], 16 * (H // 2 * b + 4 * it + (i + 1) // 2 + 1))
                    nc.scalar.activation(whl[:, (i + 1) % 2, 0, :], wA[:, (i + 1) % 2, :], ACT.Copy)\
                        .then_inc(q["whi_done"], 1)
                    since("L_done", n0)
                    act.wait_ge(q["pc2"], n0 + 1)
                    nc.scalar.activation(rel[:], bank[3][:, :], ACT.Relu, scale=-1.0).then_inc(q["rel_done"], 1)
                if h2:
                    j = h2[0]
                    jj = NG * b + 2 * h2[1] + j // 4
                    if j % HG == 0:
                        since("ssq_done", jj - 1)
                    elif j % HG > 1 or type(jj) is not int or jj > 0:
                        act.wait_ge(q["sq_add"], 3 * jj + j % HG - 1)
                    act.wait_ge(q["yb_done"], n2 + 1)
                    nc.scalar.activation(ysq[:] if j % HG else sqa[:, j // HG, :], yb[:, j, :], ACT.Square)\
                        .then_inc(q["ysq_done"], 1)
                if h0:
                    since("M_done", n0 - 1)
                    act.wait_ge(q["rel_done"], n0 + 1)
                    nc.scalar.activation(Lm[:, i % 2, :], rel[:], ACT.Exp, scale=-1.0).then_inc(q["L_done"], 1)
                    since("xT_done", n0)
                    act.wait_ge(q["cv_step"], 3 * n0 + 3)
                    nc.scalar.activation(thx[:], u[:, i % 2, :], ACT.Tanh, scale=0.5).then_inc(q["thx_done"], 1)

            act.wait_ge(d_wA[0], 16)
            nc.scalar.activation(whl[:, 0, 0, :], wA[:, 0, :], ACT.Copy).then_inc(q["whi_done"], 1)
            act.wait_ge(q["bcp_done"], 1)
            act.wait_ge(q["d_chn"], 16)
            for b in range(B):
                if b == 0:
                    group_rows(0, 0, b)
                group_rows(1, 1, b)
                group_tanh(0, 0, b)
                with act.Fori(1, G // 2) as g2:
                    for m in range(2):
                        g = 2 * g2 - 1 + m
                        group_rows(g + 1, m, b)
                        group_tanh(g, 1 - m, b)
                        group_evac(g - 1, b)
                group_tanh(G - 1, 1, b)
                group_evac(G - 2, b)
                group_evac(G - 1, b)
                act.wait_ge(q["c_bc"], 2 * G * (b + 1))
                slots(act, b, scan_slot, lambda b: group_rows(0, 0, b))

            def experts(L):
                n0, nf = 2 * L + 1, FT[L]
                w = 512 if L == 0 else 256
                base = FT[0] * B if L else 0
                modulate(n0, L)
                act.wait_ge(q["d_w13"], 16 * (L + 1))
                if L:
                    act.wait_ge(q["a_x"], B)
                def high_half(f):
                    nc.scalar.activation(w13s[:, 0, f, 0:w], w13[:, f, 0:w], ACT.Copy).then_inc(q["fw_hi"], 1)

                for f in range(2 if L == 0 else nf):
                    high_half(f)
                if L == 0:
                    act.wait_ge(q["rt_p"], 1)
                    nc.scalar.activation(pr[:].rearrange("p t e -> p (t e)"), bank[6][:, 0:NT * E], ACT.Tanh,
                                         scale=0.5).then_inc(q["rt_act"], 1)
                    for f in range(2, nf):
                        high_half(f)
                else:
                    act.wait_ge(q["rt_dve"], 1)
                    nc.scalar.activation(pr[:], pr[:], ACT.Exp).then_inc(q["rt_act"], 1)

                def hidden(f, b, par):
                    n = base + nf * b + f
                    def since(name, m):
                        if type(m) is not int or m > 0:
                            act.wait_ge(q[name], m)
                    since("fh_done", n - 1)
                    act.wait_ge(q["fu"], n + 1)
                    if L == 0:
                        nc.scalar.activation(sS[:, par, :], bank[3 * par + 2][:, :], ACT.Copy).then_inc(q["fs_c"], 1)
                        act.wait_ge(q["fa_done"], n + 1)
                        nc.scalar.activation(fth[:, par, :], ua[:, par, :], ACT.Tanh, scale=0.5)\
                            .then_inc(q["fth_done"], 1)
                    else:
                        nc.scalar.activation(fth[:, par, :], bank[3 * par][:, :], ACT.Tanh, scale=0.5)\
                            .then_inc(q["fth_done"], 1)

                for b in range(B):
                    for m in range(2):
                        hidden(m, b, (b + m) % 2)
                    with act.Fori(1, (nf - 1) // 2) as i:
                        for m in range(2):
                            hidden(2 * i + m, b, (b + m) % 2)
                    hidden(nf - 1, b, b)

            experts(0)

            def heads():
                modulate(2, 1)
                for b in range(B):
                    act.wait_ge(q["a_qk"], 2 * b + 1)
                    nc.scalar.activation(ks[:, b, :], bank[1][:, :], ACT.Copy).then_inc(q["a_qkc"], 1)
                    act.wait_ge(q["a_qk"], 2 * b + 2)
                    nc.scalar.activation(qs[:, b, :], bank[0][:, :], ACT.Copy).then_inc(q["a_qkc"], 1)
                act.wait_ge(q["a_qkc"], 2 * B)
                nc.scalar.activation(qp[:, 0], qs[:], ACT.Copy).then_inc(q["a_q0"], 1)

                def pieces(b, between):
                    for side in range(2):
                        act.wait_ge(q["a_ext"], 2 * b + side + 1)
                        if b:
                            act.wait_ge(q["a_kT"], 2 * b)
                        nc.scalar.activation(kd[:, side, :], ks[:, b, :], ACT.Identity,
                                             bias=ext[:, b, side:side + 1]).then_inc(q["a_kd"], 1)
                    if b == 0:
                        act.wait_ge(q["a_q1"], 1)
                        nc.scalar.activation(qp[:, 1], pvr[:, 0:2], ACT.Copy).then_inc(q["a_q2"], 1)
                        act.wait_ge(q["a_qp"], B)
                    else:
                        act.wait_ge(q["a_oT"], NQ // 4 * b)
                        act.wait_ge(q["a_vw"], NQ // 4 * b)
                    for qq in (2, 3, 0, 1):
                        if qq < 2:
                            act.wait_ge(q["a_kT"], 2 * b + qq + 1)
                            last = nc.scalar.activation(pvr[:, qq, :], bank[3 + qq][:, :], ACT.Copy)
                        else:
                            act.wait_ge(q["a_v"], b + 1)
                            for half in range(2):
                                last = nc.scalar.activation(
                                    pvr[:, qq, half * 2 * P:(half + 1) * 2 * P].rearrange("p (t h) -> p t h", t=2),
                                    bank[5 + half][:, :].rearrange("p (t j h) -> p t j h", t=2, j=2)[:, :, qq - 2, :],
                                    ACT.Copy)
                        last.then_inc(q["a_pvs"], 1)
                    for n, qq in enumerate((2, 3, 0, 1)):
                        act.wait_ge(q["a_pvs"], 4 * b + n + 1)
                        nc.scalar.activation(PV[:, :, 0, :, qq], pvr[:, qq, :].rearrange("p (t h) -> p t h", t=TB),
                                             ACT.Copy).then_inc(q["a_p0"], 1)
                    between()
                    for n, qq in enumerate((2, 3, 0, 1)):
                        act.wait_ge(q["a_p1"], 4 * b + n + 1)
                        nc.scalar.activation(PV[:, :, 1, :, qq], pvr[:, qq, :].rearrange("p (t h) -> p t h", t=TB),
                                             ACT.Copy).then_inc(q["a_p2"], 1)

                def turned(b):
                    act.wait_ge(q["a_attT"], b + 1)
                    for kt in range(KT):
                        last = nc.scalar.activation(attT[:, kt, :], bank[kt][:, :], ACT.Copy)
                    last.then_inc(q["a_attc"], 1)

                pieces(0, lambda: None)
                for b in range(B):
                    def part(i, n):
                        c = NQ * b + 4 * n + i
                        if not (type(c) is int and c < 4):
                            act.wait_ge(q["a_arg"], c - 3)
                        act.wait_ge(q["a_Q"], c + 1)
                        nc.scalar.activation(tb_[:, i, :], bank[QB[i]][:, :], ACT.Identity,
                                             scale=scl[:, bass.ds(4 * n + i, 1), 1:2].squeeze(1)).then_inc(q["a_tb"], 1)

                    def grow(i, n):
                        c = NQ * b + 4 * n + i
                        if not (type(c) is int and c < 4):
                            act.wait_ge(q["a_PV"], c - 3)
                        act.wait_ge(q["a_arg"], c + 1)
                        nc.scalar.activation(Ex[:, i, :], arg[:, i, :], ACT.Exp).then_inc(q["a_E"], 1)

                    def keep(n, par):
                        m = NQ // 4 * b + n
                        if not (type(m) is int and m < 2):
                            act.wait_ge(q["a_oT"], m - 1)
                        act.wait_ge(q["a_PV"], 4 * m + 4)
                        nc.scalar.activation(oc[:, par, :], bank[VB[par]][0:OC, :], ACT.Copy).then_inc(q["a_oc"], 1)

                    def attend(n, par):
                        for i in range(4):
                            part(i, n)
                            if i > 1 or type(n) is not int or n:
                                grow((i - 2) % 4, n if i > 1 else n - 1)
                        if type(n) is not int or n:
                            keep(n - 1, 1 - par)

                    act.wait_ge(q["a_iota"], 3 * (b + 1))
                    if b:
                        act.wait_ge(q["a_x"], b)
                    for n in range(3):
                        attend(n, n % 2)
                    with act.Fori(0, (NQ // 4 - 4) // 2) as r:
                        for m in range(2):
                            attend(2 * r + 3 + m, 1 - m)
                    attend(NQ // 4 - 1, 1)
                    for i in range(2, 4):
                        grow(i, NQ // 4 - 1)
                    keep(NQ // 4 - 1, 1)
                    if b + 1 < B:
                        pieces(b + 1, lambda: turned(b))
                    else:
                        turned(b)

            heads()
            experts(1)

        @block.vector
        def _(dve):
            count = [0]

            def link(ins):
                count[0] += 1
                ins.then_inc(q["dve_seq"], 1)
                dve.wait_ge(q["dve_seq"], count[0])

            link(nc.vector.memset(raw[:, :, 0:3], 0.0))
            dve.wait_ge(q["thc_done"], 1)
            link(nc.vector.scalar_tensor_tensor(out=sc[:], in0=sc[:], scalar=1.0, in1=cT[:], op0=ALU.add, op1=ALU.mult))
            nc.vector.tensor_scalar(sc[:], sc[:], 0.5, None, ALU.mult).then_inc(q["sc_done"], 1)
            dve.wait_ge(q["sc_done"], 1)
            nc.vector.tensor_copy(scb, sc[:].unsqueeze(2).to_broadcast([P, 2 * KT * B, P])).then_inc(q["scb_done"], 1)
            dve.wait_ge(q["d_cst"], 16)
            nc.vector.tensor_copy(identb[:], ident).then_inc(q["idb_done"], 1)
            nc.vector.tensor_copy(identb96[:, 0, :], cst[0:PIECES * H, C_STACK:C_STACK + H])
            nc.vector.tensor_scalar(identb96[:, 1, :], cst[0:PIECES * H, C_STACK:C_STACK + H], -1.0, None, ALU.mult)\
                .then_inc(q["idb_done"], 1)
            def row_stats(b0, b1):
                for t in range(b0 * TB, b1 * TB):
                    last = nc.vector.bn_stats(stats[:, t, :], x_sb[:, t, :])
                link(last)
                for t in range(b0 * TB, b1 * TB):
                    last = nc.vector.bn_aggr(mv[:, t, :], stats[:, t, :])
                link(last)
                part = slice(b0 * TB, b1 * TB)
                link(nc.vector.tensor_scalar(nwt[:, 2, part], mv[:, part, 1], LN_EPS, None, ALU.add))

            def row_roots(b0, b1):
                part = slice(b0 * TB, b1 * TB)
                rsqrt_steps(dve, rstd[:, part], nwt[:, 2, part], (nwt[:, 0, part], nwt[:, 1, part]), q["dve_seq"],
                            count[0])
                count[0] += NWT

            def normal_rows(b0, b1):
                for b in range(b0, b1):
                    for t in range(b * TB, (b + 1) * TB):
                        last = nc.vector.tensor_scalar(acc[:, t, :], x_sb[:, t, :], mv[:, t, 0:1], rstd[:, t:t + 1],
                                                       ALU.subtract, ALU.mult)
                    last.then_inc(q["xh_done"], 1)

            def normalise(b0, b1):
                row_stats(b0, b1)
                row_roots(b0, b1)
                normal_rows(b0, b1)

            def split_rows(n):
                for b in range(B):
                    for ft in range(KT):
                        dve.wait_ge(q["hT_done"], 4 * n + b * KT + ft + 1)
                        part = slice(b * S, (b + 1) * S)
                        link(nc.vector.tensor_copy(hTs[:, 0, ft, part], hT[:, ft, part]))
                        nc.vector.tensor_tensor(hTs[:, 1, ft, part], hT[:, ft, part], hTs[:, 0, ft, part],
                                                ALU.subtract).then_inc(q["hts_done"], 1)

            def take_modulation(L):
                dve.wait_ge(q["modp_done"], L + 1)
                link(nc.vector.tensor_copy(mods[:, L].rearrange("p b c d -> p (b c d)"), bank[4][:, 0:16]))
                for m in (1, 3):
                    last = nc.vector.tensor_scalar(mods[:, L, m], mods[:, L, m], 1.0, None, ALU.add)
                last.then_inc(q["mods_done"], 1)

            dve.wait_ge(q["d_x"], 16)
            normalise(0, B)
            take_modulation(0)
            split_rows(0)
            dve.wait_ge(q["tr_done"], 4)
            link(nc.vector.memset(acc[:], 0.0))

            dve.wait_ge(q["dtp_done"], 1)
            dve.wait_ge(q["d_small"], 64)
            z, az, adt = dtmp[:, 0], dtmp[:, 1], dtmp[:, 2]
            nc.vector.tensor_tensor(z, bank[4][:, 0:NT * H].rearrange("p (t h) -> p t h", t=NT),
                                    small[:, 0:H].unsqueeze(1).to_broadcast([P, NT, H]), ALU.add)\
                .then_inc(q["dtz_done"], 1)
            dve.wait_ge(q["dtz_done"], 1)
            nc.vector.scalar_tensor_tensor(out=az, in0=z, scalar=-1.0, in1=z, op0=ALU.mult, op1=ALU.min).then_inc(q["dtz_done"], 1)
            dve.wait_ge(q["act_seq"], 3)
            link(nc.vector.scalar_tensor_tensor(out=dtv[:], in0=z, scalar=0.0, in1=az, op0=ALU.max, op1=ALU.add))
            link(nc.vector.tensor_scalar(dtv[:], dtv[:], 0.0, None, ALU.max))
            nc.vector.scalar_tensor_tensor(out=adt, in0=dtv[:], scalar=-1.0,
                                           in1=small[:, H:2 * H].unsqueeze(1).to_broadcast([P, NT, H]),
                                           op0=ALU.mult, op1=ALU.mult).then_inc(q["dta_done"], 1)
            dve.wait_ge(q["gmod_done"], 1)
            for o in range(4):
                last = nc.vector.tensor_copy(gm[:, o // 2, o % 2].rearrange("p b d -> p (b d)"), bank[o][:, :])
            last.then_inc(q["gm_done"], 4)

            def clamp_gates(L):
                dve.wait_ge(q["gm_done"], 4)
                gv = gm[:, L].rearrange("p b c d -> p (b c d)")
                sg = (scb_sign, ex_sign)[L]
                link(nc.vector.tensor_scalar(sg, gv, 0.0, 2.0, ALU.is_ge, ALU.mult))
                link(nc.vector.scalar_tensor_tensor(out=gv, in0=gv, scalar=-1.0, in1=gv, op0=ALU.mult, op1=ALU.max))
                link(nc.vector.tensor_scalar(gv, gv, 0.25, None, ALU.max))
                link(nc.vector.scalar_tensor_tensor(out=gv, in0=sg, scalar=-1.0, in1=gv, op0=ALU.add, op1=ALU.mult))

            dve.wait_ge(q["dcs_done"], 1)
            fl = "p t h -> p (t h)"
            link(nc.vector.tensor_copy(cs[:].rearrange(fl), bank[5][:, 0:NT * H]))
            nc.vector.tensor_copy(etot[:].rearrange(fl), bank[6][:, 0:NT * H])
            link(nc.vector.tensor_tensor(dec[:].rearrange(fl), bank[6][:, 0:NT * H], cs[:].rearrange(fl), ALU.subtract))
            link(nc.vector.tensor_copy(csp[:, :, 0, :], cs[:]))
            dve.wait_ge(q["dve_seq"], count[0])
            nc.vector.tensor_tensor(dtmp[:, 0], cs[:], csp[:, :, 0, :], ALU.subtract).then_inc(q["dex_done"], 1)
            dve.wait_ge(q["dex_done"], 1)
            link(nc.vector.tensor_copy(csp[:, :, 1, :], dtmp[:, 0]))
            nc.vector.tensor_tensor(csp[:, :, 2, :], dtmp[:, 0], csp[:, :, 1, :], ALU.subtract).then_inc(q["csp_done"], 1)
            take_modulation(1)
            dve.wait_ge(q["cspT_done"], 1)
            nc.vector.tensor_copy(csT[:], bank[7][:, :].bitcast(bf16)[0:PIECES * H, :]).then_inc(q["csT_done"], 1)

            def group(g, par, b):
                n = G * b + g
                dve.wait_ge(q["c_raw"], n + 1)
                w = lambda m, tap: bcp[:, bass.ds(g, 1), m, tap:tap + 1].squeeze(1)
                for d in (1, 2, 3):
                    for m in range(2):
                        if d > 1:
                            dve.wait_ge(q["c_step"], 6 * n + 2 * (d - 2) + m + 1)
                        o = gs[:, 2 * par + m, :]
                        nc.vector.scalar_tensor_tensor(out=o, in0=rawg[:, 2 * par + m, 3 - d:3 - d + S],
                                                       scalar=w(m, 3 - d), in1=o, op0=ALU.mult, op1=ALU.add)\
                            .then_inc(q["c_step"], 1)
                if not (type(g) is int and n == 0):
                    dve.wait_ge(q["c_mm"], n)
                dve.wait_ge(q["c_step"], 6 * n + 6)
                dve.wait_ge(q["c_th"], 2 * n + 1)
                nc.vector.scalar_tensor_tensor(out=BT[:], in0=thx[:], scalar=1.0, in1=gs[:, 2 * par, :],
                                               op0=ALU.add, op1=ALU.mult).then_inc(q["c_bc"], 1)
                dve.wait_ge(q["c_th"], 2 * n + 2)
                nc.vector.scalar_tensor_tensor(out=CT[:, bass.ds(g, 1), :].squeeze(1), in0=thg[:], scalar=1.0,
                                               in1=gs[:, 2 * par + 1, :], op0=ALU.add, op1=ALU.mult)\
                    .then_inc(q["c_bc"], 1)

            def scan_slot(i, it, b):
                head = stages(i, it)
                h0, h1, h2 = head(0), head(1), head(2)
                n0, n1, n2 = (H * b + 8 * h[1] + h[0] if h else None for h in (h0, h1, h2))

                def since(name, n):
                    if type(n) is not int or n > 0:
                        dve.wait_ge(q[name], n)

                late, early = out_event(i, it, 6), out_event(i, it, 7)

                def rms_link(k):
                    e = late if k < 2 else early
                    if e and e[0] == 0:
                        root_step(k, NG * b + e[2])

                if h1:
                    j = h1[0]
                    since("py", n1 - 1)
                    dve.wait_ge(q["L_done"], n1 + 1)
                    if type(it) is int and 8 * it + i == 1:
                        dve.wait_ge(q["c_cbm"], G * (b + 1))
                    nc.vector.tensor_tensor(Mm[:, j % 2, :], CB[:, j, :, :].rearrange("p t n -> p (t n)"),
                                            Lm[:, j % 2, :], ALU.mult).then_inc(q["M_done"], 1)
                rms_link(2)
                if h1:
                    since("yb_done", n1 - 3)
                    dve.wait_ge(q["thg_done"], n1 + 1)
                    nc.vector.scalar_tensor_tensor(out=gs[:, j % 4, :], in0=thg[:], scalar=1.0, in1=bank[1][:, :],
                                                   op0=ALU.add, op1=ALU.mult).then_inc(q["gs_done"], 1)
                rms_link(3)
                def tap(d):
                    if h0:
                        hcol = 8 * h0[1] + h0[0]
                        dve.wait_ge(q["cv_step"], 3 * n0 + d - 1) if d > 1 else dve.wait_ge(q["raw_done"], n0 + 1)
                        nc.vector.scalar_tensor_tensor(out=u[:, i % 2, :], in0=raw[:, i % 2, 3 - d:3 - d + S],
                                                       scalar=chn[:, bass.ds(hcol, 1), 3 - d:4 - d].squeeze(1),
                                                       in1=u[:, i % 2, :],
                                                       op0=ALU.mult, op1=ALU.add).then_inc(q["cv_step"], 1)
                    rms_link(3 + d)

                def state(c):
                    if h1:
                        j = h1[0]
                        hcol = 8 * h1[1] + h1[0]
                        s_of = lambda c: St[:, j % 2, c * P:(c + 1) * P]
                        if c == 0:
                            since("py", n1 - 1)
                            dve.wait_ge(q["ps"], n1 + 1)
                            nc.vector.tensor_copy(s_of(0), bank[4][:, 0:P]).then_inc(q["rc_step"], 1)
                        else:
                            dve.wait_ge(q["rc_step"], 3 * n1 + c)
                            nc.vector.scalar_tensor_tensor(out=s_of(c), in0=s_of(c - 1),
                                                           scalar=etot[:, b * TB + c, bass.ds(hcol, 1)],
                                                           in1=bank[4][:, c * P:(c + 1) * P],
                                                           op0=ALU.mult, op1=ALU.add).then_inc(q["rc_step"], 1)
                    rms_link(8 + c)

                tap(1)
                if h2:
                    j = h2[0]
                    hcol = 8 * h2[1] + h2[0]
                    since("yb_done", n2 - 1)
                    dve.wait_ge(q["xT_done"], n2 + 1)
                    dve.wait_ge(q["py"], n2 + 1)
                    nc.vector.scalar_tensor_tensor(out=yv[:, j % 2, :], in0=xT[:, j % 4, :],
                                                   scalar=chn[:, bass.ds(hcol, 1), 5:6].squeeze(1), in1=bank[5][:, :],
                                                   op0=ALU.mult, op1=ALU.add).then_inc(q["yc_done"], 1)
                tap(2)
                tap(3)
                rms_link(7)
                state(0)
                state(1)
                if early and early[0]:
                    add_tile(early, b)
                state(2)
                rms_link(11)
                rms_link(0)
                if h0:
                    since("yc_done", n0 - 3)
                    dve.wait_ge(q["thx_done"], n0 + 1)
                    dve.wait_ge(q["cv_step"], 3 * n0 + 3)
                    nc.vector.scalar_tensor_tensor(out=xT[:, i % 4, :], in0=thx[:], scalar=1.0, in1=u[:, i % 2, :],
                                                   op0=ALU.add, op1=ALU.mult).then_inc(q["xT_done"], 1)
                rms_link(1)
                if early and not early[0]:
                    add_tile(early, b)

            def add_tile(event, b):
                t, j, gi = event
                jj = NG * b + gi
                if t == 0:
                    dve.wait_ge(q["rg_step"], ROOT * (jj + 1))
                if type(jj) is not int or TB * jj + t > 0:
                    dve.wait_ge(q["oa_done"], TB * jj + t)
                dve.wait_ge(q["out_done"], TB * jj + t + 1)
                nc.vector.scalar_tensor_tensor(out=acc[:, b * TB + t, :], in0=bank[6 + t % 2][:, 0:D],
                                               scalar=rg[:, t:t + 1], in1=acc[:, b * TB + t, :],
                                               op0=ALU.mult, op1=ALU.add).then_inc(q["oa_done"], 1)

            def root_step(k, jj):
                step, base = q["rg_step"], ROOT * jj
                if type(jj) is not int or jj > 0 or k:
                    dve.wait_ge(step, base + k)
                t0, t1 = nwt[:, 0, 0:TB], nwt[:, 1, 0:TB]
                if k == 0:
                    dve.wait_ge(q["ssq_done"], jj + 1)
                    ins = nc.vector.tensor_scalar(ssv[:], bank[4][:, S - P:S - P + TB], 1.0 / (HG * P), 16 * RMS_EPS,
                                                  ALU.mult, ALU.add)
                elif k == 1:
                    ins = nc.vector.tensor_scalar(t0.bitcast(i32), ssv[:].bitcast(i32), 1, None,
                                                  ALU.logical_shift_right)
                elif k == 2:
                    if type(jj) is not int or jj > 0:
                        dve.wait_ge(q["oa_done"], TB * jj)
                    ins = nc.vector.tensor_scalar(rg[:].bitcast(i32), t0.bitcast(i32), -1.0, float(0x5f3759df),
                                                  ALU.mult, ALU.add)
                elif k % 3 == 0:
                    ins = nc.vector.tensor_tensor(t0, rg[:], rg[:], ALU.mult)
                elif k % 3 == 1:
                    ins = nc.vector.scalar_tensor_tensor(out=t1, in0=t0, scalar=-0.5, in1=ssv[:], op0=ALU.mult,
                                                         op1=ALU.mult)
                else:
                    ins = nc.vector.scalar_tensor_tensor(out=rg[:], in0=t1, scalar=1.5, in1=rg[:], op0=ALU.add,
                                                         op1=ALU.mult)
                ins.then_inc(step, 1)

            def pads(b):
                if b:
                    dve.wait_ge(q["py"], H * b)
                    dve.wait_ge(q["yb_done"], H * b)
                nc.vector.memset(rawg[:, :, 0:3], 0.0).then_inc(q["pad_done"], 1)
                dve.wait_ge(q["pad_done"], b + 1)

            dve.wait_ge(q["e_dt"], 2)
            for b in range(B):
                if b == 0:
                    dve.wait_ge(q["bcp_done"], 1)
                    pads(b)
                group(0, 0, b)
                group(1, 1, b)
                with dve.Fori(1, G // 2) as g2:
                    for m in range(2):
                        group(2 * g2 + m, m, b)
                slots(dve, b, scan_slot, pads)
                if b == 0:
                    clamp_gates(0)
            dve.wait_ge(q["oa_done"], TB * NG * B)
            for b in range(B):
                part = slice(b * TB, (b + 1) * TB)
                link(nc.vector.tensor_tensor(acc[:, part, :], acc[:, part, :],
                                             gm[:, 0, 0, b, :].unsqueeze(1).to_broadcast([P, TB, D]), ALU.mult))
            nc.vector.tensor_tensor(x_sb[:], x_sb[:], acc[:], ALU.add).then_inc(q["x1_done"], 1)
            dve.wait_ge(q["x1_done"], 1)

            def experts(L):
                n0, nf = 2 * L + 1, FT[L]
                base = FT[0] * B if L else 0
                normalise(L, B)
                dve.wait_ge(q["d_sel"], 16 * (L + 1))
                nc.vector.tensor_copy(sel[:], selw).then_inc(q["sel_done"], 1)
                nc.vector.memset(zerob[:], 0.0).then_inc(q["zb_done"], 1)
                split_rows(n0)
                if L == 0:
                    dve.wait_ge(q["rt_act"], 1)
                    link(nc.vector.tensor_scalar(pr[:], pr[:], 0.5, 0.5, ALU.mult, ALU.add))
                    link(nc.vector.tensor_tensor(prb[:], pr[:],
                                                 small[:, 2 * H:2 * H + E].unsqueeze(1).to_broadcast([P, NT, E]), ALU.add))
                    crit = prb
                else:
                    dve.wait_ge(q["rt_p"], 2)
                    z = bank[6][:, 0:NT * E].rearrange("p (t e) -> p t e", t=NT)
                    link(nc.vector.tensor_reduce(r1[:], z, mybir.AxisListType.X, ALU.max))
                    nc.vector.tensor_tensor(pr[:], z, r1[:].unsqueeze(2).to_broadcast([P, NT, E]), ALU.subtract)\
                        .then_inc(q["rt_dve"], 1)
                    dve.wait_ge(q["rt_act"], 2)
                    link(nc.vector.tensor_reduce(r1[:], pr[:], mybir.AxisListType.X, ALU.add))
                    link(nc.vector.reciprocal(r1[:], r1[:]))
                    link(nc.vector.tensor_tensor(pr[:], pr[:], r1[:].unsqueeze(2).to_broadcast([P, NT, E]), ALU.mult))
                    crit = pr
                theirs = crit[:].unsqueeze(2).to_broadcast([P, NT, E, E])
                own = crit[:].unsqueeze(3).to_broadcast([P, NT, E, E])
                lower = cst[:, C_LOWER:C_LOWER + E * E].rearrange("p (a c) -> p a c", a=E).unsqueeze(1)\
                    .to_broadcast([P, NT, E, E])
                nc.vector.tensor_tensor(cmpa[:], theirs, own, ALU.is_gt)
                link(nc.vector.tensor_tensor(cmpb[:], theirs, own, ALU.is_equal))
                link(nc.vector.tensor_tensor(cmpb[:], cmpb[:], lower, ALU.mult))
                link(nc.vector.tensor_tensor(cmpa[:], cmpa[:], cmpb[:], ALU.add))
                link(nc.vector.tensor_reduce(rank[:], cmpa[:], mybir.AxisListType.X, ALU.add))
                nc.vector.memset(comb[:, :, E:E1], 1.0)
                link(nc.vector.scalar_tensor_tensor(out=comb[:, :, 0:E], in0=rank[:], scalar=2.0, in1=pr[:],
                                                    op0=ALU.is_lt, op1=ALU.mult))
                if L:
                    link(nc.vector.tensor_reduce(r1[:], comb[:, :, 0:E], mybir.AxisListType.X, ALU.add))
                    link(nc.vector.reciprocal(r1[:], r1[:]))
                    link(nc.vector.tensor_tensor(comb[:, :, 0:E], comb[:, :, 0:E],
                                                 r1[:].unsqueeze(2).to_broadcast([P, NT, E]), ALU.mult))
                link(nc.vector.tensor_copy(cpb[:, :, 0, :], comb[:]))
                link(nc.vector.tensor_tensor(cpt[:], comb[:], cpb[:, :, 0, :], ALU.subtract))
                link(nc.vector.tensor_copy(cpb[:, :, 1, :], cpt[:]))
                nc.vector.tensor_tensor(cpb[:, :, 2, :], cpt[:], cpb[:, :, 1, :], ALU.subtract).then_inc(q["cp_done"], 1)
                dve.wait_ge(q["cpT_p"], L + 1)
                nc.vector.tensor_copy(cbT[:], bank[7][:, :].bitcast(bf16)[0:PIECES * E1, :]).then_inc(q["cbT_done"], 1)

                def hidden(f, b, par):
                    n = base + nf * b + f
                    b0, b1, b2 = (bank[3 * par + m][:, :] for m in range(3))
                    def since(name, m):
                        if type(m) is not int or m > 0:
                            dve.wait_ge(q[name], m)
                    if L == 0:
                        dve.wait_ge(q["fs_c"], n + 1)
                        since("fh_done", n - 1)
                        nc.vector.tensor_tensor(ua[:, par, :], b0, sS[:, par, :], ALU.mult)
                        nc.vector.scalar_tensor_tensor(out=uc[:, par, :], in0=b1, scalar=0.5,
                                                       in1=sS[:, par, :], op0=ALU.mult, op1=ALU.mult)\
                            .then_inc(q["fa_done"], 1)
                        since("fh_done", n)
                        dve.wait_ge(q["fth_done"], n + 1)
                        dve.wait_ge(q["fa_done"], n + 1)
                        nc.vector.scalar_tensor_tensor(out=fg[:], in0=fth[:, par, :], scalar=1.0, in1=ua[:, par, :],
                                                       op0=ALU.add, op1=ALU.mult).then_inc(q["fg_done"], 1)
                        since("fout", n - 1)
                        dve.wait_ge(q["fg_done"], n + 1)
                        nc.vector.tensor_tensor(hf[:, par, :], fg[:], uc[:, par, :], ALU.mult)\
                            .then_inc(q["fh_done"], 1)
                    else:
                        since("fh_done", n)
                        dve.wait_ge(q["fth_done"], n + 1)
                        nc.vector.scalar_tensor_tensor(out=fg[:], in0=fth[:, par, :], scalar=1.0, in1=b0,
                                                       op0=ALU.add, op1=ALU.mult).then_inc(q["fg_done"], 1)
                        since("fout", n - 1)
                        dve.wait_ge(q["fg_done"], n + 1)
                        nc.vector.scalar_tensor_tensor(out=hf[:, par, :], in0=fg[:], scalar=0.5, in1=b2,
                                                       op0=ALU.mult, op1=ALU.mult).then_inc(q["fa_done"], 1)
                        dve.wait_ge(q["fa_done"], n + 1)
                        dve.sem_inc(q["fh_done"], 1)

                def add_experts(b):
                    dve.wait_ge(q["fout"], base + nf * (b + 1))
                    for m in range(2):
                        last = nc.vector.tensor_tensor(xo[:, 2 * m:2 * m + 2, :],
                                                       bank[6 + m][:, :].rearrange("p (t d) -> p t d", t=2),
                                                       gm[:, L, 1, b, :].unsqueeze(1).to_broadcast([P, 2, D]), ALU.mult)
                    link(last)
                    part = slice(b * TB, (b + 1) * TB)
                    nc.vector.tensor_tensor(x_sb[:, part, :], x_sb[:, part, :], xo[:], ALU.add).then_inc(q["xf_done"], 1)
                    dve.wait_ge(q["xf_done"], L * B + b + 1)

                for b in range(B):
                    hidden(0, b, b)
                    if b:
                        add_experts(b - 1)
                    hidden(1, b, 1 - b)
                    with dve.Fori(1, (nf - 1) // 2) as i:
                        for m in range(2):
                            hidden(2 * i + m, b, (b + m) % 2)
                    hidden(nf - 1, b, b)
                add_experts(B - 1)

            experts(0)

            def heads():
                normalise(0, B)
                nc.vector.tensor_copy(iotak[:].rearrange("p s k h -> p (s k) h"),
                                      cst[:, C_IOTA:C_IOTA + 2 * K].unsqueeze(2).to_broadcast([P, 2 * K, QG]))
                nc.vector.tensor_copy(selQ[:], identb[:].rearrange("p (g h) -> p g h", h=QG).unsqueeze(2)
                                      .to_broadcast([P, NQ, K, QG]))
                clamp_gates(1)
                block4 = cst[:, C_BLOCK:C_BLOCK + QG]
                link(nc.vector.memset(VW[:], 0.0))
                for m in range(2):
                    last = nc.vector.tensor_copy(VWd[:, m, :, :, 4], block4.unsqueeze(1).to_broadcast([P, 4, QG]))
                link(last)
                tk = (q["tk0"], q["tk1"])
                TK = 4 + 2 * (K // 8)

                def choice_starts(b):
                    dve.wait_ge(q["a_qkc"], 2 * b + 1)
                    if b:
                        dve.wait_ge(q["a_code"], b)
                    nc.vector.tensor_copy(wk[:, 0, 0, ::-1], ks[:, b, :]).then_inc(tk[0], 1)
                    nc.vector.tensor_scalar(wk[:, 1, 0, :], ks[:, b, :], -1.0, None, ALU.mult).then_inc(tk[1], 1)

                def extremes(b):
                    for side in range(2):
                        dve.wait_ge(tk[side], TK * b + 1)
                        if b:
                            dve.wait_ge(q["a_ext"], 2 * b)
                        nc.vector.max(e8[:, side, :], wk[:, side, 0, :]).then_inc(q["a_e8"], 1)
                    for side in range(2):
                        dve.wait_ge(q["a_e8"], 2 * b + side + 1)
                        nc.vector.tensor_scalar(ext[:, b, side:side + 1], e8[:, side, 0:1],
                                                2.0 * side - 1.0, None, ALU.mult).then_inc(q["a_ext"], 1)

                def next_eight(b, r, par):
                    for side in range(2):
                        dve.wait_ge(tk[side], TK * b + 2 * r + 1)
                        nc.vector.max(m8[:, side, par, :], wk[:, side, par, :]).then_inc(tk[side], 1)

                def strike_eight(b, r, par):
                    for side in range(2):
                        dve.wait_ge(tk[side], TK * b + 2 * r + 2)
                        nc.vector.match_replace(wk[:, side, 1 - par, :], m8[:, side, par, :],
                                                wk[:, side, par, :], NEG).then_inc(tk[side], 1)

                def choice_ends(b, part):
                    done = TK * b + 1 + 2 * (K // 8)
                    for side in range(2):
                        dve.wait_ge(tk[side], done + part)
                        if part == 0:
                            ins = nc.vector.tensor_scalar(hit[:, side, :], wk[:, side, 0, :], NEG, None, ALU.is_equal)
                        elif part == 1:
                            ins = nc.vector.tensor_tensor_scan(rk[:, side, :], hit[:, side, :], hit[:, side, :], 0.0,
                                                               ALU.add, ALU.max)
                        else:
                            ins = nc.vector.scalar_tensor_tensor(out=code[:, side, :], in0=rk[:, side, :],
                                                                 scalar=float(side * K), in1=hit[:, side, :],
                                                                 op0=ALU.add, op1=ALU.mult)
                        ins.then_inc(tk[side], 1)
                    if part == 2:
                        for side in range(2):
                            dve.wait_ge(tk[side], TK * (b + 1))
                        if b:
                            dve.wait_ge(q["a_cT"], b)
                        nc.vector.tensor_tensor(code[:, 2, :], code[:, 0, ::-1], code[:, 1, :], ALU.add)\
                            .then_inc(q["a_code"], 1)

                def add_heads(b):
                    dve.wait_ge(q["a_out"], b + 1)
                    for m in range(2):
                        last = nc.vector.tensor_tensor(xo1[:, 2 * m:2 * m + 2, :],
                                                       bank[m][:, :].rearrange("p (t d) -> p t d", t=2),
                                                       gm[:, 1, 0, b, :].unsqueeze(1).to_broadcast([P, 2, D]), ALU.mult)
                    link(last)
                    part = slice(b * TB, (b + 1) * TB)
                    nc.vector.tensor_tensor(x_sb[:, part, :], x_sb[:, part, :], xo1, ALU.add).then_inc(q["a_x"], 1)
                    dve.wait_ge(q["a_x"], b + 1)

                choice_starts(0)
                extremes(0)
                for r in range(K // 8):
                    next_eight(0, r, r % 2)
                    strike_eight(0, r, r % 2)
                for part in range(3):
                    choice_ends(0, part)
                for b in range(B):
                    dve.wait_ge(q["a_cT"], b + 1)
                    nc.vector.tensor_copy(cdT[:].rearrange("p t h -> p (t h)"),
                                          bank[2][:, :].bitcast(bf16)[:, 0:TB * P]).then_inc(q["a_cTc"], 1)
                    dve.wait_ge(q["a_cTc"], b + 1)
                    for t in range(TB):
                        for side in range(2):
                            last = nc.vector.tensor_tensor(
                                OH[:, t, side].rearrange("p g (k h) -> p g k h", h=QG),
                                cdT[:, t, :].rearrange("p (g h) -> p g h", h=QG).unsqueeze(2).to_broadcast([P, NQ, K, QG]),
                                iotak[:, side].unsqueeze(1).to_broadcast([P, NQ, K, QG]), ALU.is_equal)
                        last.then_inc(q["a_oh"], 1)
                        if b and t == 0:
                            add_heads(b - 1)

                    dve.wait_ge(q["a_pv"], 4 * (b + 1))
                    for n in range(NQ // 4):
                        dve.wait_ge(q["a_vw"], NQ // 4 * b + n + 1)
                        nc.vector.tensor_reduce(gat[:, 8 * n:8 * n + 8, :],
                                                bank[n][:, 0:384].rearrange("p (a c x) -> p a x c", a=8, c=3),
                                                mybir.AxisListType.X, ALU.add).then_inc(q["a_gat"], 1)
                    dve.wait_ge(q["a_gat"], NQ // 4 * (b + 1))
                    nc.vector.tensor_tensor(gam.rearrange("p a (h x) -> p a h x", h=QG),
                                            gat.rearrange("p a (h x) -> p a h x", h=QG),
                                            block4.unsqueeze(1).unsqueeze(3).to_broadcast([P, 2 * NQ, QG, 4]),
                                            ALU.mult).then_inc(q["a_iota"], 1)
                    dve.wait_ge(q["a_iota"], 3 * b + 1)
                    gams = gam.rearrange("p (g s) (h x) -> p g s h x", s=2, h=QG)
                    for side in range(2):
                        nc.vector.tensor_reduce(scl[:, :, side], gams[:, :, side, :, side],
                                                mybir.AxisListType.X, ALU.add).then_inc(q["a_iota"], 1)
                    dve.wait_ge(q["a_iota"], 3 * b + 3)

                    def value_weights(n, par):
                        c = NQ // 4 * b + n
                        if not (type(c) is int and c < 2):
                            dve.wait_ge(q["a_PV"], 4 * c - 4)
                        for side in range(2):
                            last = nc.vector.tensor_copy(VWd[:, par, :, :, 2 * side:2 * side + 2],
                                                         gams[:, bass.ds(4 * n, 4), side, :, 2:4])
                        last.then_inc(q["a_vwt"], 1)

                    def least(i, n):
                        c = NQ * b + 4 * n + i
                        if not (type(c) is int and c < 4):
                            dve.wait_ge(q["a_E"], c - 3)
                        dve.wait_ge(q["a_tb"], c + 1)
                        nc.vector.scalar_tensor_tensor(out=arg[:, i, :], in0=bank[QB[i]][:, :],
                                                       scalar=scl[:, bass.ds(4 * n + i, 1), 0:1].squeeze(1),
                                                       in1=tb_[:, i, :], op0=ALU.mult, op1=ALU.min)\
                            .then_inc(q["a_arg"], 1)

                    def collect(n):
                        dve.wait_ge(q["a_oT"], NQ // 4 * b + n + 1)
                        nc.vector.tensor_copy(
                            O5[:, :, bass.ds(16 * n, 16), :].rearrange("p t h c -> p t (h c)"),
                            bank[6][:, 0:TB * OC].rearrange("p (t x) -> p t x", t=TB)).then_inc(q["a_O5"], 1)

                    def attend(n, par):
                        more = not (type(n) is int and n == NQ // 4 - 1)
                        for i in range(4):
                            least(i, n)
                            if b + 1 < B:
                                if 3 <= n < 7:
                                    if i == 0:
                                        next_eight(b + 1, n - 3, 1 - par)
                                    if i == 1:
                                        strike_eight(b + 1, n - 3, 1 - par)
                                elif n == 0 and i == 0:
                                    choice_starts(b + 1)
                                elif n == 1 and i == 1:
                                    extremes(b + 1)
                                elif n == NQ // 4 - 1 and i < 3:
                                    choice_ends(b + 1, i)
                            elif type(n) is int and n < 3 and i == 2:
                                if n == 0:
                                    dve.wait_ge(q["a_x"], B - 1)
                                (row_stats, row_roots, normal_rows)[n](0, B - 1)
                        if more:
                            value_weights(n + 1, 1 - par)
                        if type(n) is not int or n > 1:
                            collect(n - 2)

                    value_weights(0, 0)
                    if b + 1 < B:
                        for n in range(NQ // 4):
                            attend(n, n % 2)
                    else:
                        for n in range(3):
                            attend(n, n % 2)
                        with dve.Fori(0, (NQ // 4 - 4) // 2) as r:
                            for m in range(2):
                                attend(2 * r + 3 + m, 1 - m)
                        attend(NQ // 4 - 1, 1)
                    collect(NQ // 4 - 2)
                    collect(NQ // 4 - 1)
                    dve.wait_ge(q["a_O5"], NQ // 4 * (b + 1))
                    dve.wait_ge(q["a_qT"], b + 1)
                    nc.vector.tensor_scalar(qm.rearrange("p t h -> p (t h)"), bank[7][:, :], 0.0, None, ALU.is_gt)\
                        .then_inc(q["a_mask"], 1)
                    nc.vector.reciprocal(rden, O5[:, :, :, 4]).then_inc(q["a_mask"], 1)
                    dve.wait_ge(q["a_mask"], 3 * b + 2)
                    for j in range(2):
                        last = nc.vector.copy_predicated(O5[:, :, :, 2 + j], qm.bitcast(mybir.dt.uint32),
                                                         O5[:, :, :, j])
                    last.then_inc(q["a_mask"], 1)
                    dve.wait_ge(q["a_mask"], 3 * b + 3)
                    for j in range(2):
                        last = nc.vector.tensor_tensor(att[:, :, :, j], O5[:, :, :, 2 + j], rden, ALU.mult)
                    last.then_inc(q["a_att"], 1)
                add_heads(B - 1)

            heads()
            experts(1)

        @block.gpsimd
        def _(pool):
            count = [0]

            def link(ins):
                count[0] += 1
                ins.then_inc(q["pool_seq"], 1)
                pool.wait_ge(q["pool_seq"], count[0])

            pool.wait_ge(q["d_small"], 64)
            nc.gpsimd.tensor_scalar(bcp[:], bcp[:], 0.5, None, ALU.mult).then_inc(q["bcp_done"], 1)
            pool.wait_ge(q["wbs_hi"], 1)
            nc.gpsimd.tensor_tensor(wbs[:, 1], wbf, wbs[:, 0], ALU.subtract).then_inc(q["wbs_done"], 1)
            pool.wait_ge(q["whi_done"], 1)
            nc.gpsimd.tensor_tensor(whl[:, 0, 1, :], wA[:, 0, :], whl[:, 0, 0, :], ALU.subtract)\
                .then_inc(q["wsplit"], 1)

            def scan_slot(i, it, b):
                head = stages(i, it)
                h0, h1, h2 = head(0), head(1), head(2)
                n0, n1, n2 = (H * b + 8 * h[1] + h[0] if h else None for h in (h0, h1, h2))

                def since(name, n):
                    if type(n) is not int or n > 0:
                        pool.wait_ge(q[name], n)

                if h1:
                    j = h1[0]
                    hcol = 8 * h1[1] + h1[0]
                    since("ps", n1 - 1)
                    pool.wait_ge(q["xdt_done"], n1 + 1)
                    nc.gpsimd.tensor_tensor(
                        Xw[:, j % 2, :].rearrange("p (t n) -> p t n", n=P),
                        Xdt[:, j % 2, 0:S - P].rearrange("p (t n) -> p t n", n=P),
                        dec[:, b * TB:b * TB + TB - 1, bass.ds(hcol, 1)].to_broadcast([P, TB - 1, P]),
                        ALU.mult).then_inc(q["xw_done"], 1)
                if h2:
                    j = h2[0]
                    jj = NG * b + 2 * h2[1] + j // 4
                    since("out_done", TB * (jj - 1))
                    pool.wait_ge(q["gs_done"], n2 + 1)
                    pool.wait_ge(q["yc_done"], n2 + 1)
                    nc.gpsimd.tensor_tensor(yb[:, j, :], yv[:, j % 2, :], gs[:, j % 4, :], ALU.mult)\
                        .then_inc(q["yb_done"], 1)
                if h0:
                    nx = (i + 1) % 2
                    pool.wait_ge(q["whi_done"], n0 + 2)
                    nc.gpsimd.tensor_tensor(whl[:, nx, 1, :], wA[:, nx, :], whl[:, nx, 0, :],
                                            ALU.subtract).then_inc(q["wsplit"], 1)
                    since("py", n0 - 1)
                    pool.wait_ge(q["e_done"], n0 + 1)
                    nc.gpsimd.tensor_tensor(CE[:, i % 2, :], CT[:, i, P:S], Em[:, i % 2, :], ALU.mult)\
                        .then_inc(q["ce_done"], 1)
                if h2:
                    hcol = 8 * h2[1] + j
                    pool.wait_ge(d_wB[j], 16 * (H // 8 * b + h2[1] + 1))
                    nc.gpsimd.tensor_tensor(wB[:, j, :], wB[:, j, :],
                                            chn[:, bass.ds(hcol, 1), 6:7].squeeze(1).to_broadcast([P, D]), ALU.mult)\
                        .then_inc(q["wo_done"], 1)
                    m = j % HG
                    if m:
                        if m > 1:
                            pool.wait_ge(q["sq_add"], 3 * jj + m - 1)
                        pool.wait_ge(q["ysq_done"], n2 + 1)
                        nc.gpsimd.tensor_tensor(sqa[:, j // 4, :], sqa[:, j // 4, :], ysq[:], ALU.add)\
                            .then_inc(q["sq_add"], 1)

            pool.wait_ge(q["d_chn"], 16)
            for b in range(B):
                with pool.Fori(0, G) as g:
                    pool.wait_ge(q["c_evac"], G * b + g + 1)
                    cb = CB[:, bass.ds(g, 1), :, :].squeeze(1)
                    nc.gpsimd.tensor_tensor(cb, cb, tri.unsqueeze(1).to_broadcast([P, TB, P]), ALU.mult)\
                        .then_inc(q["c_cbm"], 1)
                slots(pool, b, scan_slot)

            def low_halves(L):
                w = 512 if L == 0 else 256
                for f in range(FT[L]):
                    pool.wait_ge(q["fw_hi"], (FT[0] if L else 0) + f + 1)
                    nc.gpsimd.tensor_tensor(w13s[:, 1, f, 0:w], w13[:, f, 0:w], w13s[:, 0, f, 0:w], ALU.subtract)\
                        .then_inc(q["fw_done"], 1)

            def heads():
                pool.wait_ge(q["a_q0"], 1)
                nc.gpsimd.tensor_tensor(pvr[:, 0:2, :], qs[:], qp[:, 0], ALU.subtract).then_inc(q["a_q1"], 1)
                pool.wait_ge(q["a_q2"], 1)
                nc.gpsimd.tensor_tensor(qp[:, 2], pvr[:, 0:2, :], qp[:, 1], ALU.subtract).then_inc(q["a_qp"], B)
                for b in range(B):
                    def piece(m, done, out, n, qq):
                        pool.wait_ge(q[done], 4 * b + n + 1)
                        view = pvr[:, qq, :].rearrange("p (t h) -> p t h", t=TB)
                        return nc.gpsimd.tensor_tensor(view if out is None else out, view, PV[:, :, m, :, qq], ALU.subtract)

                    for n, qq in enumerate((2, 3, 0, 1)):
                        piece(0, "a_p0", None, n, qq).then_inc(q["a_p1"], 1)
                    for n, qq in enumerate((2, 3, 0, 1)):
                        piece(1, "a_p2", PV[:, :, 2, :, qq], n, qq).then_inc(q["a_pv"], 1)

            low_halves(0)
            heads()
            low_halves(1)


def out_event(i, it, back):
    j, n = i - back, it
    if j < 0:
        j, n = j + 8, it - 1
    if type(n) is int and not 0 <= n < H // 8:
        return None
    return j % TB, j // HG, 2 * n + j // HG


def kernel(**inputs):
    import numpy as np
    import concourse.bacc as bacc
    from concourse.bass_utils import run_bass_kernel_spmd

    def a(name):
        return np.asarray(inputs[name])

    f32 = np.float32
    I, GN = H * P, G * P
    rows = a("L0_attn_in_proj_w")

    def km(w):
        n, m, _ = w.shape
        return w.reshape(n, m, KT, P).transpose(3, 0, 2, 1)

    gate = km(rows[0:I].reshape(H, P, D))
    xs = km(rows[I:2 * I].reshape(H, P, D))
    win = np.stack([xs, gate], axis=2).transpose(1, 0, 2, 3, 4).reshape(H, P, 512)
    Bw = km(rows[2 * I:2 * I + GN].reshape(G, P, D))
    Cw = km(rows[2 * I + GN:2 * I + 2 * GN].reshape(G, P, D))
    wbc = np.stack([Bw, Cw], axis=2).reshape(P, G, 512)
    wdt = rows[2 * I + 2 * GN:].reshape(H, KT, P).transpose(2, 1, 0)
    cw, cb = a("L0_attn_conv_w")[:, 0, :], a("L0_attn_conv_b")
    chan = np.concatenate([cw, cb[:, None]], axis=1)
    wob = a("L0_attn_out_proj_w").T.reshape(H, P, D)
    chn = np.concatenate([
        chan[0:I].reshape(H, P, 5),
        np.broadcast_to(a("L0_attn_D")[:, None, None], (H, P, 1)),
        a("L0_attn_norm_w").reshape(H, P, 1),
        np.zeros((H, P, CH - 7), f32)], axis=2).transpose(1, 0, 2)
    bcp = np.stack([chan[I:I + GN].reshape(G, P, 5), chan[I + GN:].reshape(G, P, 5)], axis=2).transpose(1, 0, 2, 3)
    eye = np.eye(P, dtype=f32)
    stack = np.concatenate([np.tile(np.eye(H, dtype=f32), (PIECES, 1)), np.zeros((P - PIECES * H, H), f32)])
    k1 = np.arange(P)[:, None]
    lower = np.tril(np.ones((E, E), f32), -1).reshape(1, E * E)
    iota = np.arange(1, 2 * K + 1, dtype=f32)[None]
    consts = np.concatenate([
        eye, np.triu(np.ones((P, P), f32)), np.ones((P, P), f32), stack,
        np.broadcast_to(lower, (P, E * E)), (k1 % QG == np.arange(QG)).astype(f32),
        np.broadcast_to(iota, (P, 2 * K))], axis=1)
    expert = [np.arange(FT[0] * P) // P, np.minimum(np.arange(FT[1] * P) // HID1, E)]
    sel = np.concatenate([(e[None] == np.arange(E1)[:, None]).astype(f32) for e in expert], axis=1)
    w13_0 = np.stack([km(np.concatenate([a("L0_ffn_w1"), a("L0_ffn_sw1")[None]])),
                      km(np.concatenate([a("L0_ffn_w3"), a("L0_ffn_sw3")[None]]))], axis=2).reshape(P, E1, 512)
    w2_0 = np.concatenate([a("L0_ffn_w2"), a("L0_ffn_sw2")[None]]).transpose(2, 0, 1)
    pad = FT[1] * P - E1 * HID1
    in1 = np.concatenate([a("L1_ffn_w1"), a("L1_ffn_w_shared1")[None]]).transpose(1, 0, 2).reshape(D, E1 * HID1)
    in1 = np.concatenate([in1, np.zeros((D, pad), f32)], axis=1)
    w13_1 = in1.reshape(KT, P, FT[1], P).transpose(1, 2, 0, 3).reshape(P, FT[1], 256)
    out1 = np.concatenate([a("L1_ffn_w2"), a("L1_ffn_w_shared2")[None]]).reshape(E1 * HID1, D)
    w2_1 = np.concatenate([out1, np.zeros((pad, D), f32)]).reshape(FT[1], P, D).transpose(1, 0, 2)
    router = np.stack([a("L0_ffn_gate_w").T, a("L1_ffn_w_router")]).reshape(2, KT, P, E).transpose(2, 0, 1, 3)
    wqk = np.stack([a("L1_attn_Wq").T, a("L1_attn_Wk").T]).reshape(2, KT, P, P).transpose(2, 0, 1, 3)
    wv = a("L1_attn_Wv").reshape(P, 2, D).transpose(2, 1, 0).reshape(KT, P, D).transpose(1, 0, 2)
    wo = a("L1_attn_Wo").T.reshape(KT, P, D).transpose(1, 0, 2)
    feeds = {
        "sel": np.tile(sel, (PIECES, 1)), "w13_0": w13_0, "w2_0": w2_0, "w13_1": w13_1, "w2_1": w2_1,
        "router": router, "wqk": wqk, "wv": wv, "wo": wo,
        "x": a("L0_attn_x").reshape(T, D),
        "cst": consts,
        "cT": np.stack([a("L0_c"), a("L1_c")]).reshape(2, B, KT, P).transpose(3, 0, 2, 1).reshape(P, 2 * KT * B),
        "wmod": np.stack([a("L0_wmod"), a("L1_wmod")]).reshape(2, KT, P, 6 * D).transpose(0, 2, 1, 3),
        "small": np.concatenate([a("L0_attn_dt_bias"), a("L0_attn_A_log"), a("L0_ffn_expert_bias")]),
        "wdt": wdt, "bcp": bcp, "chn": chn, "wbc": wbc, "win": win, "wob": wob,
    }
    nc = bacc.Bacc("TRN2", target_bir_lowering=False, num_devices=1)
    feeds = {n: np.ascontiguousarray(v) for n, v in feeds.items()}
    io = {n: nc.dram_tensor(f"in_{n}", v.shape, mybir.dt.from_np(v.dtype), kind="ExternalInput").ap()
          for n, v in feeds.items()}
    io["out"] = nc.dram_tensor("out", (T, D), mybir.dt.float32, kind="ExternalOutput").ap()
    build_block(nc, io)
    r = run_bass_kernel_spmd(nc, [{f"in_{n}": v for n, v in feeds.items()}], core_ids=[0])
    return r.results[0]["out"].reshape(B, S, D)
```
